# Optimizing a Trainium2 kernel written in Bass

```python
import numpy as np
import jax
import jax.numpy as jnp

def _softmax(x, axis=-1):
    return jax.nn.softmax(x, axis=axis)

def _gelu(x):
    return jax.nn.gelu(x, approximate=True)

def _silu(x):
    return jax.nn.silu(x)

def _sigmoid(x):
    return jax.nn.sigmoid(x)

def _layernorm(x, axis=-1, eps=1e-05):
    m = jnp.mean(x, axis=axis, keepdims=True)
    v = jnp.var(x, axis=axis, keepdims=True)
    return (x - m) / jnp.sqrt(v + eps)

def _scatter_add(tgt, idx, src, axis=0):
    return tgt.at[idx].add(src)

def _segment_sum(src, seg, n):
    return jax.ops.segment_sum(src, seg, n)
kernel_name = 'mk_xattn_ffn_d2_seqx_r8_a9daf9'

def setup_inputs(seed: int=0):
    np.random.seed(seed)
    _w = jnp.asarray

    def _rec_inputs():
        import jax
        import jax.numpy as jnp
        _rk = jax.random.key(seed)
        x = 0.5 + 0.2887 * jax.random.normal(jax.random.fold_in(_rk, 1), (4, 256, 256), jnp.float32)
        _lenS = 256 - jax.random.randint(jax.random.fold_in(_rk, 7), (4,), 0, max(1, 256 // 4) + 1, jnp.int32)
        _lenS2 = 256 - jax.random.randint(jax.random.fold_in(_rk, 8), (4,), 0, max(1, 256 // 4) + 1, jnp.int32)
        _ctx_512P = jax.random.normal(jax.random.fold_in(_rk, 11), (4, 16, 64), jnp.float32)
        _ctx_512c = jax.random.dirichlet(jax.random.fold_in(_rk, 511), 0.3 * jnp.ones((16,), jnp.float32), (4, 256))
        _ctx_512t = jnp.einsum('bsk,bkd->bsd', _ctx_512c, _ctx_512P)
        _ctx_512t = _ctx_512t * jax.lax.rsqrt(jnp.mean(jnp.square(_ctx_512t)) + 1e-12) * 0.953939
        ctx_512 = 7.22013e-05 + 1.00017 * (_ctx_512t + 0.3 * jax.random.normal(jax.random.fold_in(_rk, 611), (4, 256, 64), jnp.float32))
        return (x, ctx_512)
    x, ctx_512 = _rec_inputs()

    def _L0_xattn_setup():
        import jax, jax.numpy as jnp
        import numpy as np
        P_ASEM = 0.6
        key = jax.random.key(seed)
        k1, k2, k3 = jax.random.split(key, 3)
        B, N, D = (8, 256, 64)
        x = jax.random.normal(k1, (B, N, D), dtype=jnp.float32)
        adj = jax.random.uniform(k2, (B, N, N), dtype=jnp.float32)
        bound = 1.0 / np.sqrt(2 * D)
        W = jax.random.uniform(k3, (1, 2 * D), dtype=jnp.float32, minval=-bound, maxval=bound)
        b = jnp.zeros((1,), dtype=jnp.float32)
        return {'x': x, 'adj': adj, 'W': W, 'b': b}
    _L0_xattn_all = _L0_xattn_setup()
    _L0_xattn_in = {k: v for k, v in _L0_xattn_all.items() if k in ('W', 'b')}
    del _L0_xattn_all

    def _L0_ffn_setup():
        import jax, jax.numpy as jnp
        import numpy as np
        TOP_K = 2
        key = jax.random.key(seed)
        ks = jax.random.split(key, 6)
        B, S, H, F, E = (1, 256, 256, 176, 8)
        Fs = 2 * F
        std = jnp.float32(0.02)
        return {'hidden_states': jax.random.normal(ks[0], (B, S, H), jnp.float32), 'gate_weight': jax.random.normal(ks[1], (E, H), jnp.float32) * std, 'gate_up_weights': jax.random.normal(ks[2], (E, 2 * F, H), jnp.float32) * std, 'down_weights': jax.random.normal(ks[3], (E, H, F), jnp.float32) * std, 'shared_gate_up': jax.random.normal(ks[4], (2 * Fs, H), jnp.float32) * std, 'shared_down': jax.random.normal(ks[5], (H, Fs), jnp.float32) * std}
    _L0_ffn_all = _L0_ffn_setup()
    _L0_ffn_in = {k: v for k, v in _L0_ffn_all.items() if k in ('gate_weight', 'gate_up_weights', 'down_weights', 'shared_gate_up', 'shared_down')}
    del _L0_ffn_all

    def _L1_xattn_setup():
        import jax, jax.numpy as jnp
        import numpy as np
        B, N, D = (16, 256, 64)
        H = 4
        TOP_K_RATIO = 0.3
        key = jax.random.key(seed)
        k1, k2, k3, k4 = jax.random.split(key, 4)
        h = jax.random.normal(k1, (B, N, D), dtype=jnp.float32)
        adj_raw = jax.random.uniform(k2, (B, N, N), dtype=jnp.float32)
        lim = 1.0 / np.sqrt(D)
        Wq = jax.random.uniform(k3, (D, D), minval=-lim, maxval=lim, dtype=jnp.float32)
        Wk = jax.random.uniform(k4, (D, D), minval=-lim, maxval=lim, dtype=jnp.float32)
        gamma_raw = jnp.float32(-0.85)
        return {'h': h, 'adj_raw': adj_raw, 'Wq': Wq, 'Wk': Wk, 'gamma_raw': gamma_raw}
    _L1_xattn_all = _L1_xattn_setup()
    _L1_xattn_in = {k: v for k, v in _L1_xattn_all.items() if k in ('Wq', 'Wk', 'gamma_raw')}
    del _L1_xattn_all

    def _L1_ffn_setup():
        import jax, jax.numpy as jnp
        import numpy as np
        B, S, H = (2, 256, 256)
        E, K, I = (64, 8, 96)

        def _moe_forward(hidden_states, gate_weight, w_gate, w_up, w_down):
            b, s, h = hidden_states.shape
            x = hidden_states.reshape(-1, h)
            logits = x.astype(jnp.float32) @ gate_weight.astype(jnp.float32).T
            scores = jax.nn.softmax(logits, axis=-1)
            topk_w, topk_idx = jax.lax.top_k(scores, K)
            topk_w = topk_w / jnp.sum(topk_w, axis=-1, keepdims=True)
            flat_ids = topk_idx.reshape(-1)
            expanded = jnp.repeat(x, K, axis=0)
            order = jnp.argsort(flat_ids)
            sorted_tokens = expanded[order]
            group_sizes = jnp.zeros((E,), jnp.int32).at[flat_ids].add(1)
            g = jax.lax.ragged_dot(sorted_tokens, w_gate, group_sizes)
            u = jax.lax.ragged_dot(sorted_tokens, w_up, group_sizes)
            out = jax.lax.ragged_dot(jax.nn.silu(g) * u, w_down, group_sizes)
            inv = jnp.argsort(order)
            outs = out[inv].reshape(-1, K, h)
            y = jnp.sum(outs * topk_w[:, :, None], axis=1)
            return y.reshape(b, s, h)
        key = jax.random.key(seed)
        k0, k1, k2, k3, k4 = jax.random.split(key, 5)
        hidden_states = jax.random.normal(k0, (B, S, H), dtype=jnp.float32)
        gate_weight = jax.random.normal(k1, (E, H), dtype=jnp.float32) * 0.02
        w_gate = jax.random.normal(k2, (E, H, I), dtype=jnp.float32) * 0.02
        w_up = jax.random.normal(k3, (E, H, I), dtype=jnp.float32) * 0.02
        w_down = jax.random.normal(k4, (E, I, H), dtype=jnp.float32) * 0.02
        return {'hidden_states': hidden_states, 'gate_weight': gate_weight, 'w_gate': w_gate, 'w_up': w_up, 'w_down': w_down}
    _L1_ffn_all = _L1_ffn_setup()
    _L1_ffn_in = {k: v for k, v in _L1_ffn_all.items() if k in ('gate_weight', 'w_gate', 'w_up', 'w_down')}
    del _L1_ffn_all
    return {'x': x, 'ctx_512': ctx_512, 'L0_xattn_W': _L0_xattn_in['W'], 'L0_xattn_b': _L0_xattn_in['b'], 'L0_ffn_gate_weight': _L0_ffn_in['gate_weight'], 'L0_ffn_gate_up_weights': _L0_ffn_in['gate_up_weights'], 'L0_ffn_down_weights': _L0_ffn_in['down_weights'], 'L0_ffn_shared_gate_up': _L0_ffn_in['shared_gate_up'], 'L0_ffn_shared_down': _L0_ffn_in['shared_down'], 'L1_xattn_Wq': _L1_xattn_in['Wq'], 'L1_xattn_Wk': _L1_xattn_in['Wk'], 'L1_xattn_gamma_raw': _L1_xattn_in['gamma_raw'], 'L1_ffn_gate_weight': _L1_ffn_in['gate_weight'], 'L1_ffn_w_gate': _L1_ffn_in['w_gate'], 'L1_ffn_w_up': _L1_ffn_in['w_up'], 'L1_ffn_w_down': _L1_ffn_in['w_down']}

def reference(x, ctx_512, L0_xattn_W, L0_xattn_b, L0_ffn_gate_weight, L0_ffn_gate_up_weights, L0_ffn_down_weights, L0_ffn_shared_gate_up, L0_ffn_shared_down, L1_xattn_Wq, L1_xattn_Wk, L1_xattn_gamma_raw, L1_ffn_gate_weight, L1_ffn_w_gate, L1_ffn_w_up, L1_ffn_w_down):
    import jax
    import jax.numpy as jnp

    def _L0_xattn_ref(x, adj, W, b):
        import jax, jax.numpy as jnp
        import numpy as np
        P_ASEM = 0.6
        D = x.shape[-1]
        Wi = W[:, :D]
        Wj = W[:, D:]
        si = jnp.einsum('bnd,d->bn', x, Wi[0])
        sj = jnp.einsum('bnd,d->bn', x, Wj[0])
        xij = jax.nn.sigmoid(si[:, :, None] + sj[:, None, :] + b[0])
        return P_ASEM * xij + (1.0 - P_ASEM) * adj

    def _L0_ffn_ref(hidden_states, gate_weight, gate_up_weights, down_weights, shared_gate_up, shared_down):
        import jax, jax.numpy as jnp
        import numpy as np
        TOP_K = 2
        B, S, H = hidden_states.shape
        E, twoF, _ = gate_up_weights.shape
        F = twoF // 2
        T = B * S
        x = hidden_states.reshape(T, H)
        logits = x @ gate_weight.T
        scores = jax.nn.softmax(logits, axis=-1)
        topk_w, topk_idx = jax.lax.top_k(scores, TOP_K)
        combine = jnp.zeros((T, E), x.dtype).at[jnp.arange(T)[:, None], topk_idx].add(topk_w)
        gu = jnp.einsum('th,efh->tef', x, gate_up_weights)
        act = jax.nn.silu(gu[..., :F]) * gu[..., F:]
        y = jnp.einsum('tef,te,ehf->th', act, combine, down_weights)
        Fs = shared_gate_up.shape[0] // 2
        sgu = x @ shared_gate_up.T
        sact = jax.nn.silu(sgu[:, :Fs]) * sgu[:, Fs:]
        y = y + sact @ shared_down.T
        return y.reshape(B, S, H)

    def _L1_xattn_ref(h, adj_raw, Wq, Wk, gamma_raw):
        import jax, jax.numpy as jnp
        import numpy as np
        B, N, D = (16, 256, 64)
        H = 4
        TOP_K_RATIO = 0.3
        b, n, dm = h.shape
        d = dm // H
        Q = (h @ Wq.T).reshape(b, n, H, d).transpose(0, 2, 1, 3)
        K = (h @ Wk.T).reshape(b, n, H, d).transpose(0, 2, 1, 3)
        sim = jnp.einsum('bhnd,bhmd->bnm', Q, K) / (jnp.sqrt(jnp.float32(d)) * H)
        k = max(1, int(n * TOP_K_RATIO))
        topk_vals = jax.lax.top_k(sim, k)[0]
        threshold = topk_vals[:, :, -1:]
        sparse_mask = (sim >= threshold).astype(sim.dtype)
        A_learned = jax.nn.sigmoid(sim) * sparse_mask
        A_learned = (A_learned + jnp.swapaxes(A_learned, -1, -2)) * 0.5
        gamma = jax.nn.sigmoid(gamma_raw)
        return (1.0 - gamma) * adj_raw + gamma * A_learned

    def _L1_ffn_ref(hidden_states, gate_weight, w_gate, w_up, w_down):
        import jax, jax.numpy as jnp
        import numpy as np
        B, S, H = (2, 256, 256)
        E, K, I = (64, 8, 96)

        def _moe_forward(hidden_states, gate_weight, w_gate, w_up, w_down):
            b, s, h = hidden_states.shape
            x = hidden_states.reshape(-1, h)
            logits = x.astype(jnp.float32) @ gate_weight.astype(jnp.float32).T
            scores = jax.nn.softmax(logits, axis=-1)
            topk_w, topk_idx = jax.lax.top_k(scores, K)
            topk_w = topk_w / jnp.sum(topk_w, axis=-1, keepdims=True)
            flat_ids = topk_idx.reshape(-1)
            expanded = jnp.repeat(x, K, axis=0)
            order = jnp.argsort(flat_ids)
            sorted_tokens = expanded[order]
            group_sizes = jnp.zeros((E,), jnp.int32).at[flat_ids].add(1)
            g = jax.lax.ragged_dot(sorted_tokens, w_gate, group_sizes)
            u = jax.lax.ragged_dot(sorted_tokens, w_up, group_sizes)
            out = jax.lax.ragged_dot(jax.nn.silu(g) * u, w_down, group_sizes)
            inv = jnp.argsort(order)
            outs = out[inv].reshape(-1, K, h)
            y = jnp.sum(outs * topk_w[:, :, None], axis=1)
            return y.reshape(b, s, h)
        return _moe_forward(hidden_states, gate_weight, w_gate, w_up, w_down)
    x = x + _L0_xattn_ref(ctx_512, _layernorm(x, axis=-1), L0_xattn_W, L0_xattn_b)
    x = x + _L0_ffn_ref(_layernorm(x, axis=-1), L0_ffn_gate_weight, L0_ffn_gate_up_weights, L0_ffn_down_weights, L0_ffn_shared_gate_up, L0_ffn_shared_down)
    x = x + _L1_xattn_ref(ctx_512, _layernorm(x, axis=-1), L1_xattn_Wq, L1_xattn_Wk, L1_xattn_gamma_raw)
    x = x + _L1_ffn_ref(_layernorm(x, axis=-1), L1_ffn_gate_weight, L1_ffn_w_gate, L1_ffn_w_up, L1_ffn_w_down)
    return x

_drawn_inputs = setup_inputs


def setup_inputs(seed=0):
    import zlib

    import numpy as np

    out = dict(_drawn_inputs(seed))
    spreads = {}
    factors = {'L0_ffn_gate_weight': 8.0,
     'L0_ffn_gate_up_weights': 8.0,
     'L0_ffn_down_weights': 8.0,
     'L1_ffn_gate_weight': 8.0,
     'L1_ffn_w_gate': 8.0,
     'L1_ffn_w_up': 8.0,
     'L1_ffn_w_down': 8.0,
     'L0_ffn_shared_gate_up': 7.864,
     'L0_ffn_shared_down': 8.0,
     'L1_xattn_Wq': 4.826,
     'L1_xattn_Wk': 4.775}
    for name, (base, spread) in spreads.items():
        noise = np.random.default_rng([zlib.crc32(name.encode()), seed]).standard_normal(out[name].shape)
        drawn = base * np.exp(spread * noise) if base else spread * noise
        out[name] = jnp.asarray(drawn.astype(out[name].dtype))
    for name, factor in factors.items():
        out[name] = (out[name] * factor).astype(out[name].dtype)
    return out
```

```python
from contextlib import ExitStack

import concourse.bass as bass
from concourse import mybir

F32 = mybir.dt.float32
I32 = mybir.dt.int32
U32 = mybir.dt.uint32
ALU = mybir.AluOpType
ACT = mybir.ActivationFunctionType
AX = mybir.AxisListType

P = 128
B, N, H = 4, 256, 256
D = 64
TILES = B * N // P
TPB = N // P
KH = H // P
EPS = 1e-5
P_ASEM = 0.6

E0, F0, FS = 8, 176, 352
Q0 = P // E0
RJ = F0 // Q0
SHARED = [P, P, FS - 2 * P]
NCH = len(SHARED) + RJ
NSH = len(SHARED)

TOPK = 76
ROUNDS8 = -(-TOPK // 8)
HEADS = 4
SIM_SCALE = 1.0 / ((D // HEADS) ** 0.5 * HEADS)

E1, K1, F1 = 64, 8, 96
CAP = 192
SH = CAP // 2
MORE = -(-(B * N) // CAP)
BIG = float(1 << 20)
RING = 4
UN = 2 * RING
NI = E1 // UN
LOWEST = -3.0e38


class Steps:

    def __init__(self, eng, sem, base=0):
        self.eng, self.sem, self.base, self.n = eng, sem, base, 0

    def add(self, ins):
        ins.then_inc(self.sem, 1)
        self.n += 1

    def wait(self):
        self.eng.wait_ge(self.sem, self.base + self.n)

    def link(self, *ins):
        for i in ins:
            self.add(i)
        self.wait()


SETUP_END = "setup"


def build(nc, x, ctx512, W, b0, g0w, gu0w, dn0w, sgu0w, sdn0w, Wq, Wk, gamma, g1w, wg1, wu1, wd1, out, stop=None):
    es = ExitStack()
    with es:
        def sb(name, shape, dt=F32):
            return es.enter_context(nc.sbuf_tensor(name, shape, dt))

        def sem(name):
            return es.enter_context(nc.semaphore(name))

        xs_dram = nc.dram_tensor("slots_in", [E1 * CAP, H], F32, kind="Internal").ap()
        fill = xs_dram.rearrange("(a p q) h -> a p (q h)", p=P, q=8)
        FILLS = E1 * CAP // (P * 8) - 1
        ys_dram = nc.dram_tensor("slots_out", [E1 * CAP, H], F32, kind="Internal").ap()
        fill_out = ys_dram.rearrange("(a p q) h -> a p (q h)", p=P, q=8)

        ident = sb("ident", [P, P])
        ones = sb("ones", [P, N])
        before = sb("before", [P, P])
        iota64 = sb("iota64", [P, E1])
        x1 = sb("x1", [P, TILES, H])
        ctx_sb = sb("ctx_sb", [P, TILES, D])
        ctxT = sb("ctxT", [D, B * N])
        w_ij = sb("w_ij", [D, 2])
        wi_b = sb("wi_b", [D, N])
        wj_b = sb("wj_b", [D, P])
        b_sb = sb("b_sb", [P, 2])
        wqk = sb("wqk", [D, 2, D])
        wqkT = sb("wqkT", [D, 2, D])
        gate0 = sb("gate0", [E0, H])
        gate0T = sb("gate0T", [P, KH, E0])
        gate1 = sb("gate1", [E1, H])
        gate1T = sb("gate1T", [P, KH, E1])
        gam = sb("gam", [P, 5])
        raw_gu = sb("raw_gu", [P, 2, RJ, H])
        raw_sgu = sb("raw_sgu", [P, 2, NSH, H])
        raw_dn = sb("raw_dn", [P, KH, E0, F0])
        raw_sdn = sb("raw_sdn", [P, KH, FS])
        w_gu = sb("w_gu", [P, NCH, KH, 2, P])
        w_dn = sb("w_dn", [P, NCH, H])
        st = sb("st", [P, TILES, 6])
        mv = sb("mv", [P, TILES, 2])
        rs = sb("rs", [P, TILES])
        sc = sb("sc", [P, TILES])
        of = sb("of", [P, TILES])
        xn = sb("xn", [P, TILES, H])
        xnT = sb("xnT", [P, KH, B * N])
        lg0 = sb("lg0", [P, TILES, E0])
        top0 = sb("top0", [P, TILES, 8])
        idx0 = sb("idx0", [P, TILES, 8], U32)
        idx0f = sb("idx0f", [P, TILES, 8])
        pr0 = sb("pr0", [P, TILES, E0])
        sum0 = sb("sum0", [P, TILES])
        eq0 = sb("eq0", [P, TILES, E0])
        eq1 = sb("eq1", [P, TILES, E0])
        comb_x = sb("comb_x", [P, TILES, E0, Q0])
        combT = sb("combT", [P, B * N])
        comb_b = sb("comb_b", [P, N])
        qT = sb("qT", [D, B * N])
        kT = sb("kT", [D, B * N])
        sim = sb("sim", [P, TILES, N])
        sim_t = sb("sim_t", [P, TILES, N])
        simw = sb("simw", [P, TPB, N])
        v8 = sb("v8", [P, TPB, 8])
        mask = sb("mask", [P, TPB, N])
        A = sb("A", [P, TPB, N])
        S = sb("S", [P, TPB, N])
        silu = sb("silu", [P, 2, N])
        silu_c = sb("silu_c", [P, 2, N])
        hid = sb("hid", [P, 7, N])
        x2 = sb("x2", [P, TPB, H])
        st2 = sb("st2", [P, TPB, 6])
        mv2 = sb("mv2", [P, TPB, 2])
        sm = sb("sm", [P, 4, TPB])
        x3 = sb("x3", [P, TILES, H])
        adj = x3
        xn3 = sb("xn3", [P, TPB, H])
        xn3_all = sb("xn3_all", [P, TILES, H])
        xn3T = sb("xn3T", [P, KH, N])
        lg1 = sb("lg1", [P, TPB, E1])
        lgr = sb("lgr", [P, TPB, E1])
        t8 = sb("t8", [P, TPB, K1])
        i8 = sb("i8", [P, TPB, K1], U32)
        i8f = sb("i8f", [P, TPB, K1])
        chosen = sb("chosen", [P, TPB, E1])
        chosen_sum = sb("chosen_sum", [P, E1])
        junk = sb("junk", [P, TPB * K1, E1])
        rk = sb("rk", [P, TPB, K1])
        ovf = sb("ovf", [P, TPB, K1])
        slf = sb("slf", [P, TPB, K1])
        slot = sb("slot", [P, TPB, K1], I32)

        zeros = xn3_all[:, :, :].rearrange("p t h -> p (t h)")
        flat_raw = raw_gu[:, :, :, :].rearrange("p g j h -> p (g j h)")
        W1, WD = RING * 4 * KH * F1, RING * 2 * H
        w1_sb = flat_raw[:, 0:W1].rearrange("p (a n g f) -> p a n g f", a=RING, n=2, g=2)
        wd_sb = flat_raw[0:F1, W1:W1 + WD].rearrange("p (a n h) -> p a n h", a=RING, n=2)
        flat_gu = w_gu[:, :, :, :, :].rearrange("p c k g f -> p (c k g f)")
        xs_sb = flat_gu[0:SH, 0:RING * 4 * H].rearrange("p (a n s h) -> p a n s h", a=RING, n=2, s=2)
        ys_sb = flat_gu[0:SH, RING * 4 * H:(RING + 2) * 4 * H].rearrange("p (a n s h) -> p a n s h", a=2, n=2, s=2)
        flat_dn = w_dn[:, :, :].rearrange("p c h -> p (c h)")
        xsT = flat_dn[:, 0:4 * CAP].rearrange("p (n k s) -> p n k s", n=2, k=KH)
        silu1 = flat_dn[0:F1, 4 * CAP:6 * CAP].rearrange("p (n s) -> p n s", n=2)
        hid1 = flat_dn[0:F1, 6 * CAP:8 * CAP].rearrange("p (n s) -> p n s", n=2)
        rank_all = sb("rank_all", [P, TILES, K1])
        exp_all = sb("exp_all", [P, TILES, K1])
        top_all = sb("top_all", [P, TILES, K1])
        wsum = sb("wsum", [P, TILES])
        valid = sb("valid", [P, TILES, K1])
        clamp = sb("clamp", [P, TILES, K1])
        w_now = sb("w_now", [P, TILES, K1])
        lg_all = raw_sgu[:, 0, :, :].rearrange("p c h -> p (c h)")[:, 0:TILES * E1].rearrange("p (t e) -> p t e", e=E1)
        max_all = sb("max_all", [P, TILES])
        levels = sb("levels", [P, K1])
        level_max = sb("level_max", [K1, 1])
        level_row = sb("level_row", [1, K1], I32)
        stores = sb("stores", [1, 2, K1], I32)
        slf_all = sb("slf_all", [P, TILES, K1])
        ovf_all = sb("ovf_all", [P, TILES, K1])
        gidx = sb("gidx", [P, TILES, K1], I32)
        gath = [x1, xn, xnT[:, :, :].rearrange("p k (a h) -> p (k a) h", h=H), sim, sim_t,
                raw_dn[:, :, :, :].rearrange("p k e f -> p (k e f)")[:, 0:TILES * H]
                .rearrange("p (t h) -> p t h", t=TILES)]
        cnt = sb("cnt", [P, 1])
        idle = sb("idle", [P, 1])
        more = sb("more", [P, 1], I32)

        bank = [es.enter_context(nc.psum_tensor(f"bank{i}", [P, 512], F32)) for i in range(8)]

        consts = sem("consts")
        ld_ctx = sem("ld_ctx")
        ld_x = [sem(f"ld_x{i}") for i in range(B)]
        ld_small = sem("ld_small")
        ld_sgu = sem("ld_sgu")
        ld_gu = sem("ld_gu")
        ld_dn = sem("ld_dn")
        act_steps = sem("act_steps")
        dve_steps = sem("dve_steps")
        pool_steps = sem("pool_steps")
        wij_ready = sem("wij_ready")
        ctx_tr = sem("ctx_tr")
        ctxT_ready = sem("ctxT_ready")
        small_tr = sem("small_tr")
        smallT_ready = sem("smallT_ready")
        z_ready = sem("z_ready")
        adj_ready = sem("adj_ready")
        qk_done = sem("qk_done")
        qkT_ready = sem("qkT_ready")
        sim_done = sem("sim_done")
        sim_ready = sem("sim_ready")
        xn_ready = sem("xn_ready")
        xn_tr = sem("xn_tr")
        xnT_ready = sem("xnT_ready")
        lg0_done = sem("lg0_done")
        lg0_read = sem("lg0_read")
        pr0_in = sem("pr0_in")
        pr0_ready = sem("pr0_ready")
        combx_ready = sem("combx_ready")
        comb_tr = sem("comb_tr")
        combT_ready = sem("combT_ready")
        wt_done = sem("wt_done")
        wt_ready = sem("wt_ready")
        gam_t = sem("gam_t")
        gu_done = sem("gu_done")
        silu_ready = sem("silu_ready")
        scaled_ready = sem("scaled_ready")
        hid_ready = sem("hid_ready")
        y_done = sem("y_done")
        y_read = sem("y_read")
        combb_ready = sem("combb_ready")
        topk_steps = sem("topk_steps")
        A_ready = sem("A_ready")
        AT_done = sem("AT_done")
        S_ready = sem("S_ready")
        tail_steps = sem("tail_steps")
        xn3_ready = sem("xn3_ready")
        xn3_tr = sem("xn3_tr")
        xn3T_ready = sem("xn3T_ready")
        xn3_kept = sem("xn3_kept")
        lg1_done = sem("lg1_done")
        lg1_read = sem("lg1_read")
        chosen_ready = sem("chosen_ready")
        rank_done = sem("rank_done")
        slot_ready = sem("slot_ready")
        sent = sem("sent")
        out_done = sem("out_done")
        zeros_ready = sem("zeros_ready")
        zero_fill = sem("zero_fill")
        zero_fill_out = sem("zero_fill_out")
        ld_w1 = [sem(f"ld_w1_{i}") for i in range(RING)]
        ld_xs = [sem(f"ld_xs_{i}") for i in range(RING)]
        st_ys = [sem(f"st_ys_{i}") for i in range(2)]
        xs_tr = sem("xs_tr")
        xsT_ready = sem("xsT_ready")
        gu1_done = sem("gu1_done")
        silu1_ready = sem("silu1_ready")
        hid1_ready = sem("hid1_ready")
        y1_done = sem("y1_done")
        ys_ready = sem("ys_ready")
        wexp_in = sem("wexp_in")
        wexp_ready = sem("wexp_ready")
        count_done = sem("count_done")
        more_ready = sem("more_ready")
        plan_steps = sem("plan_steps")
        acc_steps = sem("acc_steps")
        gidx_ready = sem("gidx_ready")
        levels_ready = sem("levels_ready")
        levels_tr = sem("levels_tr")
        level_max_ready = sem("level_max_ready")
        level_row_done = sem("level_row_done")
        stores_ready = sem("stores_ready")
        gathered = [sem(f"gathered_{i}") for i in range(K1 - 1)]
        gathered_last = [sem(f"gathered_last_{i}") for i in range(TILES)]
        level_added = sem("level_added")
        acc_done = sem("acc_done")
        staged = sem("staged")
        idled = sem("idled")
        sent_more = sem("sent_more")

        block = es.enter_context(nc.Block())

        def plain(eng):
            eng.wait_ge(zeros_ready, 2)

        def tiles_of(b):
            return bass.ds(b * TPB, TPB)

        @block.sync
        def _(sp):
            def dma(dst, src, s):
                return sp.dma_start(dst, src).then_inc(s, 16)

            dma(ctx_sb[:, :, :], ctx512.rearrange("b (t p) d -> p (b t) d", p=P), ld_ctx)
            for b in range(B):
                dma(x1[:, b * TPB:(b + 1) * TPB, :], x[b].rearrange("(t p) h -> p t h", p=P), ld_x[b])
            for g in range(2):
                dma(raw_sgu[:, g, 0:2, :], sgu0w[g * FS:g * FS + 2 * P, :].rearrange("(c p) h -> p c h", p=P), ld_sgu)
                dma(raw_sgu[0:SHARED[2], g, 2, :], sgu0w[g * FS + 2 * P:(g + 1) * FS, :], ld_sgu)
            for g in range(2):
                for e in range(E0):
                    dma(raw_gu[Q0 * e:Q0 * (e + 1), g, :, :].rearrange("q j h -> q (j h)"),
                        gu0w[e, g * F0:(g + 1) * F0, :].rearrange("(q j) h -> q (j h)", q=Q0), ld_gu)
            dma(raw_sdn[:, :, :], sdn0w.rearrange("(k p) f -> p k f", p=P), ld_dn)
            for k in range(KH):
                dma(raw_dn[:, k, :, :], dn0w[:, k * P:(k + 1) * P, :].rearrange("e p f -> p e f"), ld_dn)
            sp.wait_ge(zeros_ready, 2)
            for a in range(1, fill.shape[0]):
                dma(fill[a], zeros, zero_fill)
            for a in range(fill_out.shape[0]):
                dma(fill_out[a], zeros, zero_fill_out)

            w_dram = [v.rearrange("(p n) (q k) f -> p q n (k f)", n=2, k=KH) for v in (wg1, wu1)]
            wd_dram = wd1.rearrange("(p n) f h -> p f n h", n=2)
            xs_pair = xs_dram.rearrange("(p n q s) h -> p q n (s h)", n=2, q=SH, s=2)
            ys_pair = ys_dram.rearrange("(p n q s) h -> p q n (s h)", n=2, q=SH, s=2)
            out_tile = out.rearrange("b (t p) h -> (b t) p h", p=P)

            def one(v, p):
                return v[bass.ds(p, 1)].rearrange("a q n f -> (a q) n f")

            def load_weights(p, a):
                for g in range(2):
                    dma(w1_sb[:, a, :, g, :], one(w_dram[g], p), ld_w1[a])
                dma(wd_sb[:, a, :, :], one(wd_dram, p), ld_w1[a])

            def load_rows(p, a):
                dma(xs_sb[:, a, :, :, :].rearrange("p n s h -> p n (s h)"), one(xs_pair, p), ld_xs[a])

            def store_rows(r, p, a):
                sp.wait_ge(ys_ready, r * E1 + 2 * p + 2)
                plain(sp)
                dma(one(ys_pair, p), ys_sb[:, a % 2, :, :, :].rearrange("p n s h -> p n (s h)"), st_ys[a % 2])

            def experts(r):
                for a in range(RING):
                    load_rows(a, a)
                with sp.Fori(0, NI - 1) as i:
                    for a in range(RING):
                        sp.wait_ge(y1_done, r * E1 + UN * i + 2 * a + 2)
                        plain(sp)
                        load_rows(RING * (i + 1) + a, a)
                        load_weights(RING * (i + 1) + a, a)
                        store_rows(r, RING * i + a, a)
                for a in range(RING):
                    store_rows(r, E1 // 2 - RING + a, a)

            def results(r):
                with sp.Fori(0, TILES) as j:
                    sp.wait_ge(acc_done, r * TILES + j + 1)
                    plain(sp)
                    dma(out_tile[bass.ds(j, 1)].rearrange("a p h -> (a p) h"),
                        x3[:, bass.ds(j, 1), :].rearrange("p a h -> p (a h)"), out_done)

            sp.wait_ge(combT_ready, 2)
            sp.wait_ge(wt_ready, NCH + NCH // 2)
            for a in range(RING):
                load_weights(a, a)
            sp.wait_ge(zero_fill_out, 16 * fill_out.shape[0])
            sp.wait_ge(sent, 16 + 16 * TILES * K1)
            experts(0)
            results(0)
            sp.wait_ge(out_done, 16 * TILES)
            sp.wait_ge(more_ready, 1)
            again = sp.value_load(more[0:1, 0:1], min_val=0, max_val=1)
            with sp.If(again):
                with sp.Fori(1, MORE) as r:
                    sp.wait_ge(y1_done, r * E1)
                    plain(sp)
                    for a in range(RING):
                        load_weights(a, a)
                    sp.wait_ge(sent_more, r * 16 * TILES * K1)
                    plain(sp)
                    experts(r)
                    results(r)
                sp.wait_ge(out_done, MORE * 16 * TILES)

        @block.gpsimd
        def _(pool):
            pool.memset(idle[:, :], 0.0).then_inc(xn3_kept, 1)
            pool.memset(ident[:, :], 0.0).then_inc(pool_steps, 1)
            pool.memset(before[:, :], 1.0).then_inc(pool_steps, 1)
            pool.memset(ones[:, :], 1.0).then_inc(consts, 1)
            pool.memset(chosen_sum[:, :], 0.0).then_inc(consts, 1)
            pool.wait_ge(pool_steps, 2)
            pool.affine_select(out=ident[:, :], in_=ident[:, :], compare_op=ALU.not_equal, fill=1.0, base=0,
                               pattern=[[-1, P]], channel_multiplier=1).then_inc(consts, 1)
            pool.affine_select(out=before[:, :], in_=before[:, :], compare_op=ALU.is_gt, fill=0.0, base=0,
                               pattern=[[1, P]], channel_multiplier=-1).then_inc(consts, 1)
            pool.iota(iota64[:, :], pattern=[[1, E1]], base=0, channel_multiplier=0,
                      allow_small_or_imprecise_dtypes=True).then_inc(consts, 1)

            pool.wait_ge(xn3_kept, 1)
            for h in range(2):
                pool.memset(zeros[:, h * 1024:(h + 1) * 1024], 0.0).then_inc(zeros_ready, 1)

            pool.wait_ge(zeros_ready, 2)
            pool.dma_start(fill[0], zeros).then_inc(sent, 16)

            def body(b, tail):
                def scaled(c):
                    pool.wait_ge(silu_ready, b * NCH + c + 1)
                    pool.tensor_tensor(silu_c[:, c % 2, :], silu[:, c % 2, :], comb_b[:, :],
                                       ALU.mult).then_inc(scaled_ready, 1)

                pool.wait_ge(combb_ready, b + 1)
                for c in range(NSH, NCH):
                    if tail and c == 10:
                        pool.wait_ge(slot_ready, b)
                    scaled(c)
                    if tail and c >= 10:
                        send(b - 1, 2 * (c - 10), 2 * (c - 9))
                if tail:
                    send(b - 1, 2 * (NCH - 10), TPB * K1)

            def send(q, n0, n1):
                for n in range(n0, n1):
                    t, k = n // K1, n % K1
                    pool.indirect_dma_start(xs_dram, bass.IndirectOffsetOnAxis(ap=slot[:, t, k:k + 1], axis=0),
                                            xn3[:, t, :], None, bounds_check=E1 * CAP - 1,
                                            oob_is_err=False).then_inc(sent, 16)

            body(0, False)
            pool.wait_ge(zero_fill, 16 * FILLS)
            pool.wait_ge(sent, 16)
            with pool.Fori(1, B) as b:
                body(b, True)
            pool.wait_ge(slot_ready, B)
            send(B - 1, 0, TPB * K1)

            def idle_step():
                pool.tensor_tensor(idle[:, :], idle[:, :], idle[:, :], ALU.add).then_inc(idled, 1)
                pool.wait_ge(idled, 1)

            def gather_level(r, lv):
                if lv >= len(gath):
                    pool.sem_clear(idled)
                    pool.wait_ge(level_added, r * (K1 - 1) + lv - len(gath) + 1)
                    idle_step()
                for j in range(TILES):
                    pool.indirect_dma_start(gath[lv % len(gath)][:, j, :], None, ys_dram,
                                            bass.IndirectOffsetOnAxis(ap=gidx[:, j, K1 - 1 - lv:K1 - lv], axis=0))\
                        .then_inc(gathered[lv] if lv < K1 - 1 else gathered_last[j], 16)

            def gather_early():
                pool.wait_ge(gidx_ready, 1)
                pool.wait_ge(stores_ready, 2)
                for lv in range(K1):
                    for a in range(2):
                        if lv < K1 - 1:
                            k = K1 - 1 - lv
                            need = pool.value_load(stores[0:1, a, k:k + 1], min_val=16, max_val=16 * (E1 // 4))
                            pool.sem_clear(idled)
                            pool.wait_ge(st_ys[a], need)
                            idle_step()
                        else:
                            pool.wait_ge(st_ys[a], 16 * (E1 // 4))
                    gather_level(0, lv)

            def gather(r):
                for a in range(2):
                    pool.sem_clear(idled)
                    pool.wait_ge(st_ys[a], (r + 1) * 16 * (E1 // 4))
                    idle_step()
                pool.sem_clear(idled)
                pool.wait_ge(gidx_ready, r + 1)
                idle_step()
                for lv in range(K1):
                    gather_level(r, lv)

            gather_early()
            pool.wait_ge(more_ready, 1)
            again = pool.value_load(more[0:1, 0:1], min_val=0, max_val=1)
            with pool.If(again):
                with pool.Fori(1, MORE) as r:
                    with pool.Fori(0, TILES) as j:
                        pool.sem_clear(idled)
                        pool.wait_ge(staged, 2 * ((r - 1) * TILES + j + 1))
                        idle_step()
                        for k in range(K1):
                            pool.indirect_dma_start(xs_dram, bass.IndirectOffsetOnAxis(ap=slot[:, 0, k:k + 1], axis=0),
                                                    xn3[:, 0, :], None, bounds_check=E1 * CAP - 1,
                                                    oob_is_err=False).then_inc(sent_more, 16)
                    gather(r)

        @block.tensor
        def _(pe):
            pe.wait_ge(consts, 5)
            pe.wait_ge(ld_ctx, 16)
            for j in range(TILES):
                i = pe.transpose(bank[4 + j // 4][0:D, (j % 4) * P:(j % 4 + 1) * P], ctx_sb[:, j, :], ident[:, :])
                if j % 4 == 3:
                    i.then_inc(ctx_tr, 1)
            pe.wait_ge(ld_small, 16 * 7)
            for n in range(2):
                pe.transpose(bank[6][0:D, n * D:(n + 1) * D], wqk[:, n, :], ident[0:D, 0:D])
            for k in range(KH):
                pe.transpose(bank[6][:, 128 + k * E0:128 + (k + 1) * E0], gate0[:, k * P:(k + 1) * P],
                             ident[0:E0, 0:E0])
            for k in range(KH):
                i = pe.transpose(bank[6][:, 256 + k * E1:256 + (k + 1) * E1], gate1[:, k * P:(k + 1) * P],
                                 ident[0:E1, 0:E1])
            i.then_inc(small_tr, 1)
            pe.wait_ge(ctxT_ready, 2)
            pe.wait_ge(wij_ready, 2)
            pe.wait_ge(smallT_ready, 3)
            for b in range(B):
                for t in range(TPB):
                    z = bank[4 + b][:, t * N:(t + 1) * N]
                    j = b * TPB + t
                    pe.matmul(z, ctxT[:, j * P:(j + 1) * P], wi_b[:, :], start=True, stop=False)
                    i = pe.matmul(z, wj_b[:, :], ctxT[:, b * N:(b + 1) * N], start=False, stop=True)
                i.then_inc(z_ready, 1)
            for n in range(2):
                for h in range(2):
                    pe.wait_ge(adj_ready, 2 * n + h + 1)
                    pe.matmul(bank[4 + 2 * n + h][0:D, :], wqkT[:, n, :], ctxT[:, h * 512:(h + 1) * 512],
                              start=True, stop=True).then_inc(qk_done, 1)
            pe.wait_ge(qkT_ready, 4)
            for b in range(B):
                for t in range(TPB):
                    j = b * TPB + t
                    i = pe.matmul(bank[4 + b][:, t * N:(t + 1) * N], qT[:, j * P:(j + 1) * P],
                                  kT[:, b * N:(b + 1) * N], start=True, stop=True)
                i.then_inc(sim_done, 1)

            def transpose_weights(g):
                if g >= 4:
                    pe.wait_ge(wt_ready, g - 3)
                o = bank[g % 4]
                if g < NCH:
                    c = g
                    if c == 0:
                        pe.wait_ge(ld_sgu, 64)
                    if c == NSH:
                        pe.wait_ge(ld_gu, 16 * 2 * E0)
                    m = SHARED[c] if c < NSH else P
                    for k in range(KH):
                        for gu in range(2):
                            src = raw_sgu[0:m, gu, c, k * P:(k + 1) * P] if c < NSH else \
                                raw_gu[:, gu, c - NSH, k * P:(k + 1) * P]
                            i = pe.transpose(o[:, (k * 2 + gu) * P:(k * 2 + gu) * P + m], src, ident[0:m, 0:m])
                else:
                    if g == NCH:
                        pe.wait_ge(ld_dn, 48)
                    for n in range(2):
                        c = 2 * (g - NCH) + n
                        for k in range(KH):
                            if c < NSH:
                                m = SHARED[c]
                                src = raw_sdn[:, k, c * P:c * P + m]
                            else:
                                m = P
                                src = raw_dn[:, k, :, :].rearrange("p e (q j) -> p j (e q)", j=RJ)[:, c - NSH, :]
                            i = pe.transpose(o[0:m, (n * KH + k) * P:(n * KH + k + 1) * P], src, ident[:, :])
                i.then_inc(wt_done, 1)

            for b in range(B):
                pe.wait_ge(xn_ready, TPB * (b + 1))
                pe.wait_ge(sim_ready, 2 * (b + 1))
                for k in range(KH):
                    for t in range(TPB):
                        i = pe.transpose(bank[4 + b][:, k * N + t * P:k * N + (t + 1) * P],
                                         xn[:, b * TPB + t, k * P:(k + 1) * P], ident[:, :])
                i.then_inc(xn_tr, 1)
                for g in range(4 * b, 4 * b + 4):
                    transpose_weights(g)
            pe.wait_ge(xnT_ready, B)
            for j in range(TILES):
                for k in range(KH):
                    i = pe.matmul(bank[4][:, j * E0:(j + 1) * E0], xnT[:, k, j * P:(j + 1) * P], gate0T[:, k, :],
                                  start=(k == 0), stop=(k == KH - 1))
            i.then_inc(lg0_done, 1)
            for g in range(4 * B, NCH + NCH // 2):
                transpose_weights(g)
            pe.wait_ge(combx_ready, 1)
            for j in range(TILES):
                i = pe.transpose(bank[5 + j // 4][:, (j % 4) * P:(j % 4 + 1) * P],
                                 comb_x[:, j, :, :].rearrange("p e q -> p (e q)"), ident[:, :])
                if j % 4 == 3:
                    i.then_inc(comb_tr, 1)
            pe.wait_ge(wt_ready, NCH + NCH // 2)
            pe.wait_ge(combT_ready, 2)

            def gate_up(b, c, first):
                m = SHARED[c] if c < NSH else P
                if not (first and c < 2):
                    pe.wait_ge(hid_ready, b * NCH + c - 1)
                for gu in range(2):
                    for k in range(KH):
                        i = pe.matmul(bank[c % 2][0:m, gu * N:(gu + 1) * N], w_gu[:, c, k, gu, 0:m],
                                      xnT[:, k, bass.ds(b * N, N)], start=(k == 0), stop=(k == KH - 1))
                i.then_inc(gu_done, 1)

            def down(b, c, first):
                m = SHARED[c] if c < NSH else P
                pe.wait_ge(hid_ready, b * NCH + c + 1)
                if c == 0 and not first:
                    pe.wait_ge(y_read, b)
                for t in range(TPB):
                    i = pe.matmul(bank[2 + t][:, 0:H], hid[0:m, c % 7, t * P:(t + 1) * P], w_dn[0:m, c, :],
                                  start=(c == 0), stop=(c == NCH - 1))
                if c == NCH - 1:
                    i.then_inc(y_done, 1)

            def tail_transposes(q):
                pe.wait_ge(xn3_ready, q + 1)
                for k in range(KH):
                    for t in range(TPB):
                        i = pe.transpose(bank[4][:, k * N + t * P:k * N + (t + 1) * P],
                                         xn3[:, t, k * P:(k + 1) * P], ident[:, :])
                i.then_inc(xn3_tr, 1)

            def tail_logits(q):
                pe.wait_ge(xn3T_ready, q + 1)
                for t in range(TPB):
                    for k in range(KH):
                        i = pe.matmul(bank[5][:, t * E1:(t + 1) * E1], xn3T[:, k, t * P:(t + 1) * P],
                                      gate1T[:, k, :], start=(k == 0), stop=(k == KH - 1))
                i.then_inc(lg1_done, 1)

            def tail_ranks(q):
                pe.wait_ge(chosen_ready, q + 1)
                for t in range(TPB):
                    o = bank[5][:, (2 + t) * E1:(3 + t) * E1]
                    pe.matmul(o, before[:, :], chosen[:, t, :], start=True, stop=False)
                    if t == 1:
                        pe.matmul(o, ones[:, 0:P], chosen[:, 0, :], start=False, stop=False)
                    i = pe.matmul(o, ones[:, 0:P], chosen_sum[:, :], start=False, stop=True)
                i.then_inc(rank_done, 1)

            def turn_A(b):
                pe.wait_ge(A_ready, b + 1)
                for r in range(TPB):
                    for c in range(TPB):
                        i = pe.transpose(bank[6][:, c * N + r * P:c * N + (r + 1) * P],
                                         A[:, r, c * P:(c + 1) * P], ident[:, :])
                i.then_inc(AT_done, 1)

            def body(b, first):
                for c in range(NCH + 2):
                    if c < NCH:
                        gate_up(b, c, first)
                    if c >= 2:
                        down(b, c - 2, first)
                    if not first:
                        if c == 5:
                            tail_transposes(b - 1)
                        if c == 6:
                            tail_logits(b - 1)
                        if c == 8:
                            tail_ranks(b - 1)
                turn_A(b)

            body(0, True)
            with pe.Fori(1, B) as b:
                body(b, False)
            tail_transposes(B - 1)
            tail_logits(B - 1)
            tail_ranks(B - 1)
            pe.wait_ge(slot_ready, B)
            pe.matmul(bank[4][:, 0:E1], ones[:, 0:P], chosen_sum[:, :], start=True, stop=True)\
                .then_inc(count_done, 1)
            pe.wait_ge(levels_ready, 1)
            pe.transpose(bank[4][0:K1, P:2 * P], levels[:, :], ident[:, :]).then_inc(levels_tr, 1)
            pe.wait_ge(level_max_ready, 1)
            pe.matmul(bank[4][0:1, 2 * P:2 * P + K1], level_max[:, :], ident[0:K1, 0:K1], start=True, stop=True)\
                .then_inc(level_row_done, 1)

            def turn_rows(r, i, u):
                a, n = u // 2 % RING, u % 2
                if n == 0:
                    pe.wait_ge(ld_xs[a], (r * NI + i + u // UN + 1) * 16)
                if not (isinstance(r, int) and isinstance(i, int) and r == 0 and i == 0 and u < 2):
                    pe.wait_ge(xsT_ready, r * E1 + i * UN + u - 1)
                for k in range(KH):
                    for h in range(2):
                        ins = pe.transpose(bank[6 + n][:, k * CAP + h * SH:k * CAP + (h + 1) * SH],
                                           xs_sb[:, a, n, h, :].rearrange("p (q k) -> p k q", k=KH)[:, k, :],
                                           ident[0:SH, 0:SH])
                ins.then_inc(xs_tr, 1)

            def gate_up1(r, i, u, warm):
                a, n = u // 2, u % 2
                if n == 0:
                    pe.wait_ge(ld_w1[a], (r * NI + i + 1) * 48)
                if warm:
                    pe.wait_ge(hid1_ready, r * E1 + i * UN + u - 1)
                pe.wait_ge(xsT_ready, r * E1 + i * UN + u + 1)
                for g in range(2):
                    for k in range(KH):
                        ins = pe.matmul(bank[n][0:F1, g * CAP:(g + 1) * CAP],
                                        w1_sb[:, a, n, g, k * F1:(k + 1) * F1], xsT[:, n, k, :],
                                        start=(k == 0), stop=(k == KH - 1))
                ins.then_inc(gu1_done, 1)

            def down1(r, i, u, warm):
                a, n = u // 2 % RING, u % 2
                pe.wait_ge(hid1_ready, r * E1 + i * UN + u + 1)
                if warm:
                    pe.wait_ge(ys_ready, r * E1 + i * UN + u - 1)
                for h in range(2):
                    ins = pe.matmul(bank[2 + n][0:SH, h * H:(h + 1) * H], hid1[:, n, h * SH:(h + 1) * SH],
                                    wd_sb[:, a, n, :], start=True, stop=True)
                ins.then_inc(y1_done, 1)

            def experts(r):
                later = not isinstance(r, int)
                turn_rows(r, 0, 0)
                for u in range(UN):
                    turn_rows(r, 0, u + 1)
                    gate_up1(r, 0, u, u >= 2 or later)
                    if u >= 1:
                        down1(r, 0, u - 1, u >= 3 or later)
                with pe.Fori(1, NI - 1) as i:
                    for u in range(UN):
                        turn_rows(r, i, u + 1)
                        gate_up1(r, i, u, True)
                        down1(r, i, u - 1, True)
                for u in range(UN):
                    if u < UN - 1:
                        turn_rows(r, NI - 1, u + 1)
                    gate_up1(r, NI - 1, u, True)
                    down1(r, NI - 1, u - 1, True)
                down1(r, NI - 1, UN - 1, True)

            experts(0)
            pe.wait_ge(more_ready, 1)
            again = pe.value_load(more[0:1, 0:1], min_val=0, max_val=1)
            with pe.If(again):
                with pe.Fori(1, MORE) as r:
                    experts(r)

        @block.scalar
        def _(act):
            def dma(dst, src, s):
                return act.dma_start(dst, src).then_inc(s, 16)

            act.dma_start(w_ij[:, :], W.rearrange("a (n d) -> d (a n)", n=2), allow_slow_non_contiguous=True)\
               .then_inc(ld_small, 16)
            dma(b_sb[:, 0:1], b0.to_broadcast([P, 1]), ld_small)
            dma(gam[:, 0:1], gamma.to_broadcast([P, 1]), ld_small)
            dma(wqk[:, 0, :], Wq, ld_small)
            dma(wqk[:, 1, :], Wk, ld_small)
            dma(gate0[:, :], g0w, ld_small)
            dma(gate1[:, :], g1w, ld_small)
            for n in range(2):
                act.wait_ge(ctx_tr, n + 1)
                act.copy(ctxT[:, n * 512:(n + 1) * 512], bank[4 + n][0:D, :]).then_inc(ctxT_ready, 1)
            act.wait_ge(small_tr, 1)
            act.copy(wqkT[:, :, :].rearrange("p n d -> p (n d)"), bank[6][0:D, 0:128]).then_inc(smallT_ready, 1)
            act.copy(gate0T[:, :, :].rearrange("p k e -> p (k e)"), bank[6][:, 128:128 + KH * E0])\
               .then_inc(smallT_ready, 1)
            act.copy(gate1T[:, :, :].rearrange("p k e -> p (k e)"), bank[6][:, 256:256 + KH * E1])\
               .then_inc(smallT_ready, 1)
            act.wait_ge(ld_small, 16 * 7)
            act.activation(gam[:, 1:2], gam[:, 0:1], ACT.Tanh, scale=0.5).then_inc(gam_t, 1)
            act.wait_ge(wij_ready, 3)
            for b in range(B):
                act.wait_ge(z_ready, b + 1)
                act.activation(adj[:, b * TPB:(b + 1) * TPB, :].rearrange("p t n -> p (t n)"),
                               bank[4 + b][:, :], ACT.Tanh, bias=b_sb[:, 1:2], scale=0.5).then_inc(adj_ready, 1)
            for n in range(2):
                for h in range(2):
                    act.wait_ge(qk_done, 2 * n + h + 1)
                    act.copy((qT if n == 0 else kT)[:, h * 512:(h + 1) * 512], bank[4 + 2 * n + h][0:D, :])\
                       .then_inc(qkT_ready, 1)
            for b in range(B):
                act.wait_ge(sim_done, b + 1)
                dst = [v[:, b * TPB:(b + 1) * TPB, :].rearrange("p t n -> p (t n)") for v in (sim, sim_t)]
                act.mul(dst[0], bank[4 + b][:, :], SIM_SCALE).then_inc(sim_ready, 1)
                act.activation(dst[1], bank[4 + b][:, :], ACT.Tanh, scale=0.5 * SIM_SCALE).then_inc(sim_ready, 1)

            def keep_weights(g):
                act.wait_ge(wt_done, g + 1)
                o = bank[g % 4]
                if g < NCH:
                    m = SHARED[g] if g < NSH else P
                    act.copy(w_gu[:, g, :, :, 0:m].rearrange("p k g f -> p (k g) f"),
                             o[:, :].rearrange("p (n f) -> p n f", n=4)[:, :, 0:m]).then_inc(wt_ready, 1)
                elif 2 * (g - NCH) == 2:
                    m = SHARED[2]
                    act.copy(w_dn[0:m, 2, :], o[0:m, 0:H]).then_inc(act_steps, 1)
                    act.wait_ge(act_steps, 1)
                    act.copy(w_dn[:, 3, :], o[:, H:2 * H]).then_inc(wt_ready, 1)
                else:
                    c = 2 * (g - NCH)
                    act.copy(w_dn[:, c:c + 2, :].rearrange("p c h -> p (c h)"), o[:, :]).then_inc(wt_ready, 1)

            for b in range(B):
                act.wait_ge(xn_tr, b + 1)
                act.copy(xnT[:, :, b * N:(b + 1) * N], bank[4 + b][:, :].rearrange("p (k n) -> p k n", k=KH))\
                   .then_inc(xnT_ready, 1)
                for g in range(4 * b, 4 * b + 4):
                    keep_weights(g)
            act.wait_ge(pr0_in, 1)
            act.activation(pr0[:, :, :].rearrange("p t e -> p (t e)"), pr0[:, :, :].rearrange("p t e -> p (t e)"),
                           ACT.Exp).then_inc(pr0_ready, 1)
            for g in range(4 * B, NCH + NCH // 2):
                keep_weights(g)
            for n in range(2):
                act.wait_ge(comb_tr, n + 1)
                act.copy(combT[:, n * 512:(n + 1) * 512], bank[5 + n][:, :]).then_inc(combT_ready, 1)

            def keep_tail(q):
                act.wait_ge(xn3_tr, q + 1)
                act.copy(xn3T[:, :, :].rearrange("p k n -> p (k n)"), bank[4][:, :]).then_inc(xn3T_ready, 1)
                act.copy(xn3_all[:, tiles_of(q), :], xn3[:, :, :]).then_inc(xn3_kept, 1)

            def body(b, first):
                for c in range(NCH):
                    m = SHARED[c] if c < NSH else P
                    act.wait_ge(gu_done, b * NCH + c + 1)
                    act.activation(silu[0:m, c % 2, :], bank[c % 2][0:m, 0:N], ACT.Silu).then_inc(silu_ready, 1)
                    if c == 2:
                        act.copy(comb_b[:, :], combT[:, bass.ds(b * N, N)]).then_inc(combb_ready, 1)
                    if c == 6 and not first:
                        keep_tail(b - 1)

            body(0, True)
            act.wait_ge(zero_fill, 16 * FILLS)
            act.wait_ge(zero_fill_out, 16 * fill_out.shape[0])
            act.wait_ge(sent, 16)
            with act.Fori(1, B) as b:
                body(b, False)
            keep_tail(B - 1)
            act.wait_ge(wexp_in, 1)
            act.activation(top_all[:, :, :], top_all[:, :, :], ACT.Exp).then_inc(wexp_ready, 1)

            def gate(r, i, u):
                n = u % 2
                act.wait_ge(gu1_done, r * E1 + i * UN + u + 1)
                act.activation(silu1[:, n, :], bank[n][0:F1, 0:CAP], ACT.Silu).then_inc(silu1_ready, 1)

            def take(r, i, u):
                a, n = u // 2 % 2, u % 2
                if n == 0 and not (isinstance(i, int) and isinstance(r, int) and i == 0 and u < 4):
                    act.wait_ge(st_ys[a], (r * (E1 // 4) + i * (RING // 2) + u // 4) * 16)
                act.wait_ge(y1_done, r * E1 + i * UN + u + 1)
                act.copy(ys_sb[:, a, n, :, :].rearrange("p s h -> p (s h)"), bank[2 + n][0:SH, :])\
                   .then_inc(ys_ready, 1)

            def experts(r):
                for u in range(UN):
                    gate(r, 0, u)
                    if u >= 1:
                        take(r, 0, u - 1)
                with act.Fori(1, NI) as i:
                    for u in range(UN):
                        gate(r, i, u)
                        take(r, i, u - 1)
                take(r, NI - 1, UN - 1)

            experts(0)
            act.wait_ge(more_ready, 1)
            again = act.value_load(more[0:1, 0:1], min_val=0, max_val=1)
            with act.If(again):
                with act.Fori(1, MORE) as r:
                    experts(r)

        @block.vector
        def _(dve):
            s = Steps(dve, dve_steps)
            dve.wait_ge(consts, 5)
            dve.wait_ge(ld_small, 16 * 7)
            dve.tensor_scalar(wi_b[:, :], ones[0:D, :], w_ij[:, 0:1], None, ALU.mult).then_inc(wij_ready, 1)
            dve.tensor_scalar(wj_b[:, :], ones[0:D, 0:P], w_ij[:, 1:2], None, ALU.mult).then_inc(wij_ready, 1)
            dve.tensor_scalar(b_sb[:, 1:2], b_sb[:, 0:1], 0.5, None, ALU.mult).then_inc(wij_ready, 1)

            def rsqrt(s, y, var, v, t):
                s.link(dve.tensor_scalar(v, var, EPS, None, ALU.add))
                s.link(dve.tensor_scalar(y.bitcast(I32), v.bitcast(I32), 1, None, ALU.logical_shift_right))
                s.link(dve.tensor_scalar(y.bitcast(I32), y.bitcast(I32), -1.0, float(0x5F3759DF),
                                         ALU.mult, ALU.add))
                for _ in range(3):
                    s.link(dve.scalar_tensor_tensor(out=t, in0=y, scalar=-0.5, in1=y, op0=ALU.mult, op1=ALU.mult))
                    s.link(dve.tensor_tensor(t, t, v, ALU.mult))
                    s.link(dve.scalar_tensor_tensor(out=y, in0=t, scalar=1.5, in1=y, op0=ALU.add, op1=ALU.mult))

            def norm_stats(src, n, s, st, mv, rs, v, t):
                s.link(*[dve.bn_stats(st[:, j, :], src(j)) for j in range(n)])
                s.link(*[dve.bn_aggr(mv[:, j, :], st[:, j, :]) for j in range(n)])
                rsqrt(s, rs, mv[:, :, 1], v, t)

            for b in range(B):
                dve.wait_ge(ld_x[b], 16)
            norm_stats(lambda j: x1[:, j, :], TILES, s, st, mv, rs[:, :], sc[:, :], of[:, :])
            q = 1.0 - P_ASEM
            s.link(dve.tensor_scalar(sc[:, :], rs[:, :], q, 1.0, ALU.mult, ALU.add),
                   dve.scalar_tensor_tensor(out=of[:, :], in0=mv[:, :, 0], scalar=-q, in1=rs[:, :],
                                            op0=ALU.mult, op1=ALU.mult))
            s.link(dve.tensor_scalar(of[:, :], of[:, :], P_ASEM / 2, None, ALU.add))
            s.link(*[dve.tensor_scalar(x1[:, j, :], x1[:, j, :], sc[:, j:j + 1], of[:, j:j + 1],
                                       ALU.mult, ALU.add) for j in range(TILES)])
            for b in range(B):
                dve.wait_ge(adj_ready, b + 1)
                s.add(dve.scalar_tensor_tensor(out=x1[:, b * TPB:(b + 1) * TPB, :], in0=adj[:, b * TPB:(b + 1) * TPB, :],
                                               scalar=P_ASEM / 2, in1=x1[:, b * TPB:(b + 1) * TPB, :],
                                               op0=ALU.mult, op1=ALU.add))
            s.wait()
            norm_stats(lambda j: x1[:, j, :], TILES, s, st, mv, rs[:, :], sc[:, :], of[:, :])
            s.link(dve.scalar_tensor_tensor(out=of[:, :], in0=mv[:, :, 0], scalar=-1.0, in1=rs[:, :],
                                            op0=ALU.mult, op1=ALU.mult))
            for j in range(TILES):
                dve.tensor_scalar(xn[:, j, :], x1[:, j, :], rs[:, j:j + 1], of[:, j:j + 1],
                                  ALU.mult, ALU.add).then_inc(xn_ready, 1)
            dve.wait_ge(gam_t, 1)
            s.link(dve.tensor_scalar(gam[:, 2:3], gam[:, 1:2], 0.125, 0.125, ALU.mult, ALU.add),
                   dve.tensor_scalar(gam[:, 3:4], gam[:, 1:2], -0.5, 0.5, ALU.mult, ALU.add),
                   dve.tensor_scalar(gam[:, 4:5], gam[:, 1:2], 0.5, -0.5, ALU.mult, ALU.add))
            dve.wait_ge(lg0_done, 1)
            s.link(dve.tensor_copy(lg0[:, :, :].rearrange("p t e -> p (t e)"), bank[4][:, 0:TILES * E0]))
            s.link(*[dve.max(top0[:, j, :], lg0[:, j, :]) for j in range(TILES)])
            for j in range(TILES):
                s.add(dve.max_index(idx0[:, j, :], top0[:, j, :], lg0[:, j, :]))
            dve.tensor_tensor(pr0[:, :, :], lg0[:, :, :], top0[:, :, 0:1].to_broadcast([P, TILES, E0]),
                              ALU.subtract).then_inc(pr0_in, 1)
            s.wait()
            s.link(dve.tensor_copy(idx0f[:, :, :], idx0[:, :, :]))
            iota8 = iota64[:, 0:E0].unsqueeze(1).to_broadcast([P, TILES, E0])
            s.link(dve.tensor_tensor(eq0[:, :, :], iota8, idx0f[:, :, 0:1].to_broadcast([P, TILES, E0]),
                                     ALU.is_equal),
                   dve.tensor_tensor(eq1[:, :, :], iota8, idx0f[:, :, 1:2].to_broadcast([P, TILES, E0]),
                                     ALU.is_equal))
            s.link(dve.tensor_tensor(eq0[:, :, :], eq0[:, :, :], eq1[:, :, :], ALU.add))
            dve.wait_ge(pr0_ready, 1)
            s.link(dve.tensor_reduce(sum0[:, :], pr0[:, :, :], AX.X, ALU.add),
                   dve.tensor_tensor(eq0[:, :, :], eq0[:, :, :], pr0[:, :, :], ALU.mult))
            s.link(dve.reciprocal(sum0[:, :], sum0[:, :]))
            s.link(dve.tensor_tensor(eq0[:, :, :], eq0[:, :, :],
                                     sum0[:, :].unsqueeze(2).to_broadcast([P, TILES, E0]), ALU.mult))
            dve.tensor_copy(comb_x[:, :, :, :].rearrange("p t e q -> p (t e) q"),
                            eq0[:, :, :].rearrange("p t e -> p (t e)").unsqueeze(2)
                            .to_broadcast([P, TILES * E0, Q0])).then_inc(combx_ready, 1)

            dve.wait_ge(sim_ready, 2 * B)

            def hidden(b, c):
                m = SHARED[c] if c < NSH else P
                if c < NSH:
                    dve.wait_ge(silu_ready, b * NCH + c + 1)
                    src = silu
                else:
                    dve.wait_ge(scaled_ready, b * RJ + c - NSH + 1)
                    src = silu_c
                dve.tensor_tensor(hid[0:m, c % 7, :], src[0:m, c % 2, :], bank[c % 2][0:m, N:2 * N],
                                  ALU.mult).then_inc(hid_ready, 1)

            def topk(s, r0, r1):
                for r in range(r0, r1):
                    s.link(*[dve.max(v8[:, t, :], simw[:, t, :]) for t in range(TPB)])
                    if r < ROUNDS8 - 1:
                        s.link(*[dve.match_replace(simw[:, t, :], v8[:, t, :], simw[:, t, :], LOWEST)
                                 for t in range(TPB)])

            def learned(b, s):
                k = (TOPK - 1) % 8
                s.link(*[dve.tensor_scalar(mask[:, t, :], sim[:, bass.ds(b * TPB + t, 1), :]
                                           .rearrange("p a n -> p (a n)"), v8[:, t, k:k + 1],
                                           gam[:, 2:3], ALU.is_ge, ALU.mult) for t in range(TPB)])
                dve.scalar_tensor_tensor(out=A[:, :, :], in0=sim_t[:, tiles_of(b), :], scalar=1.0,
                                         in1=mask[:, :, :], op0=ALU.add, op1=ALU.mult).then_inc(A_ready, 1)
                dve.wait_ge(AT_done, b + 1)
                dve.tensor_tensor(S[:, :, :].rearrange("p t n -> p (t n)"), A[:, :, :].rearrange("p t n -> p (t n)"),
                                  bank[6][:, :], ALU.add).then_inc(S_ready, 1)

            def take_y(q, s):
                dve.wait_ge(y_done, q + 1)
                s.add(dve.tensor_tensor(x2[:, 0, :], bank[2][:, 0:H], x1[:, bass.ds(q * TPB, 1), :]
                                        .rearrange("p a n -> p (a n)"), ALU.add))
                dve.tensor_tensor(x2[:, 1, :], bank[3][:, 0:H], x1[:, bass.ds(q * TPB + 1, 1), :]
                                  .rearrange("p a n -> p (a n)"), ALU.add).then_inc(y_read, 1)
                dve.wait_ge(y_read, q + 1)
                s.wait()

            def x3_tile(q, t):
                return x3[:, bass.ds(q * TPB + t, 1), :].rearrange("p a n -> p (a n)")

            def mix(q, s):
                norm_stats(lambda t: x2[:, t, :], TPB, s, st2, mv2, sm[:, 0, :], sm[:, 1, :], sm[:, 2, :])
                s.link(dve.tensor_scalar(sm[:, 1, :], sm[:, 0, :], gam[:, 3:4], 1.0, ALU.mult, ALU.add),
                       dve.scalar_tensor_tensor(out=sm[:, 2, :], in0=mv2[:, :, 0], scalar=gam[:, 4:5],
                                                in1=sm[:, 0, :], op0=ALU.mult, op1=ALU.mult))
                s.link(*[dve.tensor_scalar(x2[:, t, :], x2[:, t, :], sm[:, 1, t:t + 1], sm[:, 2, t:t + 1],
                                           ALU.mult, ALU.add) for t in range(TPB)])
                dve.wait_ge(S_ready, q + 1)
                s.link(dve.tensor_tensor(x3[:, tiles_of(q), :], x2[:, :, :], S[:, :, :], ALU.add))

            def norm3(q, s, first):
                norm_stats(lambda t: x3_tile(q, t), TPB, s, st2, mv2, sm[:, 0, :], sm[:, 1, :], sm[:, 2, :])
                s.link(dve.scalar_tensor_tensor(out=sm[:, 1, :], in0=mv2[:, :, 0], scalar=-1.0, in1=sm[:, 0, :],
                                                op0=ALU.mult, op1=ALU.mult))
                if not first:
                    dve.wait_ge(sent, 16 + q * 16 * TPB * K1)
                    dve.wait_ge(xn3_kept, q + 1)
                s.link(dve.tensor_scalar(xn3[:, 0, :], x3_tile(q, 0), sm[:, 0, 0:1], sm[:, 1, 0:1],
                                         ALU.mult, ALU.add))
                dve.tensor_scalar(xn3[:, 1, :], x3_tile(q, 1), sm[:, 0, 1:2], sm[:, 1, 1:2],
                                  ALU.mult, ALU.add).then_inc(xn3_ready, 1)

            def choose(q, s):
                dve.wait_ge(lg1_done, q + 1)
                s.link(dve.tensor_copy(lg1[:, :, :].rearrange("p t e -> p (t e)"), bank[5][:, 0:TPB * E1]))
                s.link(*[dve.max(t8[:, t, :], lg1[:, t, :]) for t in range(TPB)])
                s.link(*[dve.match_replace(lgr[:, t, :], t8[:, t, :], lg1[:, t, :], LOWEST) for t in range(TPB)],
                       dve.tensor_scalar(lg_all[:, tiles_of(q), :], lg1[:, :, :], 1.0, None, ALU.mult))
                dve.tensor_tensor(chosen[:, :, :], lg1[:, :, :], lgr[:, :, :], ALU.not_equal)\
                   .then_inc(chosen_ready, 1)
                dve.wait_ge(chosen_ready, q + 1)
                s.link(*[dve.scalar_tensor_tensor(out=lgr[:, t, :], in0=iota64[:, :], scalar=1.0,
                                                  in1=chosen[:, t, :], op0=ALU.add, op1=ALU.mult)
                         for t in range(TPB)])
                s.link(*[dve.max(i8f[:, t, :], lgr[:, t, :]) for t in range(TPB)])
                s.link(dve.tensor_scalar(i8f[:, :, :], i8f[:, :, :], -1.0, None, ALU.add))

            def slots(q, s):
                dve.wait_ge(rank_done, q + 1)
                for t in range(TPB):
                    for k in range(K1):
                        s.add(dve.scalar_tensor_tensor(out=junk[:, t * K1 + k, :], in0=iota64[:, :],
                                                       scalar=i8f[:, t, k:k + 1],
                                                       in1=bank[5][:, (2 + t) * E1:(3 + t) * E1],
                                                       op0=ALU.is_equal, op1=ALU.mult, accum_out=rk[:, t, k:k + 1]))
                s.wait()
                s.link(*[dve.tensor_scalar(d[:, tiles_of(q), :], v[:, :, :], 1.0, None, ALU.mult)
                         for d, v in ((rank_all, rk), (exp_all, i8f), (top_all, t8))],
                       dve.tensor_scalar(ovf[:, :, :], rk[:, :, :], float(CAP), BIG, ALU.is_ge, ALU.mult),
                       dve.scalar_tensor_tensor(out=slf[:, :, :], in0=i8f[:, :, :], scalar=float(CAP),
                                                in1=rk[:, :, :], op0=ALU.mult, op1=ALU.add),
                       dve.tensor_tensor(chosen_sum[:, :], chosen_sum[:, :], chosen[:, 0, :], ALU.add))
                s.link(dve.tensor_tensor(chosen_sum[:, :], chosen_sum[:, :], chosen[:, 1, :], ALU.add))
                dve.tensor_tensor(slot[:, :, :], slf[:, :, :], ovf[:, :, :], ALU.add).then_inc(slot_ready, 1)

            def body(b, first):
                dve.sem_clear(topk_steps)
                s = Steps(dve, topk_steps)
                if not first:
                    dve.sem_clear(tail_steps)
                tl = Steps(dve, tail_steps)
                for c in range(NCH):
                    hidden(b, c)
                    if not first:
                        if c == 0:
                            take_y(b - 1, tl)
                        if c == 1:
                            mix(b - 1, tl)
                        if c == 3:
                            norm3(b - 1, tl, False)
                        if c == 6:
                            choose(b - 1, tl)
                        if c == 8:
                            slots(b - 1, tl)
                    if c == 7:
                        s.link(dve.tensor_scalar(simw[:, :, :], sim[:, tiles_of(b), :], 1.0, None, ALU.mult))
                    if 7 <= c < 12:
                        topk(s, 2 * (c - 7), 2 * (c - 6))
                learned(b, s)

            def plan_slots(s):
                s.link(dve.tensor_scalar(valid[:, :, :], rank_all[:, :, :], float(CAP), None, ALU.is_lt),
                       dve.tensor_scalar(clamp[:, :, :], rank_all[:, :, :], 0.0, float(CAP - 1), ALU.max, ALU.min))
                s.link(dve.scalar_tensor_tensor(out=valid[:, :, :], in0=rank_all[:, :, :], scalar=0.0,
                                                in1=valid[:, :, :], op0=ALU.is_ge, op1=ALU.mult))
                dve.scalar_tensor_tensor(out=gidx[:, :, :], in0=exp_all[:, :, :], scalar=float(CAP),
                                         in1=clamp[:, :, :], op0=ALU.mult, op1=ALU.add).then_inc(gidx_ready, 1)

            body(0, True)
            with dve.Fori(1, B) as b:
                body(b, False)
            dve.sem_clear(tail_steps)
            tl = Steps(dve, tail_steps)
            take_y(B - 1, tl)
            mix(B - 1, tl)
            norm3(B - 1, tl, False)
            choose(B - 1, tl)
            slots(B - 1, tl)
            dve.wait_ge(count_done, 1)
            tl.link(dve.tensor_reduce(cnt[:, :], bank[4][:, 0:E1], AX.X, ALU.max))
            dve.tensor_scalar(more[:, :], cnt[:, :], float(CAP), None, ALU.is_gt).then_inc(more_ready, 1)
            dve.tensor_reduce(levels[:, :], exp_all[:, :, :].rearrange("p t k -> p k t"), AX.X, ALU.max)\
               .then_inc(levels_ready, 1)
            tl.link(dve.tensor_copy(max_all[:, :], top_all[:, :, 0]))
            plan_slots(tl)
            dve.wait_ge(levels_tr, 1)
            dve.tensor_reduce(level_max[:, :], bank[4][0:K1, P:2 * P], AX.X, ALU.max).then_inc(level_max_ready, 1)
            dve.wait_ge(level_row_done, 1)
            tl.link(dve.tensor_copy(level_row[:, :], bank[4][0:1, 2 * P:2 * P + K1]))
            tl.link(dve.tensor_scalar(stores[:, 1, :], level_row[:, :], 2, None, ALU.add))
            tl.link(dve.tensor_scalar(stores[:, 0, :], level_row[:, :], 2, None, ALU.logical_shift_right),
                    dve.tensor_scalar(stores[:, 1, :], stores[:, 1, :], 2, None, ALU.logical_shift_right))
            dve.tensor_scalar(stores[:, 0, :], stores[:, 0, :], 16.0, 16.0, ALU.mult, ALU.add)\
               .then_inc(stores_ready, 1)
            dve.tensor_scalar(stores[:, 1, :], stores[:, 1, :], 16.0, 16.0, ALU.mult, ALU.max)\
               .then_inc(stores_ready, 1)
            for j in range(TILES):
                for k in range(K1):
                    tl.add(dve.scalar_tensor_tensor(out=junk[:, j % TPB * K1 + k, :], in0=iota64[:, :],
                                                    scalar=exp_all[:, j, k:k + 1], in1=lg_all[:, j, :],
                                                    op0=ALU.is_equal, op1=ALU.mult,
                                                    accum_out=top_all[:, j, k:k + 1]))
                if j % TPB == TPB - 1:
                    tl.wait()
            dve.tensor_tensor(top_all[:, :, :], top_all[:, :, :],
                              max_all[:, :].unsqueeze(2).to_broadcast([P, TILES, K1]),
                              ALU.subtract).then_inc(wexp_in, 1)
            dve.wait_ge(wexp_ready, 1)
            tl.link(dve.tensor_reduce(wsum[:, :], top_all[:, :, :], AX.X, ALU.add))
            tl.link(dve.reciprocal(wsum[:, :], wsum[:, :]))
            tl.link(dve.tensor_tensor(top_all[:, :, :], top_all[:, :, :],
                                      wsum[:, :].unsqueeze(2).to_broadcast([P, TILES, K1]), ALU.mult))
            tl.link(dve.tensor_tensor(w_now[:, :, :], valid[:, :, :], top_all[:, :, :], ALU.mult))

            def rows_out(r, i, u):
                n = u % 2
                dve.wait_ge(xs_tr, r * E1 + i * UN + u + 1)
                dve.tensor_copy(xsT[:, n, :, :].rearrange("p k s -> p (k s)"), bank[6 + n][:, 0:KH * CAP])\
                   .then_inc(xsT_ready, 1)

            def hidden1(r, i, u):
                n = u % 2
                dve.wait_ge(silu1_ready, r * E1 + i * UN + u + 1)
                dve.tensor_tensor(hid1[:, n, :], silu1[:, n, :], bank[n][0:F1, CAP:2 * CAP], ALU.mult)\
                   .then_inc(hid1_ready, 1)

            def experts(r):
                rows_out(r, 0, 0)
                rows_out(r, 0, 1)
                with dve.Fori(0, NI - 1) as i:
                    for u in range(UN):
                        hidden1(r, i, u)
                        rows_out(r, i, u + 2)
                for u in range(UN):
                    hidden1(r, NI - 1, u)
                    if u < UN - 2:
                        rows_out(r, NI - 1, u + 2)

            def combine(r):
                dve.sem_clear(acc_steps)
                steps = Steps(dve, acc_steps)
                for lv in range(K1):
                    last = lv == K1 - 1
                    if not last:
                        dve.wait_ge(gathered[lv], (r + 1) * 16 * TILES)
                    for j in range(TILES):
                        if last:
                            dve.wait_ge(gathered_last[j], (r + 1) * 16)
                        ins = dve.scalar_tensor_tensor(out=x3[:, j, :], in0=gath[lv % len(gath)][:, j, :],
                                                       scalar=w_now[:, j, K1 - 1 - lv:K1 - lv], in1=x3[:, j, :],
                                                       op0=ALU.mult, op1=ALU.add)
                        if last:
                            ins.then_inc(acc_done, 1)
                        elif j == TILES - 1:
                            ins.then_inc(level_added, 1)
                        else:
                            steps.add(ins)
                    if not last:
                        steps.wait()
                        dve.wait_ge(level_added, r * (K1 - 1) + lv + 1)

            experts(0)
            combine(0)
            dve.wait_ge(more_ready, 1)
            again = dve.value_load(more[0:1, 0:1], min_val=0, max_val=1)
            with dve.If(again):
                with dve.Fori(1, MORE) as r:
                    dve.wait_ge(out_done, r * 16 * TILES)
                    dve.memset(cnt[:, :], 0.0)
                    dve.sem_clear(plan_steps)
                    s2 = Steps(dve, plan_steps)
                    s2.link(dve.tensor_scalar(rank_all[:, :, :], rank_all[:, :, :], -float(CAP), None, ALU.add))
                    plan_slots(s2)
                    s2.link(dve.tensor_tensor(w_now[:, :, :], valid[:, :, :], top_all[:, :, :], ALU.mult))
                    s2.link(dve.tensor_scalar(ovf_all[:, :, :], valid[:, :, :], -BIG, BIG, ALU.mult, ALU.add),
                            dve.scalar_tensor_tensor(out=slf_all[:, :, :], in0=exp_all[:, :, :], scalar=float(CAP),
                                                     in1=clamp[:, :, :], op0=ALU.mult, op1=ALU.add))
                    s2.link(dve.tensor_tensor(slf_all[:, :, :], slf_all[:, :, :], ovf_all[:, :, :], ALU.add))
                    with dve.Fori(0, TILES) as j:
                        dve.wait_ge(sent, 16 + 16 * TILES * K1)
                        dve.tensor_scalar(slot[:, 0:1, :], slf_all[:, bass.ds(j, 1), :], 1.0, None, ALU.mult)\
                           .then_inc(staged, 1)
                        dve.tensor_scalar(xn3[:, 0:1, :], xn3_all[:, bass.ds(j, 1), :], 1.0, None, ALU.mult)\
                           .then_inc(staged, 1)
                        dve.wait_ge(sent_more, ((r - 1) * TILES + j + 1) * 16 * K1)
                        dve.memset(cnt[:, :], 0.0)
                    experts(r)
                    combine(r)


_INS = ['x', 'ctx_512', 'L0_xattn_W', 'L0_xattn_b', 'L0_ffn_gate_weight', 'L0_ffn_gate_up_weights',
        'L0_ffn_down_weights', 'L0_ffn_shared_gate_up', 'L0_ffn_shared_down', 'L1_xattn_Wq', 'L1_xattn_Wk',
        'L1_xattn_gamma_raw', 'L1_ffn_gate_weight', 'L1_ffn_w_gate', 'L1_ffn_w_up', 'L1_ffn_w_down']


def kernel(**inputs):
    import numpy as _np
    import concourse.bacc as _bacc
    from concourse import mybir as _mybir
    from concourse.bass_utils import run_bass_kernel_spmd as _run

    nc = _bacc.Bacc("TRN2", target_bir_lowering=False, num_devices=1)
    arrays, args = {}, []
    for name in _INS:
        a = _np.ascontiguousarray(inputs[name])
        if a.ndim < 2:
            a = a.reshape(1, 1)
        arrays[f"in_{name}_dram"] = a
        args.append(nc.dram_tensor(f"in_{name}_dram", a.shape, _mybir.dt.from_np(a.dtype), kind="ExternalInput").ap())
    args.append(nc.dram_tensor("out_0_dram", (B, N, H), F32, kind="ExternalOutput").ap())
    build(nc, *args)
    r = _run(nc, [arrays], core_ids=[0])
    return r.results[0]["out_0_dram"]
```

```python
from contextlib import ExitStack

import concourse.bass as bass
from concourse import mybir

F32 = mybir.dt.float32
I32 = mybir.dt.int32
U32 = mybir.dt.uint32
ALU = mybir.AluOpType
ACT = mybir.ActivationFunctionType
AX = mybir.AxisListType

P = 128
B, N, H = 4, 256, 256
D = 64
TILES = B * N // P
TPB = N // P
KH = H // P
EPS = 1e-5
P_ASEM = 0.6

E0, F0, FS = 8, 176, 352
Q0 = P // E0
RJ = F0 // Q0
SHARED = [P, P, FS - 2 * P]
NCH = len(SHARED) + RJ
NSH = len(SHARED)
FIRST_GROUPS = 4
HIDS = 5

TOPK = 76
ROUNDS8 = -(-TOPK // 8)
HEADS = 4
SIM_SCALE = 1.0 / ((D // HEADS) ** 0.5 * HEADS)

E1, K1, F1 = 64, 8, 96
CAP = 192
SH = CAP // 2
MORE = -(-(B * N) // CAP)
BIG = float(1 << 20)
RING = 4
UN = 2 * RING
NI = E1 // UN
LOWEST = -3.0e38
SEND = 11
EARLY = 5
MAXIMA0 = [1, 1, 1, 1, 1, 1, 1, 1, 1, 1, 1, 1, 1, 2]
FINISH = 5
MAXIMA = [0, 1, 0, 0, 1, 1, 2, 0, 1, 0, 0, 1, 2, 1]
assert EARLY + sum(MAXIMA0) == 2 * ROUNDS8 and EARLY + sum(MAXIMA0[:FINISH]) == ROUNDS8 == sum(MAXIMA)


class Steps:

    def __init__(self, eng, sem, base=0):
        self.eng, self.sem, self.base, self.n = eng, sem, base, 0

    def add(self, ins):
        ins.then_inc(self.sem, 1)
        self.n += 1

    def wait(self):
        self.eng.wait_ge(self.sem, self.base + self.n)

    def link(self, *ins):
        for i in ins:
            self.add(i)
        self.wait()


SETUP_END = "setup"


def build(nc, x, ctx512, W, b0, g0w, gu0w, dn0w, sgu0w, sdn0w, Wq, Wk, gamma, g1w, wg1, wu1, wd1, out, stop=None):
    es = ExitStack()
    with es:
        def sb(name, shape, dt=F32):
            return es.enter_context(nc.sbuf_tensor(name, shape, dt))

        def sem(name):
            return es.enter_context(nc.semaphore(name))

        xs_dram = nc.dram_tensor("slots_in", [E1 * CAP, H], F32, kind="Internal").ap()
        fill = xs_dram.rearrange("(a p q) h -> a p (q h)", p=P, q=8)
        FILLS = E1 * CAP // (P * 8) - 1
        ys_dram = nc.dram_tensor("slots_out", [E1 * CAP, H], F32, kind="Internal").ap()
        fill_out = ys_dram.rearrange("(a p q) h -> a p (q h)", p=P, q=8)

        ident = sb("ident", [P, P])
        ones = sb("ones", [P, N])
        before = sb("before", [P, P])
        iota64 = sb("iota64", [P, E1])
        x1 = sb("x1", [P, TILES, H])
        ctx_sb = sb("ctx_sb", [P, TILES, D])
        ctxT = sb("ctxT", [D, B * N])
        w_ij = sb("w_ij", [D, 2])
        wj_b = sb("wj_b", [D, P])
        b_sb = sb("b_sb", [P, 2])
        si = sb("si", [P, TILES])
        wqk = sb("wqk", [D, 2, D])
        wqkT = sb("wqkT", [D, 2, D])
        gate0 = sb("gate0", [E0, H])
        gate0T = sb("gate0T", [P, KH, E0])
        gate1 = sb("gate1", [E1, H])
        gate1T = sb("gate1T", [P, KH, E1])
        gam = sb("gam", [P, 5])
        raw_gu = sb("raw_gu", [P, 2, RJ, H])
        raw_sgu = sb("raw_sgu", [P, 2, NSH, H])
        raw_dn = sb("raw_dn", [P, KH, E0, F0])
        raw_sdn = sb("raw_sdn", [P, KH, FS])
        w_gu = sb("w_gu", [P, NCH, KH, 2, P])
        w_dn = sb("w_dn", [P, NCH, H])
        st = sb("st", [P, TILES, 6])
        mv = sb("mv", [P, TILES, 2])
        rs = sb("rs", [P, TILES])
        sc = sb("sc", [P, TILES])
        of = sb("of", [P, TILES])
        xn = sb("xn", [P, TILES, H])
        xnT = sb("xnT", [P, KH, B * N])
        lg0 = sb("lg0", [P, TILES, E0])
        top0 = sb("top0", [P, TILES, 8])
        idx0 = sb("idx0", [P, TILES, 8], U32)
        idx0f = sb("idx0f", [P, TILES, 8])
        pr0 = sb("pr0", [P, TILES, E0])
        sum0 = sb("sum0", [P, TILES])
        eq0 = sb("eq0", [P, TILES, E0])
        eq1 = sb("eq1", [P, TILES, E0])
        comb_x = sb("comb_x", [P, TILES, E0, Q0])
        combT = sb("combT", [P, B * N])
        comb_b = sb("comb_b", [P, N])
        qT = sb("qT", [D, B * N])
        kT = sb("kT", [D, B * N])
        sim = sb("sim", [P, TILES, N])
        sim_t = sb("sim_t", [P, TILES, N])
        simw = sb("simw", [P, TPB, N])
        v8 = sb("v8", [P, TPB, 8])
        least = sb("least", [P, TPB])
        A = sb("A", [P, TPB, N])
        S = sb("S", [P, TPB, N])
        silu = sb("silu", [P, 3, N])
        silu_c = sb("silu_c", [P, 3, N])
        hid = sb("hid", [P, HIDS, N])
        x2 = sb("x2", [P, TPB, H])
        st2 = sb("st2", [P, TPB, 6])
        mv2 = sb("mv2", [P, TPB, 2])
        sm = sb("sm", [P, 4, TPB])
        x3 = sb("x3", [P, TILES, H])
        adj = x3
        xn3 = sb("xn3", [P, TPB, H])
        rows = sb("rows", [P, TPB, H])
        xn3_all = sb("xn3_all", [P, TILES, H])
        xn3T = sb("xn3T", [P, KH, N])
        lg1 = sb("lg1", [P, TPB, E1])
        lgr = sb("lgr", [P, TPB, E1])
        t8 = sb("t8", [P, TPB, K1])
        i8f = sb("i8f", [P, TPB, K1])
        chosen = sb("chosen", [P, TPB, E1])
        chosen_sum = sb("chosen_sum", [P, E1])
        junk = comb_x[:, :, :, :].rearrange("p t e q -> p (t e q)").rearrange("p (n e) -> p n e", e=E1)
        rk = sb("rk", [P, TPB, K1])
        ovf = sb("ovf", [P, TPB, K1])
        slf = sb("slf", [P, TPB, K1])
        slot = sb("slot", [P, TPB, K1], I32)

        zeros = xn3_all[:, :, :].rearrange("p t h -> p (t h)")
        flat_raw = raw_gu[:, :, :, :].rearrange("p g j h -> p (g j h)")
        W1, WD = RING * 4 * KH * F1, RING * 2 * H
        w1_sb = flat_raw[:, 0:W1].rearrange("p (a n g f) -> p a n g f", a=RING, n=2, g=2)
        wd_sb = flat_raw[0:F1, W1:W1 + WD].rearrange("p (a n h) -> p a n h", a=RING, n=2)
        flat_gu = w_gu[:, :, :, :, :].rearrange("p c k g f -> p (c k g f)")
        xs_sb = flat_gu[0:SH, 0:RING * 4 * H].rearrange("p (a n s h) -> p a n s h", a=RING, n=2, s=2)
        ys_sb = flat_gu[0:SH, RING * 4 * H:(RING + 2) * 4 * H].rearrange("p (a n s h) -> p a n s h", a=2, n=2, s=2)
        flat_dn = w_dn[:, :, :].rearrange("p c h -> p (c h)")
        xsT = flat_dn[:, 0:4 * CAP].rearrange("p (n k s) -> p n k s", n=2, k=KH)
        silu1 = flat_dn[0:F1, 4 * CAP:6 * CAP].rearrange("p (n s) -> p n s", n=2)
        hid1 = flat_dn[0:F1, 6 * CAP:8 * CAP].rearrange("p (n s) -> p n s", n=2)
        rank_all = sb("rank_all", [P, TILES, K1])
        exp_all = sb("exp_all", [P, TILES, K1])
        top_all = sb("top_all", [P, TILES, K1])
        wsum = sb("wsum", [P, TILES])
        valid = sb("valid", [P, TILES, K1])
        clamp = sb("clamp", [P, TILES, K1])
        w_now = sb("w_now", [P, TILES, K1])
        lg_all = raw_sgu[:, 0, :, :].rearrange("p c h -> p (c h)")[:, 0:TILES * E1].rearrange("p (t e) -> p t e", e=E1)
        max_all = sb("max_all", [P, TILES])
        levels = sb("levels", [P, K1])
        level_max = sb("level_max", [K1, 1])
        level_row = sb("level_row", [1, K1], I32)
        stores = sb("stores", [1, 2, K1], I32)
        slf_all = sb("slf_all", [P, TILES, K1])
        ovf_all = sb("ovf_all", [P, TILES, K1])
        gidx = sb("gidx", [P, TILES, K1], I32)
        gath = [x1, xn, xnT[:, :, :].rearrange("p k (a h) -> p (k a) h", h=H), sim, sim_t,
                raw_dn[:, :, :, :].rearrange("p k e f -> p (k e f)")[:, 0:TILES * H]
                .rearrange("p (t h) -> p t h", t=TILES)]
        cnt = sb("cnt", [P, 1])
        idle = sb("idle", [P, 1])
        more = sb("more", [P, 1], I32)

        bank = [es.enter_context(nc.psum_tensor(f"bank{i}", [P, 512], F32)) for i in range(8)]

        gu_bank = [bank[0], bank[1], bank[7]]

        consts = sem("consts")
        ld_ctx = sem("ld_ctx")
        ld_x = [sem(f"ld_x{i}") for i in range(B)]
        ld_small = sem("ld_small")
        ld_gates = sem("ld_gates")
        qkw_tr = sem("qkw_tr")
        qkwT_ready = sem("qkwT_ready")
        si_done = sem("si_done")
        si_ready = sem("si_ready")
        ld_sgu = sem("ld_sgu")
        ld_gu = sem("ld_gu")
        ld_dn = sem("ld_dn")
        act_steps = sem("act_steps")
        dve_steps = sem("dve_steps")
        pool_steps = sem("pool_steps")
        wij_ready = sem("wij_ready")
        ctx_tr = sem("ctx_tr")
        ctxT_ready = sem("ctxT_ready")
        small_tr = sem("small_tr")
        smallT_ready = sem("smallT_ready")
        z_ready = sem("z_ready")
        adj_ready = sem("adj_ready")
        qk_done = sem("qk_done")
        qkT_ready = sem("qkT_ready")
        sim_done = sem("sim_done")
        sim_ready = sem("sim_ready")
        xn_ready = sem("xn_ready")
        xn_tr = sem("xn_tr")
        xnT_ready = sem("xnT_ready")
        lg0_done = sem("lg0_done")
        lg0_read = sem("lg0_read")
        pr0_in = sem("pr0_in")
        pr0_ready = sem("pr0_ready")
        combx_ready = sem("combx_ready")
        comb_tr = sem("comb_tr")
        combT_ready = sem("combT_ready")
        wt_done = sem("wt_done")
        wt_ready = sem("wt_ready")
        gam_t = sem("gam_t")
        gu_done = sem("gu_done")
        silu_ready = sem("silu_ready")
        scaled_ready = sem("scaled_ready")
        hid_ready = sem("hid_ready")
        y_done = sem("y_done")
        y_read = sem("y_read")
        combb_ready = sem("combb_ready")
        topk_steps = sem("topk_steps")
        A_ready = sem("A_ready")
        AT_done = sem("AT_done")
        S_ready = sem("S_ready")
        tail_steps = sem("tail_steps")
        xn3_ready = sem("xn3_ready")
        xn3_tr = sem("xn3_tr")
        xn3T_ready = sem("xn3T_ready")
        xn3_kept = sem("xn3_kept")
        rows_ready = sem("rows_ready")
        lg1_done = sem("lg1_done")
        lg1_read = sem("lg1_read")
        chosen_ready = sem("chosen_ready")
        rank_done = sem("rank_done")
        slot_ready = sem("slot_ready")
        sent = sem("sent")
        out_done = sem("out_done")
        zeros_ready = sem("zeros_ready")
        zero_fill = sem("zero_fill")
        zero_fill_out = sem("zero_fill_out")
        ld_w1 = [sem(f"ld_w1_{i}") for i in range(RING)]
        ld_xs = [sem(f"ld_xs_{i}") for i in range(RING)]
        st_ys = [sem(f"st_ys_{i}") for i in range(2)]
        xs_tr = sem("xs_tr")
        xsT_ready = sem("xsT_ready")
        gu1_done = sem("gu1_done")
        silu1_ready = sem("silu1_ready")
        hid1_ready = sem("hid1_ready")
        y1_done = sem("y1_done")
        ys_ready = sem("ys_ready")
        wexp_in = sem("wexp_in")
        wexp_ready = sem("wexp_ready")
        count_done = sem("count_done")
        more_ready = sem("more_ready")
        plan_steps = sem("plan_steps")
        acc_steps = sem("acc_steps")
        gidx_ready = sem("gidx_ready")
        levels_ready = sem("levels_ready")
        levels_tr = sem("levels_tr")
        level_max_ready = sem("level_max_ready")
        level_row_done = sem("level_row_done")
        stores_ready = sem("stores_ready")
        gathered = [sem(f"gathered_{i}") for i in range(K1 - 1)]
        gathered_last = [sem(f"gathered_last_{i}") for i in range(TILES)]
        level_added = sem("level_added")
        acc_done = sem("acc_done")
        staged = sem("staged")
        idled = sem("idled")
        sent_more = sem("sent_more")

        block = es.enter_context(nc.Block())

        def plain(eng):
            eng.wait_ge(zeros_ready, 2)

        def tiles_of(b):
            return bass.ds(b * TPB, TPB)

        @block.sync
        def _(sp):
            def dma(dst, src, s):
                return sp.dma_start(dst, src).then_inc(s, 16)

            dma(ctx_sb[:, :, :], ctx512.rearrange("b (t p) d -> p (b t) d", p=P), ld_ctx)
            for b in range(B):
                dma(x1[:, b * TPB:(b + 1) * TPB, :], x[b].rearrange("(t p) h -> p t h", p=P), ld_x[b])
            dma(gate0[:, :], g0w, ld_gates)
            dma(gate1[:, :], g1w, ld_gates)
            dma(gam[:, 0:1], gamma.to_broadcast([P, 1]), ld_gates)
            for g in range(2):
                dma(raw_sgu[:, g, 0:2, :], sgu0w[g * FS:g * FS + 2 * P, :].rearrange("(c p) h -> p c h", p=P), ld_sgu)
                dma(raw_sgu[0:SHARED[2], g, 2, :], sgu0w[g * FS + 2 * P:(g + 1) * FS, :], ld_sgu)
            for g in range(2):
                for e in range(E0):
                    dma(raw_gu[Q0 * e:Q0 * (e + 1), g, :, :].rearrange("q j h -> q (j h)"),
                        gu0w[e, g * F0:(g + 1) * F0, :].rearrange("(q j) h -> q (j h)", q=Q0), ld_gu)
            dma(raw_sdn[:, :, :], sdn0w.rearrange("(k p) f -> p k f", p=P), ld_dn)
            for k in range(KH):
                dma(raw_dn[:, k, :, :], dn0w[:, k * P:(k + 1) * P, :].rearrange("e p f -> p e f"), ld_dn)
            sp.wait_ge(zeros_ready, 2)
            for a in range(1, fill.shape[0]):
                dma(fill[a], zeros, zero_fill)
            for a in range(fill_out.shape[0]):
                dma(fill_out[a], zeros, zero_fill_out)

            w_dram = [v.rearrange("(p n) (q k) f -> p q n (k f)", n=2, k=KH) for v in (wg1, wu1)]
            wd_dram = wd1.rearrange("(p n) f h -> p f n h", n=2)
            xs_pair = xs_dram.rearrange("(p n q s) h -> p q n (s h)", n=2, q=SH, s=2)
            ys_pair = ys_dram.rearrange("(p n q s) h -> p q n (s h)", n=2, q=SH, s=2)
            out_tile = out.rearrange("b (t p) h -> (b t) p h", p=P)

            def one(v, p):
                return v[bass.ds(p, 1)].rearrange("a q n f -> (a q) n f")

            def load_weights(p, a):
                for g in range(2):
                    dma(w1_sb[:, a, :, g, :], one(w_dram[g], p), ld_w1[a])
                dma(wd_sb[:, a, :, :], one(wd_dram, p), ld_w1[a])

            def load_rows(p, a):
                dma(xs_sb[:, a, :, :, :].rearrange("p n s h -> p n (s h)"), one(xs_pair, p), ld_xs[a])

            def store_rows(r, p, a):
                sp.wait_ge(ys_ready, r * E1 + 2 * p + 2)
                plain(sp)
                dma(one(ys_pair, p), ys_sb[:, a % 2, :, :, :].rearrange("p n s h -> p n (s h)"), st_ys[a % 2])

            def experts(r):
                for a in range(RING):
                    load_rows(a, a)
                with sp.Fori(0, NI - 1) as i:
                    for a in range(RING):
                        sp.wait_ge(y1_done, r * E1 + UN * i + 2 * a + 2)
                        plain(sp)
                        load_rows(RING * (i + 1) + a, a)
                        load_weights(RING * (i + 1) + a, a)
                        store_rows(r, RING * i + a, a)
                for a in range(RING):
                    store_rows(r, E1 // 2 - RING + a, a)

            def results(r):
                with sp.Fori(0, TILES) as j:
                    sp.wait_ge(acc_done, r * TILES + j + 1)
                    plain(sp)
                    dma(out_tile[bass.ds(j, 1)].rearrange("a p h -> (a p) h"),
                        x3[:, bass.ds(j, 1), :].rearrange("p a h -> p (a h)"), out_done)

            sp.wait_ge(combT_ready, 2)
            sp.wait_ge(wt_ready, NCH + NCH // 2)
            for a in range(RING):
                load_weights(a, a)
            sp.wait_ge(zero_fill_out, 16 * fill_out.shape[0])
            sp.wait_ge(sent, 16 + 16 * TILES * K1)
            experts(0)
            results(0)
            sp.wait_ge(out_done, 16 * TILES)
            sp.wait_ge(more_ready, 1)
            again = sp.value_load(more[0:1, 0:1], min_val=0, max_val=1)
            with sp.If(again):
                with sp.Fori(1, MORE) as r:
                    sp.wait_ge(y1_done, r * E1)
                    plain(sp)
                    for a in range(RING):
                        load_weights(a, a)
                    sp.wait_ge(sent_more, r * 16 * TILES * K1)
                    plain(sp)
                    experts(r)
                    results(r)
                sp.wait_ge(out_done, MORE * 16 * TILES)

        @block.gpsimd
        def _(pool):
            pool.memset(idle[:, :], 0.0).then_inc(xn3_kept, 1)
            pool.memset(ident[:, :], 0.0).then_inc(pool_steps, 1)
            pool.memset(before[:, :], 1.0).then_inc(pool_steps, 1)
            pool.memset(ones[:, :], 1.0).then_inc(consts, 1)
            pool.memset(chosen_sum[:, :], 0.0).then_inc(consts, 1)
            pool.wait_ge(pool_steps, 2)
            pool.affine_select(out=ident[:, :], in_=ident[:, :], compare_op=ALU.not_equal, fill=1.0, base=0,
                               pattern=[[-1, P]], channel_multiplier=1).then_inc(consts, 1)
            pool.affine_select(out=before[:, :], in_=before[:, :], compare_op=ALU.is_gt, fill=0.0, base=0,
                               pattern=[[1, P]], channel_multiplier=-1).then_inc(consts, 1)
            pool.iota(iota64[:, :], pattern=[[1, E1]], base=0, channel_multiplier=0,
                      allow_small_or_imprecise_dtypes=True).then_inc(consts, 1)

            pool.wait_ge(xn3_kept, 1)
            for h in range(2):
                pool.memset(zeros[:, h * 1024:(h + 1) * 1024], 0.0).then_inc(zeros_ready, 1)

            pool.wait_ge(zeros_ready, 2)
            pool.wait_ge(ld_gu, 16 * 2 * E0)
            pool.dma_start(fill[0], zeros).then_inc(sent, 16)

            def body(b, tail):
                def scaled(c):
                    pool.wait_ge(silu_ready, b * NCH + c + 1)
                    pool.tensor_tensor(silu_c[:, c % 3, :], silu[:, c % 3, :], comb_b[:, :],
                                       ALU.mult).then_inc(scaled_ready, 1)

                pool.wait_ge(combb_ready, b + 1)
                for c in range(NSH, NCH):
                    if tail and c == SEND:
                        pool.wait_ge(rows_ready, b)
                        pool.wait_ge(slot_ready, b)
                    scaled(c)
                    if tail and c >= SEND:
                        send(b - 1, 2 * (c - SEND), 2 * (c - SEND + 1))
                if tail:
                    send(b - 1, 2 * (NCH - SEND), TPB * K1)

            def send(q, n0, n1):
                for n in range(n0, n1):
                    t, k = n // K1, n % K1
                    pool.indirect_dma_start(xs_dram, bass.IndirectOffsetOnAxis(ap=slot[:, t, k:k + 1], axis=0),
                                            rows[:, t, :], None, bounds_check=E1 * CAP - 1,
                                            oob_is_err=False).then_inc(sent, 16)

            body(0, False)
            pool.wait_ge(zero_fill, 16 * FILLS)
            pool.wait_ge(sent, 16)
            with pool.Fori(1, B) as b:
                body(b, True)
            pool.wait_ge(rows_ready, B)
            pool.wait_ge(slot_ready, B)
            send(B - 1, 0, TPB * K1)

            def idle_step():
                pool.tensor_tensor(idle[:, :], idle[:, :], idle[:, :], ALU.add).then_inc(idled, 1)
                pool.wait_ge(idled, 1)

            def gather_level(r, lv):
                if lv >= len(gath):
                    pool.sem_clear(idled)
                    pool.wait_ge(level_added, r * (K1 - 1) + lv - len(gath) + 1)
                    idle_step()
                for j in range(TILES):
                    pool.indirect_dma_start(gath[lv % len(gath)][:, j, :], None, ys_dram,
                                            bass.IndirectOffsetOnAxis(ap=gidx[:, j, K1 - 1 - lv:K1 - lv], axis=0))\
                        .then_inc(gathered[lv] if lv < K1 - 1 else gathered_last[j], 16)

            def gather_early():
                pool.wait_ge(gidx_ready, 1)
                pool.wait_ge(stores_ready, 2)
                for lv in range(K1):
                    for a in range(2):
                        if lv < K1 - 1:
                            k = K1 - 1 - lv
                            need = pool.value_load(stores[0:1, a, k:k + 1], min_val=16, max_val=16 * (E1 // 4))
                            pool.sem_clear(idled)
                            pool.wait_ge(st_ys[a], need)
                            idle_step()
                        else:
                            pool.wait_ge(st_ys[a], 16 * (E1 // 4))
                    gather_level(0, lv)

            def gather(r):
                for a in range(2):
                    pool.sem_clear(idled)
                    pool.wait_ge(st_ys[a], (r + 1) * 16 * (E1 // 4))
                    idle_step()
                pool.sem_clear(idled)
                pool.wait_ge(gidx_ready, r + 1)
                idle_step()
                for lv in range(K1):
                    gather_level(r, lv)

            gather_early()
            pool.wait_ge(more_ready, 1)
            again = pool.value_load(more[0:1, 0:1], min_val=0, max_val=1)
            with pool.If(again):
                with pool.Fori(1, MORE) as r:
                    with pool.Fori(0, TILES) as j:
                        pool.sem_clear(idled)
                        pool.wait_ge(staged, 2 * ((r - 1) * TILES + j + 1))
                        idle_step()
                        for k in range(K1):
                            pool.indirect_dma_start(xs_dram, bass.IndirectOffsetOnAxis(ap=slot[:, 0, k:k + 1], axis=0),
                                                    xn3[:, 0, :], None, bounds_check=E1 * CAP - 1,
                                                    oob_is_err=False).then_inc(sent_more, 16)
                    gather(r)

        @block.tensor
        def _(pe):
            pe.wait_ge(consts, 5)
            pe.wait_ge(ld_ctx, 16)
            for j in range(TILES):
                i = pe.transpose(bank[4 + j // 4][0:D, (j % 4) * P:(j % 4 + 1) * P], ctx_sb[:, j, :], ident[:, :])
                if j % 4 == 3:
                    i.then_inc(ctx_tr, 1)
            pe.wait_ge(ld_small, 16 * 4)
            for n in range(2):
                i = pe.transpose(bank[6][0:D, n * D:(n + 1) * D], wqk[:, n, :], ident[0:D, 0:D])
            i.then_inc(qkw_tr, 1)
            pe.wait_ge(ctxT_ready, 2)
            for j in range(TILES):
                i = pe.matmul(bank[7][:, j:j + 1], ctxT[:, j * P:(j + 1) * P], w_ij[:, 0:1], start=True, stop=True)
            i.then_inc(si_done, 1)
            pe.wait_ge(wij_ready, 2)
            for h in range(2):
                pe.matmul(bank[4 + h][:, :], wj_b[:, :], ctxT[:, h * 512:(h + 1) * 512], start=True, stop=True)\
                    .then_inc(z_ready, 1)
            pe.wait_ge(qkwT_ready, 1)
            pe.wait_ge(si_ready, 1)
            for n in (1, 0):
                for h in range(2):
                    if n == 0:
                        pe.wait_ge(adj_ready, 4 * h + 4)
                    pe.matmul(bank[4 + 2 * n + h][0:D, :], wqkT[:, n, :], ctxT[:, h * 512:(h + 1) * 512],
                              start=True, stop=True).then_inc(qk_done, 1)
            pe.wait_ge(ld_gates, 16 * 3)
            for k in range(KH):
                pe.transpose(bank[0][:, k * E0:(k + 1) * E0], gate0[:, k * P:(k + 1) * P], ident[0:E0, 0:E0])
            for k in range(KH):
                i = pe.transpose(bank[0][:, 256 + k * E1:256 + (k + 1) * E1], gate1[:, k * P:(k + 1) * P],
                                 ident[0:E1, 0:E1])
            i.then_inc(small_tr, 1)
            def transpose_weights(g):
                if g == 0:
                    pe.wait_ge(smallT_ready, 2)
                if g >= 4:
                    pe.wait_ge(wt_ready, g - 3)
                o = bank[g % 4]
                if g < NCH:
                    c = g
                    if c == 0:
                        pe.wait_ge(ld_sgu, 64)
                    if c == NSH:
                        pe.wait_ge(ld_gu, 16 * 2 * E0)
                    m = SHARED[c] if c < NSH else P
                    for k in range(KH):
                        for gu in range(2):
                            src = raw_sgu[0:m, gu, c, k * P:(k + 1) * P] if c < NSH else \
                                raw_gu[:, gu, c - NSH, k * P:(k + 1) * P]
                            i = pe.transpose(o[:, (k * 2 + gu) * P:(k * 2 + gu) * P + m], src, ident[0:m, 0:m])
                else:
                    if g == NCH:
                        pe.wait_ge(ld_dn, 48)
                    for n in range(2):
                        c = 2 * (g - NCH) + n
                        for k in range(KH):
                            if c < NSH:
                                m = SHARED[c]
                                src = raw_sdn[:, k, c * P:c * P + m]
                            else:
                                m = P
                                src = raw_dn[:, k, :, :].rearrange("p e (q j) -> p j (e q)", j=RJ)[:, c - NSH, :]
                            i = pe.transpose(o[0:m, (n * KH + k) * P:(n * KH + k + 1) * P], src, ident[:, :])
                i.then_inc(wt_done, 1)

            for g in range(FIRST_GROUPS):
                transpose_weights(g)
            pe.wait_ge(qkT_ready, 4)
            for b in range(B):
                for t in range(TPB):
                    j = b * TPB + t
                    i = pe.matmul(bank[4 + b][:, t * N:(t + 1) * N], qT[:, j * P:(j + 1) * P],
                                  kT[:, b * N:(b + 1) * N], start=True, stop=True)
                i.then_inc(sim_done, 1)

            for g in range(FIRST_GROUPS, 8):
                transpose_weights(g)
            for b in range(B):
                pe.wait_ge(xn_ready, TPB * (b + 1))
                pe.wait_ge(sim_ready, 2 * (b + 1))
                for k in range(KH):
                    for t in range(TPB):
                        i = pe.transpose(bank[4 + b][:, k * N + t * P:k * N + (t + 1) * P],
                                         xn[:, b * TPB + t, k * P:(k + 1) * P], ident[:, :])
                i.then_inc(xn_tr, 1)
                for g in range(8 + 2 * b, 10 + 2 * b):
                    transpose_weights(g)
            pe.wait_ge(xnT_ready, B)
            for j in range(TILES):
                for k in range(KH):
                    i = pe.matmul(bank[4][:, j * E0:(j + 1) * E0], xnT[:, k, j * P:(j + 1) * P], gate0T[:, k, :],
                                  start=(k == 0), stop=(k == KH - 1))
            i.then_inc(lg0_done, 1)
            for g in range(8 + 2 * B, NCH + NCH // 2):
                transpose_weights(g)
            pe.wait_ge(combx_ready, 1)
            for j in range(TILES):
                i = pe.transpose(bank[5 + j // 4][:, (j % 4) * P:(j % 4 + 1) * P],
                                 comb_x[:, j, :, :].rearrange("p e q -> p (e q)"), ident[:, :])
                if j % 4 == 3:
                    i.then_inc(comb_tr, 1)
            pe.wait_ge(wt_ready, NCH + NCH // 2)
            pe.wait_ge(combT_ready, 2)

            def gate_up(b, c, first):
                m = SHARED[c] if c < NSH else P
                if not (first and c < 3):
                    pe.wait_ge(hid_ready, b * NCH + (c - 1 if c < 2 else c - 2))
                for gu in range(2):
                    for k in range(KH):
                        i = pe.matmul(gu_bank[c % 3][0:m, gu * N:(gu + 1) * N], w_gu[:, c, k, gu, 0:m],
                                      xnT[:, k, bass.ds(b * N, N)], start=(k == 0), stop=(k == KH - 1))
                i.then_inc(gu_done, 1)

            def down(b, c, first):
                m = SHARED[c] if c < NSH else P
                pe.wait_ge(hid_ready, b * NCH + c + 1)
                if c == 0 and not first:
                    pe.wait_ge(y_read, b)
                for t in range(TPB):
                    i = pe.matmul(bank[2 + t][:, 0:H], hid[0:m, c % HIDS, t * P:(t + 1) * P], w_dn[0:m, c, :],
                                  start=(c == 0), stop=(c == NCH - 1))
                if c == NCH - 1:
                    i.then_inc(y_done, 1)

            def tail_transposes(q):
                pe.wait_ge(xn3_ready, q + 1)
                for k in range(KH):
                    for t in range(TPB):
                        i = pe.transpose(bank[4][:, k * N + t * P:k * N + (t + 1) * P],
                                         xn3[:, t, k * P:(k + 1) * P], ident[:, :])
                i.then_inc(xn3_tr, 1)

            def tail_logits(q):
                pe.wait_ge(xn3T_ready, q + 1)
                for t in range(TPB):
                    for k in range(KH):
                        i = pe.matmul(bank[5][:, t * E1:(t + 1) * E1], xn3T[:, k, t * P:(t + 1) * P],
                                      gate1T[:, k, :], start=(k == 0), stop=(k == KH - 1))
                i.then_inc(lg1_done, 1)

            def tail_ranks(q):
                pe.wait_ge(chosen_ready, q + 1)
                for t in range(TPB):
                    o = bank[5][:, (2 + t) * E1:(3 + t) * E1]
                    pe.matmul(o, before[:, :], chosen[:, t, :], start=True, stop=False)
                    if t == 1:
                        pe.matmul(o, ones[:, 0:P], chosen[:, 0, :], start=False, stop=False)
                    i = pe.matmul(o, ones[:, 0:P], chosen_sum[:, :], start=False, stop=True)
                i.then_inc(rank_done, 1)

            def turn_A(b):
                pe.wait_ge(A_ready, b + 1)
                for r in range(TPB):
                    for c in range(TPB):
                        i = pe.transpose(bank[6][:, c * N + r * P:c * N + (r + 1) * P],
                                         A[:, r, c * P:(c + 1) * P], ident[:, :])
                i.then_inc(AT_done, 1)

            def body(b, first, last=False):
                for c in range(2, NCH + 2):
                    if c < NCH:
                        gate_up(b, c, first)
                    elif not last:
                        gate_up(b + 1, c - NCH, False)
                    down(b, c - 2, first)
                    if last and c == NCH - 1:
                        turn_A(b)
                    if not first:
                        if c == 3:
                            turn_A(b - 1)
                        if c == 6:
                            tail_transposes(b - 1)
                        if c == 7:
                            tail_logits(b - 1)
                        if c == 9:
                            tail_ranks(b - 1)

            gate_up(0, 0, True)
            gate_up(0, 1, True)
            body(0, True)
            with pe.Fori(1, B - 1) as b:
                body(b, False)
            body(B - 1, False, True)
            tail_transposes(B - 1)
            tail_logits(B - 1)
            tail_ranks(B - 1)
            pe.wait_ge(slot_ready, B)
            pe.matmul(bank[4][:, 0:E1], ones[:, 0:P], chosen_sum[:, :], start=True, stop=True)\
                .then_inc(count_done, 1)
            pe.wait_ge(levels_ready, 1)
            pe.transpose(bank[4][0:K1, P:2 * P], levels[:, :], ident[:, :]).then_inc(levels_tr, 1)
            pe.wait_ge(level_max_ready, 1)
            pe.matmul(bank[4][0:1, 2 * P:2 * P + K1], level_max[:, :], ident[0:K1, 0:K1], start=True, stop=True)\
                .then_inc(level_row_done, 1)

            def turn_rows(r, i, u):
                a, n = u // 2 % RING, u % 2
                if n == 0:
                    pe.wait_ge(ld_xs[a], (r * NI + i + u // UN + 1) * 16)
                if not (isinstance(r, int) and isinstance(i, int) and r == 0 and i == 0 and u < 2):
                    pe.wait_ge(xsT_ready, r * E1 + i * UN + u - 1)
                for k in range(KH):
                    for h in range(2):
                        ins = pe.transpose(bank[6 + n][:, k * CAP + h * SH:k * CAP + (h + 1) * SH],
                                           xs_sb[:, a, n, h, :].rearrange("p (q k) -> p k q", k=KH)[:, k, :],
                                           ident[0:SH, 0:SH])
                ins.then_inc(xs_tr, 1)

            def gate_up1(r, i, u, warm):
                a, n = u // 2, u % 2
                if n == 0:
                    pe.wait_ge(ld_w1[a], (r * NI + i + 1) * 48)
                if warm:
                    pe.wait_ge(hid1_ready, r * E1 + i * UN + u - 1)
                pe.wait_ge(xsT_ready, r * E1 + i * UN + u + 1)
                for g in range(2):
                    for k in range(KH):
                        ins = pe.matmul(bank[n][0:F1, g * CAP:(g + 1) * CAP],
                                        w1_sb[:, a, n, g, k * F1:(k + 1) * F1], xsT[:, n, k, :],
                                        start=(k == 0), stop=(k == KH - 1))
                ins.then_inc(gu1_done, 1)

            def down1(r, i, u, warm):
                a, n = u // 2 % RING, u % 2
                pe.wait_ge(hid1_ready, r * E1 + i * UN + u + 1)
                if warm:
                    pe.wait_ge(ys_ready, r * E1 + i * UN + u - 1)
                for h in range(2):
                    ins = pe.matmul(bank[2 + n][0:SH, h * H:(h + 1) * H], hid1[:, n, h * SH:(h + 1) * SH],
                                    wd_sb[:, a, n, :], start=True, stop=True)
                ins.then_inc(y1_done, 1)

            def experts(r):
                later = not isinstance(r, int)
                turn_rows(r, 0, 0)
                for u in range(UN):
                    turn_rows(r, 0, u + 1)
                    gate_up1(r, 0, u, u >= 2 or later)
                    if u >= 1:
                        down1(r, 0, u - 1, u >= 3 or later)
                with pe.Fori(1, NI - 1) as i:
                    for u in range(UN):
                        turn_rows(r, i, u + 1)
                        gate_up1(r, i, u, True)
                        down1(r, i, u - 1, True)
                for u in range(UN):
                    if u < UN - 1:
                        turn_rows(r, NI - 1, u + 1)
                    gate_up1(r, NI - 1, u, True)
                    down1(r, NI - 1, u - 1, True)
                down1(r, NI - 1, UN - 1, True)

            experts(0)
            pe.wait_ge(more_ready, 1)
            again = pe.value_load(more[0:1, 0:1], min_val=0, max_val=1)
            with pe.If(again):
                with pe.Fori(1, MORE) as r:
                    experts(r)

        @block.scalar
        def _(act):
            def dma(dst, src, s):
                return act.dma_start(dst, src).then_inc(s, 16)

            act.dma_start(w_ij[:, :], W.rearrange("a (n d) -> d (a n)", n=2), allow_slow_non_contiguous=True)\
               .then_inc(ld_small, 16)
            dma(b_sb[:, 0:1], b0.to_broadcast([P, 1]), ld_small)
            dma(wqk[:, 0, :], Wq, ld_small)
            dma(wqk[:, 1, :], Wk, ld_small)
            for n in range(2):
                act.wait_ge(ctx_tr, n + 1)
                act.copy(ctxT[:, n * 512:(n + 1) * 512], bank[4 + n][0:D, :]).then_inc(ctxT_ready, 1)
            act.wait_ge(qkw_tr, 1)
            act.copy(wqkT[:, :, :].rearrange("p n d -> p (n d)"), bank[6][0:D, 0:128]).then_inc(qkwT_ready, 1)
            act.wait_ge(si_ready, 1)
            for j in range(TILES):
                act.wait_ge(z_ready, j // 4 + 1)
                act.activation(adj[:, j, :], bank[4 + j // 4][:, j // TPB % 2 * N:(j // TPB % 2 + 1) * N], ACT.Tanh,
                               bias=si[:, j:j + 1], scale=0.5).then_inc(adj_ready, 1)
            for i in range(4):
                n, h = 1 - i // 2, i % 2
                act.wait_ge(qk_done, i + 1)
                act.copy((qT if n == 0 else kT)[:, h * 512:(h + 1) * 512], bank[4 + 2 * n + h][0:D, :])\
                   .then_inc(qkT_ready, 1)
            act.wait_ge(small_tr, 1)
            act.copy(gate0T[:, :, :].rearrange("p k e -> p (k e)"), bank[0][:, 0:KH * E0]).then_inc(smallT_ready, 1)
            act.copy(gate1T[:, :, :].rearrange("p k e -> p (k e)"), bank[0][:, 256:256 + KH * E1])\
               .then_inc(smallT_ready, 1)
            act.activation(gam[:, 1:2], gam[:, 0:1], ACT.Tanh, scale=0.5).then_inc(gam_t, 1)

            def keep_weights(g):
                act.wait_ge(wt_done, g + 1)
                o = bank[g % 4]
                if g < NCH:
                    m = SHARED[g] if g < NSH else P
                    act.copy(w_gu[:, g, :, :, 0:m].rearrange("p k g f -> p (k g) f"),
                             o[:, :].rearrange("p (n f) -> p n f", n=4)[:, :, 0:m]).then_inc(wt_ready, 1)
                elif 2 * (g - NCH) == 2:
                    m = SHARED[2]
                    act.copy(w_dn[0:m, 2, :], o[0:m, 0:H]).then_inc(act_steps, 1)
                    act.wait_ge(act_steps, 1)
                    act.copy(w_dn[:, 3, :], o[:, H:2 * H]).then_inc(wt_ready, 1)
                else:
                    c = 2 * (g - NCH)
                    act.copy(w_dn[:, c:c + 2, :].rearrange("p c h -> p (c h)"), o[:, :]).then_inc(wt_ready, 1)

            for g in range(FIRST_GROUPS):
                keep_weights(g)
            for b in range(B):
                act.wait_ge(sim_done, b + 1)
                dst = [v[:, b * TPB:(b + 1) * TPB, :].rearrange("p t n -> p (t n)") for v in (sim, sim_t)]
                act.mul(dst[0], bank[4 + b][:, :], SIM_SCALE).then_inc(sim_ready, 1)
                act.activation(dst[1], bank[4 + b][:, :], ACT.Tanh, scale=0.5 * SIM_SCALE).then_inc(sim_ready, 1)
            for g in range(FIRST_GROUPS, 8):
                keep_weights(g)
            for b in range(B):
                act.wait_ge(xn_tr, b + 1)
                act.copy(xnT[:, :, b * N:(b + 1) * N], bank[4 + b][:, :].rearrange("p (k n) -> p k n", k=KH))\
                   .then_inc(xnT_ready, 1)
                for g in range(8 + 2 * b, 10 + 2 * b):
                    keep_weights(g)
            for g in range(8 + 2 * B, NCH + NCH // 2):
                keep_weights(g)
            act.wait_ge(pr0_in, 1)
            act.activation(pr0[:, :, :].rearrange("p t e -> p (t e)"), pr0[:, :, :].rearrange("p t e -> p (t e)"),
                           ACT.Exp).then_inc(pr0_ready, 1)
            for n in range(2):
                act.wait_ge(comb_tr, n + 1)
                act.copy(combT[:, n * 512:(n + 1) * 512], bank[5 + n][:, :]).then_inc(combT_ready, 1)

            def keep_tail(q):
                act.wait_ge(xn3_tr, q + 1)
                act.copy(xn3T[:, :, :].rearrange("p k n -> p (k n)"), bank[4][:, :]).then_inc(xn3T_ready, 1)

            def rows_to_send(q):
                act.wait_ge(sent, 16 + q * 16 * TPB * K1)
                act.copy(rows[:, :, :], xn3[:, :, :]).then_inc(rows_ready, 1)
                act.copy(xn3_all[:, tiles_of(q), :], xn3[:, :, :]).then_inc(xn3_kept, 1)

            def body(b, first):
                for c in range(NCH):
                    m = SHARED[c] if c < NSH else P
                    act.wait_ge(gu_done, b * NCH + c + 1)
                    act.activation(silu[0:m, c % 3, :], gu_bank[c % 3][0:m, 0:N], ACT.Silu).then_inc(silu_ready, 1)
                    if c == 2:
                        act.copy(comb_b[:, :], combT[:, bass.ds(b * N, N)]).then_inc(combb_ready, 1)
                    if c == 7 and not first:
                        keep_tail(b - 1)
                    if c == 10 and not first:
                        rows_to_send(b - 1)

            body(0, True)
            act.wait_ge(zero_fill, 16 * FILLS)
            act.wait_ge(zero_fill_out, 16 * fill_out.shape[0])
            act.wait_ge(sent, 16)
            with act.Fori(1, B) as b:
                body(b, False)
            keep_tail(B - 1)
            rows_to_send(B - 1)
            act.wait_ge(wexp_in, 1)
            act.activation(top_all[:, :, :], top_all[:, :, :], ACT.Exp).then_inc(wexp_ready, 1)

            def gate(r, i, u):
                n = u % 2
                act.wait_ge(gu1_done, r * E1 + i * UN + u + 1)
                act.activation(silu1[:, n, :], bank[n][0:F1, 0:CAP], ACT.Silu).then_inc(silu1_ready, 1)

            def take(r, i, u):
                a, n = u // 2 % 2, u % 2
                if n == 0 and not (isinstance(i, int) and isinstance(r, int) and i == 0 and u < 4):
                    act.wait_ge(st_ys[a], (r * (E1 // 4) + i * (RING // 2) + u // 4) * 16)
                act.wait_ge(y1_done, r * E1 + i * UN + u + 1)
                act.copy(ys_sb[:, a, n, :, :].rearrange("p s h -> p (s h)"), bank[2 + n][0:SH, :])\
                   .then_inc(ys_ready, 1)

            def experts(r):
                for u in range(UN):
                    gate(r, 0, u)
                    if u >= 1:
                        take(r, 0, u - 1)
                with act.Fori(1, NI) as i:
                    for u in range(UN):
                        gate(r, i, u)
                        take(r, i, u - 1)
                take(r, NI - 1, UN - 1)

            experts(0)
            act.wait_ge(more_ready, 1)
            again = act.value_load(more[0:1, 0:1], min_val=0, max_val=1)
            with act.If(again):
                with act.Fori(1, MORE) as r:
                    experts(r)

        @block.vector
        def _(dve):
            s = Steps(dve, dve_steps)
            dve.wait_ge(consts, 5)
            dve.wait_ge(ld_small, 16 * 4)
            dve.tensor_scalar(wj_b[:, :], ones[0:D, 0:P], w_ij[:, 1:2], None, ALU.mult).then_inc(wij_ready, 1)
            dve.tensor_scalar(b_sb[:, 1:2], b_sb[:, 0:1], 0.5, None, ALU.mult).then_inc(wij_ready, 1)
            dve.wait_ge(wij_ready, 2)
            dve.wait_ge(si_done, 1)
            dve.tensor_scalar(si[:, :], bank[7][:, 0:TILES], 0.5, b_sb[:, 1:2], ALU.mult, ALU.add)\
               .then_inc(si_ready, 1)

            def rsqrt(s, y, var, v, t):
                s.link(dve.tensor_scalar(v, var, EPS, None, ALU.add))
                s.link(dve.tensor_scalar(y.bitcast(I32), v.bitcast(I32), 1, None, ALU.logical_shift_right))
                s.link(dve.tensor_scalar(y.bitcast(I32), y.bitcast(I32), -1.0, float(0x5F3759DF),
                                         ALU.mult, ALU.add))
                for _ in range(3):
                    s.link(dve.scalar_tensor_tensor(out=t, in0=y, scalar=-0.5, in1=y, op0=ALU.mult, op1=ALU.mult))
                    s.link(dve.tensor_tensor(t, t, v, ALU.mult))
                    s.link(dve.scalar_tensor_tensor(out=y, in0=t, scalar=1.5, in1=y, op0=ALU.add, op1=ALU.mult))

            def norm_stats(src, n, s, st, mv, rs, v, t):
                s.link(*[dve.bn_stats(st[:, j, :], src(j)) for j in range(n)])
                s.link(*[dve.bn_aggr(mv[:, j, :], st[:, j, :]) for j in range(n)])
                rsqrt(s, rs, mv[:, :, 1], v, t)

            for b in range(B):
                dve.wait_ge(ld_x[b], 16)
            norm_stats(lambda j: x1[:, j, :], TILES, s, st, mv, rs[:, :], sc[:, :], of[:, :])
            q = 1.0 - P_ASEM
            s.link(dve.tensor_scalar(sc[:, :], rs[:, :], q, 1.0, ALU.mult, ALU.add),
                   dve.scalar_tensor_tensor(out=of[:, :], in0=mv[:, :, 0], scalar=-q, in1=rs[:, :],
                                            op0=ALU.mult, op1=ALU.mult))
            s.link(dve.tensor_scalar(of[:, :], of[:, :], P_ASEM / 2, None, ALU.add))
            s.link(*[dve.tensor_scalar(x1[:, j, :], x1[:, j, :], sc[:, j:j + 1], of[:, j:j + 1],
                                       ALU.mult, ALU.add) for j in range(TILES)])
            for b in range(B):
                dve.wait_ge(adj_ready, TPB * (b + 1))
                s.add(dve.scalar_tensor_tensor(out=x1[:, b * TPB:(b + 1) * TPB, :], in0=adj[:, b * TPB:(b + 1) * TPB, :],
                                               scalar=P_ASEM / 2, in1=x1[:, b * TPB:(b + 1) * TPB, :],
                                               op0=ALU.mult, op1=ALU.add))
            s.wait()
            norm_stats(lambda j: x1[:, j, :], TILES, s, st, mv, rs[:, :], sc[:, :], of[:, :])
            s.link(dve.scalar_tensor_tensor(out=of[:, :], in0=mv[:, :, 0], scalar=-1.0, in1=rs[:, :],
                                            op0=ALU.mult, op1=ALU.mult))
            for j in range(TILES):
                dve.tensor_scalar(xn[:, j, :], x1[:, j, :], rs[:, j:j + 1], of[:, j:j + 1],
                                  ALU.mult, ALU.add).then_inc(xn_ready, 1)
            dve.wait_ge(gam_t, 1)
            s.link(dve.tensor_scalar(gam[:, 2:3], gam[:, 1:2], 0.125, 0.125, ALU.mult, ALU.add),
                   dve.tensor_scalar(gam[:, 3:4], gam[:, 1:2], -0.5, 0.5, ALU.mult, ALU.add),
                   dve.tensor_scalar(gam[:, 4:5], gam[:, 1:2], 0.5, -0.5, ALU.mult, ALU.add))
            def topk_take(s, b):
                s.link(dve.tensor_scalar(simw[:, :, :], sim[:, tiles_of(b), :], 1.0, None, ALU.mult))

            def topk(s, rounds):
                for _ in range(rounds):
                    s.link(*[dve.max(v8[:, t, :], simw[:, t, :]) for t in range(TPB)])
                    s.link(*[dve.match_replace(simw[:, t, :], v8[:, t, :], simw[:, t, :], LOWEST)
                             for t in range(TPB)])

            def topk_keep(s):
                s.link(dve.tensor_copy(least[:, :], v8[:, :, (TOPK - 1) % 8]))

            dve.wait_ge(sim_ready, 2 * B)
            topk_take(s, 0)
            topk(s, EARLY)

            dve.wait_ge(lg0_done, 1)
            s.link(dve.tensor_copy(lg0[:, :, :].rearrange("p t e -> p (t e)"), bank[4][:, 0:TILES * E0]))
            s.link(*[dve.max(top0[:, j, :], lg0[:, j, :]) for j in range(TILES)])
            for j in range(TILES):
                s.add(dve.max_index(idx0[:, j, :], top0[:, j, :], lg0[:, j, :]))
            dve.tensor_tensor(pr0[:, :, :], lg0[:, :, :], top0[:, :, 0:1].to_broadcast([P, TILES, E0]),
                              ALU.subtract).then_inc(pr0_in, 1)
            s.wait()
            s.link(dve.tensor_copy(idx0f[:, :, :], idx0[:, :, :]))
            iota8 = iota64[:, 0:E0].unsqueeze(1).to_broadcast([P, TILES, E0])
            s.link(dve.tensor_tensor(eq0[:, :, :], iota8, idx0f[:, :, 0:1].to_broadcast([P, TILES, E0]),
                                     ALU.is_equal),
                   dve.tensor_tensor(eq1[:, :, :], iota8, idx0f[:, :, 1:2].to_broadcast([P, TILES, E0]),
                                     ALU.is_equal))
            s.link(dve.tensor_tensor(eq0[:, :, :], eq0[:, :, :], eq1[:, :, :], ALU.add))
            dve.wait_ge(pr0_ready, 1)
            s.link(dve.tensor_reduce(sum0[:, :], pr0[:, :, :], AX.X, ALU.add),
                   dve.tensor_tensor(eq0[:, :, :], eq0[:, :, :], pr0[:, :, :], ALU.mult))
            s.link(dve.reciprocal(sum0[:, :], sum0[:, :]))
            s.link(dve.tensor_tensor(eq0[:, :, :], eq0[:, :, :],
                                     sum0[:, :].unsqueeze(2).to_broadcast([P, TILES, E0]), ALU.mult))
            dve.tensor_copy(comb_x[:, :, :, :].rearrange("p t e q -> p (t e) q"),
                            eq0[:, :, :].rearrange("p t e -> p (t e)").unsqueeze(2)
                            .to_broadcast([P, TILES * E0, Q0])).then_inc(combx_ready, 1)
            s.link(*[dve.tensor_scalar(sim_t[:, j, :], sim_t[:, j, :], 1.0, gam[:, 2:3], ALU.add, ALU.mult)
                     for j in range(TILES)])

            def hidden(b, c):
                m = SHARED[c] if c < NSH else P
                if c < NSH:
                    dve.wait_ge(silu_ready, b * NCH + c + 1)
                    src = silu
                else:
                    dve.wait_ge(scaled_ready, b * RJ + c - NSH + 1)
                    src = silu_c
                dve.tensor_tensor(hid[0:m, c % HIDS, :], src[0:m, c % 3, :], gu_bank[c % 3][0:m, N:2 * N],
                                  ALU.mult).then_inc(hid_ready, 1)

            def learned(q, s):
                for t in range(TPB):
                    sim_tile, sig_tile = [v[:, bass.ds(q * TPB + t, 1), :].rearrange("p a n -> p (a n)")
                                          for v in (sim, sim_t)]
                    ins = dve.scalar_tensor_tensor(out=A[:, t, :], in0=sim_tile, scalar=least[:, t:t + 1],
                                                   in1=sig_tile, op0=ALU.is_ge, op1=ALU.mult)
                    if t < TPB - 1:
                        s.link(ins)
                ins.then_inc(A_ready, 1)
                dve.wait_ge(A_ready, q + 1)

            def mirror(q, s):
                dve.wait_ge(AT_done, q + 1)
                s.link(dve.tensor_tensor(S[:, :, :].rearrange("p t n -> p (t n)"),
                                         A[:, :, :].rearrange("p t n -> p (t n)"), bank[6][:, :], ALU.add))

            def take_y(q, s):
                dve.wait_ge(y_done, q + 1)
                s.add(dve.tensor_tensor(x2[:, 0, :], bank[2][:, 0:H], x1[:, bass.ds(q * TPB, 1), :]
                                        .rearrange("p a n -> p (a n)"), ALU.add))
                dve.tensor_tensor(x2[:, 1, :], bank[3][:, 0:H], x1[:, bass.ds(q * TPB + 1, 1), :]
                                  .rearrange("p a n -> p (a n)"), ALU.add).then_inc(y_read, 1)
                dve.wait_ge(y_read, q + 1)
                s.wait()

            def x3_tile(q, t):
                return x3[:, bass.ds(q * TPB + t, 1), :].rearrange("p a n -> p (a n)")

            def mix(q, s, mirrored=False):
                norm_stats(lambda t: x2[:, t, :], TPB, s, st2, mv2, sm[:, 0, :], sm[:, 1, :], sm[:, 2, :])
                s.link(dve.tensor_scalar(sm[:, 1, :], sm[:, 0, :], gam[:, 3:4], 1.0, ALU.mult, ALU.add),
                       dve.scalar_tensor_tensor(out=sm[:, 2, :], in0=mv2[:, :, 0], scalar=gam[:, 4:5],
                                                in1=sm[:, 0, :], op0=ALU.mult, op1=ALU.mult))
                s.link(*[dve.tensor_scalar(x2[:, t, :], x2[:, t, :], sm[:, 1, t:t + 1], sm[:, 2, t:t + 1],
                                           ALU.mult, ALU.add) for t in range(TPB)])
                if not mirrored:
                    mirror(q, s)
                s.link(dve.tensor_tensor(x3[:, tiles_of(q), :], x2[:, :, :], S[:, :, :], ALU.add))

            def norm3(q, s, first):
                norm_stats(lambda t: x3_tile(q, t), TPB, s, st2, mv2, sm[:, 0, :], sm[:, 1, :], sm[:, 2, :])
                s.link(dve.scalar_tensor_tensor(out=sm[:, 1, :], in0=mv2[:, :, 0], scalar=-1.0, in1=sm[:, 0, :],
                                                op0=ALU.mult, op1=ALU.mult))
                if not first:
                    dve.wait_ge(xn3_kept, q + 1)
                s.link(dve.tensor_scalar(xn3[:, 0, :], x3_tile(q, 0), sm[:, 0, 0:1], sm[:, 1, 0:1],
                                         ALU.mult, ALU.add))
                dve.tensor_scalar(xn3[:, 1, :], x3_tile(q, 1), sm[:, 0, 1:2], sm[:, 1, 1:2],
                                  ALU.mult, ALU.add).then_inc(xn3_ready, 1)

            def choose(q, s):
                dve.wait_ge(lg1_done, q + 1)
                s.link(dve.tensor_copy(lg1[:, :, :].rearrange("p t e -> p (t e)"), bank[5][:, 0:TPB * E1]))
                s.link(*[dve.max(t8[:, t, :], lg1[:, t, :]) for t in range(TPB)])
                s.link(*[dve.match_replace(lgr[:, t, :], t8[:, t, :], lg1[:, t, :], LOWEST) for t in range(TPB)],
                       dve.tensor_scalar(lg_all[:, tiles_of(q), :], lg1[:, :, :], 1.0, None, ALU.mult))
                dve.tensor_tensor(chosen[:, :, :], lg1[:, :, :], lgr[:, :, :], ALU.not_equal)\
                   .then_inc(chosen_ready, 1)
                dve.wait_ge(chosen_ready, q + 1)
                s.link(*[dve.scalar_tensor_tensor(out=lgr[:, t, :], in0=iota64[:, :], scalar=1.0,
                                                  in1=chosen[:, t, :], op0=ALU.add, op1=ALU.mult)
                         for t in range(TPB)])
                s.link(*[dve.max(i8f[:, t, :], lgr[:, t, :]) for t in range(TPB)])
                s.link(dve.tensor_scalar(i8f[:, :, :], i8f[:, :, :], -1.0, None, ALU.add))

            def ranks(q, s, ts):
                dve.wait_ge(rank_done, q + 1)
                for t in ts:
                    for k in range(K1):
                        s.add(dve.scalar_tensor_tensor(out=junk[:, t * K1 + k, :], in0=iota64[:, :],
                                                       scalar=i8f[:, t, k:k + 1],
                                                       in1=bank[5][:, (2 + t) * E1:(3 + t) * E1],
                                                       op0=ALU.is_equal, op1=ALU.mult, accum_out=rk[:, t, k:k + 1]))

            def slots(q, s, first):
                s.wait()
                s.link(*[dve.tensor_scalar(d[:, tiles_of(q), :], v[:, :, :], 1.0, None, ALU.mult)
                         for d, v in ((rank_all, rk), (exp_all, i8f), (top_all, t8))],
                       dve.tensor_scalar(ovf[:, :, :], rk[:, :, :], float(CAP), BIG, ALU.is_ge, ALU.mult),
                       dve.scalar_tensor_tensor(out=slf[:, :, :], in0=i8f[:, :, :], scalar=float(CAP),
                                                in1=rk[:, :, :], op0=ALU.mult, op1=ALU.add),
                       dve.tensor_tensor(chosen_sum[:, :], chosen_sum[:, :], chosen[:, 0, :], ALU.add))
                s.link(dve.tensor_tensor(chosen_sum[:, :], chosen_sum[:, :], chosen[:, 1, :], ALU.add))
                if not first:
                    dve.wait_ge(sent, 16 + q * 16 * TPB * K1)
                dve.tensor_tensor(slot[:, :, :], slf[:, :, :], ovf[:, :, :], ALU.add).then_inc(slot_ready, 1)

            def plan_slots(s):
                s.link(dve.tensor_scalar(valid[:, :, :], rank_all[:, :, :], float(CAP), None, ALU.is_lt),
                       dve.tensor_scalar(clamp[:, :, :], rank_all[:, :, :], 0.0, float(CAP - 1), ALU.max, ALU.min))
                s.link(dve.scalar_tensor_tensor(out=valid[:, :, :], in0=rank_all[:, :, :], scalar=0.0,
                                                in1=valid[:, :, :], op0=ALU.is_ge, op1=ALU.mult))
                dve.scalar_tensor_tensor(out=gidx[:, :, :], in0=exp_all[:, :, :], scalar=float(CAP),
                                         in1=clamp[:, :, :], op0=ALU.mult, op1=ALU.add).then_inc(gidx_ready, 1)

            def body(b, first, last=False):
                dve.sem_clear(topk_steps)
                s = Steps(dve, topk_steps)
                if not first:
                    dve.sem_clear(tail_steps)
                tl = Steps(dve, tail_steps)
                for c in range(NCH):
                    hidden(b, c)
                    if not first:
                        if c == 0:
                            take_y(b - 1, tl)
                            learned(b - 1, tl)
                        if c == 2:
                            mix(b - 1, tl)
                        if c == 3:
                            norm3(b - 1, tl, False)
                        if c == 7:
                            choose(b - 1, tl)
                        if c == 9:
                            ranks(b - 1, tl, (0,))
                        if c == 10:
                            ranks(b - 1, tl, (1,))
                            slots(b - 1, tl, False)
                    if first:
                        if c == FINISH:
                            topk_keep(s)
                            topk_take(s, 1)
                        topk(s, MAXIMA0[c])
                    else:
                        if c == 0:
                            topk_keep(s)
                            if not last:
                                topk_take(s, b + 1)
                        if not last:
                            topk(s, MAXIMA[c])
                    if last and c == 11:
                        learned(b, tl)
                    if last and c == NCH - 1:
                        mirror(b, tl)
            body(0, True)
            with dve.Fori(1, B - 1) as b:
                body(b, False)
            body(B - 1, False, True)
            dve.sem_clear(tail_steps)
            tl = Steps(dve, tail_steps)
            take_y(B - 1, tl)
            mix(B - 1, tl, True)
            norm3(B - 1, tl, False)
            choose(B - 1, tl)
            ranks(B - 1, tl, range(TPB))
            slots(B - 1, tl, False)
            dve.wait_ge(count_done, 1)
            tl.link(dve.tensor_reduce(cnt[:, :], bank[4][:, 0:E1], AX.X, ALU.max))
            dve.tensor_scalar(more[:, :], cnt[:, :], float(CAP), None, ALU.is_gt).then_inc(more_ready, 1)
            dve.tensor_reduce(levels[:, :], exp_all[:, :, :].rearrange("p t k -> p k t"), AX.X, ALU.max)\
               .then_inc(levels_ready, 1)
            tl.link(dve.tensor_copy(max_all[:, :], top_all[:, :, 0]))
            plan_slots(tl)
            dve.wait_ge(levels_tr, 1)
            dve.tensor_reduce(level_max[:, :], bank[4][0:K1, P:2 * P], AX.X, ALU.max).then_inc(level_max_ready, 1)
            dve.wait_ge(level_row_done, 1)
            tl.link(dve.tensor_copy(level_row[:, :], bank[4][0:1, 2 * P:2 * P + K1]))
            tl.link(dve.tensor_scalar(stores[:, 1, :], level_row[:, :], 2, None, ALU.add))
            tl.link(dve.tensor_scalar(stores[:, 0, :], level_row[:, :], 2, None, ALU.logical_shift_right),
                    dve.tensor_scalar(stores[:, 1, :], stores[:, 1, :], 2, None, ALU.logical_shift_right))
            dve.tensor_scalar(stores[:, 0, :], stores[:, 0, :], 16.0, 16.0, ALU.mult, ALU.add)\
               .then_inc(stores_ready, 1)
            dve.tensor_scalar(stores[:, 1, :], stores[:, 1, :], 16.0, 16.0, ALU.mult, ALU.max)\
               .then_inc(stores_ready, 1)
            for j in range(TILES):
                for k in range(K1):
                    tl.add(dve.scalar_tensor_tensor(out=junk[:, j % TPB * K1 + k, :], in0=iota64[:, :],
                                                    scalar=exp_all[:, j, k:k + 1], in1=lg_all[:, j, :],
                                                    op0=ALU.is_equal, op1=ALU.mult,
                                                    accum_out=top_all[:, j, k:k + 1]))
                if j % TPB == TPB - 1:
                    tl.wait()
            dve.tensor_tensor(top_all[:, :, :], top_all[:, :, :],
                              max_all[:, :].unsqueeze(2).to_broadcast([P, TILES, K1]),
                              ALU.subtract).then_inc(wexp_in, 1)
            dve.wait_ge(wexp_ready, 1)
            tl.link(dve.tensor_reduce(wsum[:, :], top_all[:, :, :], AX.X, ALU.add))
            tl.link(dve.reciprocal(wsum[:, :], wsum[:, :]))
            tl.link(dve.tensor_tensor(top_all[:, :, :], top_all[:, :, :],
                                      wsum[:, :].unsqueeze(2).to_broadcast([P, TILES, K1]), ALU.mult))
            tl.link(dve.tensor_tensor(w_now[:, :, :], valid[:, :, :], top_all[:, :, :], ALU.mult))

            def rows_out(r, i, u):
                n = u % 2
                dve.wait_ge(xs_tr, r * E1 + i * UN + u + 1)
                dve.tensor_copy(xsT[:, n, :, :].rearrange("p k s -> p (k s)"), bank[6 + n][:, 0:KH * CAP])\
                   .then_inc(xsT_ready, 1)

            def hidden1(r, i, u):
                n = u % 2
                dve.wait_ge(silu1_ready, r * E1 + i * UN + u + 1)
                dve.tensor_tensor(hid1[:, n, :], silu1[:, n, :], bank[n][0:F1, CAP:2 * CAP], ALU.mult)\
                   .then_inc(hid1_ready, 1)

            def experts(r):
                rows_out(r, 0, 0)
                rows_out(r, 0, 1)
                with dve.Fori(0, NI - 1) as i:
                    for u in range(UN):
                        hidden1(r, i, u)
                        rows_out(r, i, u + 2)
                for u in range(UN):
                    hidden1(r, NI - 1, u)
                    if u < UN - 2:
                        rows_out(r, NI - 1, u + 2)

            def combine(r):
                dve.sem_clear(acc_steps)
                steps = Steps(dve, acc_steps)
                for lv in range(K1):
                    last = lv == K1 - 1
                    if not last:
                        dve.wait_ge(gathered[lv], (r + 1) * 16 * TILES)
                    for j in range(TILES):
                        if last:
                            dve.wait_ge(gathered_last[j], (r + 1) * 16)
                        ins = dve.scalar_tensor_tensor(out=x3[:, j, :], in0=gath[lv % len(gath)][:, j, :],
                                                       scalar=w_now[:, j, K1 - 1 - lv:K1 - lv], in1=x3[:, j, :],
                                                       op0=ALU.mult, op1=ALU.add)
                        if last:
                            ins.then_inc(acc_done, 1)
                        elif j == TILES - 1:
                            ins.then_inc(level_added, 1)
                        else:
                            steps.add(ins)
                    if not last:
                        steps.wait()
                        dve.wait_ge(level_added, r * (K1 - 1) + lv + 1)

            experts(0)
            combine(0)
            dve.wait_ge(more_ready, 1)
            again = dve.value_load(more[0:1, 0:1], min_val=0, max_val=1)
            with dve.If(again):
                with dve.Fori(1, MORE) as r:
                    dve.wait_ge(out_done, r * 16 * TILES)
                    dve.memset(cnt[:, :], 0.0)
                    dve.sem_clear(plan_steps)
                    s2 = Steps(dve, plan_steps)
                    s2.link(dve.tensor_scalar(rank_all[:, :, :], rank_all[:, :, :], -float(CAP), None, ALU.add))
                    plan_slots(s2)
                    s2.link(dve.tensor_tensor(w_now[:, :, :], valid[:, :, :], top_all[:, :, :], ALU.mult))
                    s2.link(dve.tensor_scalar(ovf_all[:, :, :], valid[:, :, :], -BIG, BIG, ALU.mult, ALU.add),
                            dve.scalar_tensor_tensor(out=slf_all[:, :, :], in0=exp_all[:, :, :], scalar=float(CAP),
                                                     in1=clamp[:, :, :], op0=ALU.mult, op1=ALU.add))
                    s2.link(dve.tensor_tensor(slf_all[:, :, :], slf_all[:, :, :], ovf_all[:, :, :], ALU.add))
                    with dve.Fori(0, TILES) as j:
                        dve.wait_ge(sent, 16 + 16 * TILES * K1)
                        dve.tensor_scalar(slot[:, 0:1, :], slf_all[:, bass.ds(j, 1), :], 1.0, None, ALU.mult)\
                           .then_inc(staged, 1)
                        dve.tensor_scalar(xn3[:, 0:1, :], xn3_all[:, bass.ds(j, 1), :], 1.0, None, ALU.mult)\
                           .then_inc(staged, 1)
                        dve.wait_ge(sent_more, ((r - 1) * TILES + j + 1) * 16 * K1)
                        dve.memset(cnt[:, :], 0.0)
                    experts(r)
                    combine(r)


_INS = ['x', 'ctx_512', 'L0_xattn_W', 'L0_xattn_b', 'L0_ffn_gate_weight', 'L0_ffn_gate_up_weights',
        'L0_ffn_down_weights', 'L0_ffn_shared_gate_up', 'L0_ffn_shared_down', 'L1_xattn_Wq', 'L1_xattn_Wk',
        'L1_xattn_gamma_raw', 'L1_ffn_gate_weight', 'L1_ffn_w_gate', 'L1_ffn_w_up', 'L1_ffn_w_down']


def kernel(**inputs):
    import numpy as _np
    import concourse.bacc as _bacc
    from concourse import mybir as _mybir
    from concourse.bass_utils import run_bass_kernel_spmd as _run

    nc = _bacc.Bacc("TRN2", target_bir_lowering=False, num_devices=1)
    arrays, args = {}, []
    for name in _INS:
        a = _np.ascontiguousarray(inputs[name])
        if a.ndim < 2:
            a = a.reshape(1, 1)
        arrays[f"in_{name}_dram"] = a
        args.append(nc.dram_tensor(f"in_{name}_dram", a.shape, _mybir.dt.from_np(a.dtype), kind="ExternalInput").ap())
    args.append(nc.dram_tensor("out_0_dram", (B, N, H), F32, kind="ExternalOutput").ap())
    build(nc, *args)
    r = _run(nc, [arrays], core_ids=[0])
    return r.results[0]["out_0_dram"]
```

```python
from contextlib import ExitStack

import concourse.bass as bass
from concourse import mybir

F32 = mybir.dt.float32
F32R = mybir.dt.float32r
I32 = mybir.dt.int32
U32 = mybir.dt.uint32
ALU = mybir.AluOpType
ACT = mybir.ActivationFunctionType
AX = mybir.AxisListType

P = 128
B, N, H = 4, 256, 256
D = 64
TILES = B * N // P
TPB = N // P
KH = H // P
EPS = 1e-5
P_ASEM = 0.6

E0, F0, FS = 8, 176, 352
Q0 = P // E0
RJ = F0 // Q0
SHARED = [P, P, FS - 2 * P]
NCH = len(SHARED) + RJ
NSH = len(SHARED)
GROUPS = NCH + NCH // 2
DVE_GROUPS = [9, 11, 13, 15, 17, 19]
FIRST_GROUPS = 4
HIDS = 5

TOPK = 76
ROUNDS8 = -(-TOPK // 8)
HEADS = 4
SIM_SCALE = 1.0 / ((D // HEADS) ** 0.5 * HEADS)

E1, K1, F1 = 64, 8, 96
CAP = 192
SH = CAP // 2
MORE = -(-(B * N) // CAP)
BIG = float(1 << 20)
RING = 4
UN = 2 * RING
NI = E1 // UN
SENT_LEVEL = 16 * TPB
LOWEST = -3.0e38
SEND = 11
EARLY = 4
MAXIMA0 = [1, 1, 1, 1, 2, 1, 1, 1, 1, 1, 1, 1, 1, 2]
FINISH = 5
MAXIMA = [0, 0, 0, 1, 0, 1, 2, 1, 1, 0, 0, 1, 2, 1]
assert EARLY + sum(MAXIMA0) == 2 * ROUNDS8 and EARLY + sum(MAXIMA0[:FINISH]) == ROUNDS8 == sum(MAXIMA)


class Steps:

    def __init__(self, eng, sem, base=0):
        self.eng, self.sem, self.base, self.n = eng, sem, base, 0

    def add(self, ins):
        ins.then_inc(self.sem, 1)
        self.n += 1

    def wait(self):
        self.eng.wait_ge(self.sem, self.base + self.n)

    def link(self, *ins):
        for i in ins:
            self.add(i)
        self.wait()


def build(nc, x, ctx512, W, b0, g0w, gu0w, dn0w, sgu0w, sdn0w, Wq, Wk, gamma, g1w, wg1, wu1, wd1, out):
    es = ExitStack()
    with es:
        def sb(name, shape, dt=F32, scope=es):
            return scope.enter_context(nc.sbuf_tensor(name, shape, dt))

        def sem(name):
            return es.enter_context(nc.semaphore(name))

        xs_dram = nc.dram_tensor("slots_in", [E1 * CAP, H], F32, kind="Internal").ap()
        fill = xs_dram.rearrange("(a p q) h -> a p (q h)", p=P, q=8)
        FILLS = E1 * CAP // (P * 8) - 1
        ys_dram = nc.dram_tensor("slots_out", [E1 * CAP, H], F32, kind="Internal").ap()
        fill_out = ys_dram.rearrange("(a p q) h -> a p (q h)", p=P, q=8)

        ident = sb("ident", [P, P])
        ones = sb("ones", [P, N])
        before = sb("before", [P, P])
        iota64 = sb("iota64", [P, E1])
        x1 = sb("x1", [P, TILES, H])
        w_ij = sb("w_ij", [D, 2])
        wj_b = sb("wj_b", [D, P])
        b_sb = sb("b_sb", [P, 2])
        si = sb("si", [P, TILES])
        wqkT = sb("wqkT", [D, 2, D])
        gate0T = sb("gate0T", [P, KH, E0])
        gate1T = sb("gate1T", [P, KH, E1])
        gam = sb("gam", [P, 5])
        raw_gu = sb("raw_gu", [P, 2, RJ, H])
        raw_sgu = sb("raw_sgu", [P, 2, NSH, H])
        raw_dn = sb("raw_dn", [P, KH, E0, F0])
        w_gu = sb("w_gu", [P, NCH, KH, 2, P])
        w_dn = sb("w_dn", [P, NCH, H])
        st = sb("st", [P, TILES, 6])
        mv = sb("mv", [P, TILES, 2])
        rs = sb("rs", [P, TILES])
        sc = sb("sc", [P, TILES])
        of = sb("of", [P, TILES])
        xn = sb("xn", [P, TILES, H])
        xnT = sb("xnT", [P, KH, B * N])
        lg0 = sb("lg0", [P, TILES, E0])
        top0 = sb("top0", [P, TILES, 8])
        idx0 = sb("idx0", [P, TILES, 8], U32)
        idx0f = sb("idx0f", [P, TILES, 8])
        pr0 = sb("pr0", [P, TILES, E0])
        sum0 = sb("sum0", [P, TILES])
        eq0 = sb("eq0", [P, TILES, E0])
        eq1 = sb("eq1", [P, TILES, E0])
        comb_x = sb("comb_x", [P, TILES, E0, Q0])
        combT = sb("combT", [P, B * N])
        comb_b = sb("comb_b", [P, N])
        sim = sb("sim", [P, TILES, N])
        sim_t = sb("sim_t", [P, TILES, N])
        simw = sb("simw", [P, TPB, N])
        v8 = sb("v8", [P, TPB, 8])
        least = sb("least", [P, TPB])
        A = sb("A", [P, TPB, N])
        S = sb("S", [P, TPB, N])
        silu = sb("silu", [P, 3, N])
        silu_c = sb("silu_c", [P, 3, N])
        hid = sb("hid", [P, HIDS, N])
        x2 = sb("x2", [P, TPB, H])
        st2 = sb("st2", [P, TPB, 6])
        mv2 = sb("mv2", [P, TPB, 2])
        sm = sb("sm", [P, 4, TPB])
        x3 = sb("x3", [P, TILES, H])
        adj = x3
        xn3 = sb("xn3", [P, TPB, H])
        rows = sb("rows", [P, TPB, H])
        xn3_all = sb("xn3_all", [P, TILES, H])
        xn3T = sb("xn3T", [P, KH, N])
        lg1 = sb("lg1", [P, TPB, E1])
        lgr = sb("lgr", [P, TPB, E1])
        t8 = sb("t8", [P, TPB, K1])
        i8f = sb("i8f", [P, TPB, K1])
        chosen = sb("chosen", [P, TPB, E1])
        chosen_sum = sb("chosen_sum", [P, E1])
        junk = comb_x[:, :, :, :].rearrange("p t e q -> p (t e q)").rearrange("p (n e) -> p n e", e=E1)
        rk = sb("rk", [P, TPB, K1])
        ovf = sb("ovf", [P, TPB, K1])
        slf = sb("slf", [P, TPB, K1])
        slot = sb("slot", [P, TPB, K1], I32)

        zeros = xn3_all[:, :, :].rearrange("p t h -> p (t h)")
        flat_raw = raw_gu[:, :, :, :].rearrange("p g j h -> p (g j h)")
        W1, WD = RING * 4 * KH * F1, RING * 2 * H
        w1_sb = flat_raw[:, 0:W1].rearrange("p (a n g f) -> p a n g f", a=RING, n=2, g=2)

        def w1_pair(a):
            return flat_raw[:, a * W1 // RING:(a + 1) * W1 // RING]

        wd_sb = flat_raw[0:F1, W1:W1 + WD].rearrange("p (a n h) -> p a n h", a=RING, n=2)
        flat_gu = w_gu[:, :, :, :, :].rearrange("p c k g f -> p (c k g f)")
        xs_sb = flat_gu[0:SH, 0:RING * 4 * H].rearrange("p (a n s h) -> p a n s h", a=RING, n=2, s=2)
        ys_sb = flat_gu[0:SH, RING * 4 * H:(RING + 2) * 4 * H].rearrange("p (a n s h) -> p a n s h", a=2, n=2, s=2)
        flat_dn = w_dn[:, :, :].rearrange("p c h -> p (c h)")
        silu1 = flat_dn[0:F1, 4 * CAP:6 * CAP].rearrange("p (n s) -> p n s", n=2)
        hid1 = flat_dn[0:F1, 6 * CAP:8 * CAP].rearrange("p (n s) -> p n s", n=2)
        rank_all = sb("rank_all", [P, TILES, K1])
        exp_all = sb("exp_all", [P, TILES, K1])
        top_all = sb("top_all", [P, TILES, K1])
        exp_j = sb("exp_j", [P, 1, K1])
        lg_j = sb("lg_j", [P, 1, E1])
        top_j = sb("top_j", [P, 1, K1])
        wsum = sb("wsum", [P, TILES])
        valid = sb("valid", [P, TILES, K1])
        clamp = sb("clamp", [P, TILES, K1])
        w_now = sb("w_now", [P, TILES, K1])
        lg_all = raw_sgu[:, 0, :, :].rearrange("p c h -> p (c h)")[:, 0:TILES * E1].rearrange("p (t e) -> p t e", e=E1)
        max_all = sb("max_all", [P, TILES])
        levels = sb("levels", [P, 2 * K1])
        level_max = sb("level_max", [2 * K1, 1])
        level_hits = sb("level_hits", [1, RING, K1])
        level_count = sb("level_count", [1, RING])
        sends = sb("sends", [1, 2, RING], I32)
        level_row = sb("level_row", [1, K1], I32)
        stores = sb("stores", [1, 2, K1], I32)
        slf_all = sb("slf_all", [P, TILES, K1])
        ovf_all = sb("ovf_all", [P, TILES, K1])
        gidx = sb("gidx", [P, TILES, K1], I32)
        gath = [x1, xn, xnT[:, :, :].rearrange("p k (a h) -> p (k a) h", h=H), sim, sim_t,
                raw_dn[:, :, :, :].rearrange("p k e f -> p (k e f)")[:, 0:TILES * H]
                .rearrange("p (t h) -> p t h", t=TILES)]
        LATE = len(gath)
        gath += [flat_raw[:, i * TILES * H:(i + 1) * TILES * H].rearrange("p (t h) -> p t h", t=TILES)
                 for i in range(K1 - LATE)]
        cnt = sb("cnt", [P, 1])
        idle = sb("idle", [P, 1])
        more = sb("more", [P, 1], I32)

        with ExitStack() as setup:
            ctx_sb = sb("ctx_sb", [P, TILES, D], F32, setup)
            ctxT = sb("ctxT", [D, B * N], F32, setup)
            qT = sb("qT", [D, B * N], F32, setup)
            kT = sb("kT", [D, B * N], F32, setup)
            raw_sdn = sb("raw_sdn", [P, KH, FS], F32, setup)
            gate0 = sb("gate0", [E0, H], F32, setup)
            gate1 = sb("gate1", [E1, H], F32, setup)
            wqk = sb("wqk", [D, 2, D], F32, setup)
        w1_hi = sb("w1_hi", [P, 2, 4 * KH * F1], F32R)
        w1_lo = sb("w1_lo", [P, 2, 4 * KH * F1], F32R)
        xsT_hi = sb("xsT_hi", [P, 2, KH, CAP], F32R)
        xsT_lo = sb("xsT_lo", [P, 2, KH, CAP], F32R)

        bank = [es.enter_context(nc.psum_tensor(f"bank{i}", [P, 512], F32)) for i in range(8)]

        level_bank = bank[0]
        gu_bank = [bank[0], bank[1], bank[7]]

        consts = sem("consts")
        ld_ctx = sem("ld_ctx")
        ld_x = [sem(f"ld_x{i}") for i in range(B)]
        ld_small = sem("ld_small")
        ld_gates = sem("ld_gates")
        qkw_tr = sem("qkw_tr")
        qkwT_ready = sem("qkwT_ready")
        si_done = sem("si_done")
        si_ready = sem("si_ready")
        ld_sgu = sem("ld_sgu")
        ld_gu = sem("ld_gu")
        ld_dn = sem("ld_dn")
        dve_steps = sem("dve_steps")
        pool_steps = sem("pool_steps")
        wij_ready = sem("wij_ready")
        ctx_tr = sem("ctx_tr")
        ctxT_ready = sem("ctxT_ready")
        small_tr = sem("small_tr")
        smallT_ready = sem("smallT_ready")
        z_ready = sem("z_ready")
        adj_ready = sem("adj_ready")
        qk_done = sem("qk_done")
        qkT_ready = sem("qkT_ready")
        sim_done = sem("sim_done")
        sim_ready = sem("sim_ready")
        xn_ready = sem("xn_ready")
        xn_tr = sem("xn_tr")
        xnT_ready = sem("xnT_ready")
        lg0_done = sem("lg0_done")
        pr0_in = sem("pr0_in")
        pr0_ready = sem("pr0_ready")
        combx_ready = sem("combx_ready")
        comb_tr = sem("comb_tr")
        combT_ready = sem("combT_ready")
        wt_done = sem("wt_done")
        wt_taken = [sem("wt_taken_act"), sem("wt_taken_dve")]
        half_taken = sem("half_taken")
        gam_t = sem("gam_t")
        gu_done = sem("gu_done")
        silu_ready = sem("silu_ready")
        scaled_ready = sem("scaled_ready")
        hid_ready = sem("hid_ready")
        y_done = sem("y_done")
        y_read = sem("y_read")
        combb_ready = sem("combb_ready")
        topk_steps = sem("topk_steps")
        A_ready = sem("A_ready")
        AT_done = sem("AT_done")
        tail_steps = sem("tail_steps")
        xn3_ready = sem("xn3_ready")
        xn3_tr = sem("xn3_tr")
        xn3T_ready = sem("xn3T_ready")
        xn3_kept = sem("xn3_kept")
        rows_ready = sem("rows_ready")
        lg1_done = sem("lg1_done")
        chosen_ready = sem("chosen_ready")
        rank_done = sem("rank_done")
        slot_ready = sem("slot_ready")
        sent = sem("sent")
        sent_last = [sem(f"sent_last_{i}") for i in range(2)]
        sends_ready = sem("sends_ready")
        out_done = sem("out_done")
        zeros_ready = sem("zeros_ready")
        zero_fill = sem("zero_fill")
        zero_fill_out = sem("zero_fill_out")
        ld_w1 = [sem(f"ld_w1_{i}") for i in range(RING)]
        ld_xs = [sem(f"ld_xs_{i}") for i in range(RING)]
        st_ys = [sem(f"st_ys_{i}") for i in range(2)]
        xs_tr = sem("xs_tr")
        xsT_high = sem("xsT_high")
        xsT_ready = sem("xsT_ready")
        w1_high = sem("w1_high")
        w1_ready = sem("w1_ready")
        gu1_done = sem("gu1_done")
        silu1_ready = sem("silu1_ready")
        hid1_ready = sem("hid1_ready")
        y1_done = sem("y1_done")
        ys_ready = sem("ys_ready")
        wexp_in = sem("wexp_in")
        wexp_ready = sem("wexp_ready")
        count_done = sem("count_done")
        chosen_counted = sem("chosen_counted")
        more_ready = sem("more_ready")
        plan_steps = sem("plan_steps")
        acc_steps = sem("acc_steps")
        pick_steps = sem("pick_steps")
        gidx_ready = sem("gidx_ready")
        levels_ready = sem("levels_ready")
        levels_tr = sem("levels_tr")
        level_max_ready = sem("level_max_ready")
        level_row_done = sem("level_row_done")
        stores_ready = sem("stores_ready")
        gathered = [sem(f"gathered_{i}") for i in range(K1 - 1)]
        gathered_last = [sem(f"gathered_last_{i}") for i in range(TILES)]
        acc_done = sem("acc_done")
        staged = sem("staged")
        idled = sem("idled")
        sent_more = sem("sent_more")

        block = es.enter_context(nc.Block())

        def taken(g):
            by_dve = g in DVE_GROUPS
            return wt_taken[by_dve], sum((v in DVE_GROUPS) == by_dve for v in range(g + 1))

        def keep_weights(eng, copy, g):
            eng.wait_ge(wt_done, g + 1)
            o = bank[g % 4]
            c = 2 * (g - NCH)
            if g < NCH:
                m = SHARED[g] if g < NSH else P
                i = copy(w_gu[:, g, :, :, 0:m].rearrange("p k g f -> p (k g) f"),
                         o[:, :].rearrange("p (n f) -> p n f", n=4)[:, :, 0:m])
            elif c + 1 == NSH:
                m = SHARED[c]
                copy(w_dn[0:m, c, :], o[0:m, 0:H]).then_inc(half_taken, 1)
                eng.wait_ge(half_taken, 1)
                i = copy(w_dn[:, c + 1, :], o[:, H:2 * H])
            else:
                i = copy(w_dn[:, c:c + 2, :].rearrange("p c h -> p (c h)"), o[:, :])
            i.then_inc(taken(g)[0], 1)

        def plain(eng):
            eng.wait_ge(zeros_ready, 2)

        def tiles_of(b):
            return bass.ds(b * TPB, TPB)

        @block.sync
        def _(sp):
            def dma(dst, src, s):
                return sp.dma_start(dst, src).then_inc(s, 16)

            dma(ctx_sb[:, :, :], ctx512.rearrange("b (t p) d -> p (b t) d", p=P), ld_ctx)
            for b in range(B):
                dma(x1[:, b * TPB:(b + 1) * TPB, :], x[b].rearrange("(t p) h -> p t h", p=P), ld_x[b])
            dma(gate0[:, :], g0w, ld_gates)
            dma(gate1[:, :], g1w, ld_gates)
            dma(gam[:, 0:1], gamma.to_broadcast([P, 1]), ld_gates)
            for g in range(2):
                dma(raw_sgu[:, g, 0:2, :], sgu0w[g * FS:g * FS + 2 * P, :].rearrange("(c p) h -> p c h", p=P), ld_sgu)
                dma(raw_sgu[0:SHARED[2], g, 2, :], sgu0w[g * FS + 2 * P:(g + 1) * FS, :], ld_sgu)
            for g in range(2):
                for e in range(E0):
                    dma(raw_gu[Q0 * e:Q0 * (e + 1), g, :, :].rearrange("q j h -> q (j h)"),
                        gu0w[e, g * F0:(g + 1) * F0, :].rearrange("(q j) h -> q (j h)", q=Q0), ld_gu)
            dma(raw_sdn[:, :, :], sdn0w.rearrange("(k p) f -> p k f", p=P), ld_dn)
            for k in range(KH):
                dma(raw_dn[:, k, :, :], dn0w[:, k * P:(k + 1) * P, :].rearrange("e p f -> p e f"), ld_dn)
            sp.wait_ge(zeros_ready, 2)
            for a in range(1, fill.shape[0]):
                dma(fill[a], zeros, zero_fill)
            for a in range(fill_out.shape[0]):
                dma(fill_out[a], zeros, zero_fill_out)

            w_dram = [v.rearrange("(p n) (q k) f -> p q n (k f)", n=2, k=KH) for v in (wg1, wu1)]
            wd_dram = wd1.rearrange("(p n) f h -> p f n h", n=2)
            xs_pair = xs_dram.rearrange("(p n q s) h -> p q n (s h)", n=2, q=SH, s=2)
            ys_pair = ys_dram.rearrange("(p n q s) h -> p q n (s h)", n=2, q=SH, s=2)
            out_tile = out.rearrange("b (t p) h -> (b t) p h", p=P)

            def one(v, p):
                return v[bass.ds(p, 1)].rearrange("a q n f -> (a q) n f")

            def load_weights(p, a):
                for g in range(2):
                    dma(w1_sb[:, a, :, g, :], one(w_dram[g], p), ld_w1[a])
                dma(wd_sb[:, a, :, :], one(wd_dram, p), ld_w1[a])

            def load_rows(p, a):
                dma(xs_sb[:, a, :, :, :].rearrange("p n s h -> p n (s h)"), one(xs_pair, p), ld_xs[a])

            def store_rows(r, p, a):
                sp.wait_ge(ys_ready, r * E1 + 2 * p + 2)
                plain(sp)
                dma(one(ys_pair, p), ys_sb[:, a % 2, :, :, :].rearrange("p n s h -> p n (s h)"), st_ys[a % 2])

            def experts(r):
                if not isinstance(r, int):
                    for a in range(RING):
                        load_rows(a, a)
                with sp.Fori(0, NI - 1) as i:
                    for a in range(RING):
                        sp.wait_ge(y1_done, r * E1 + UN * i + 2 * a + 2)
                        plain(sp)
                        load_rows(RING * (i + 1) + a, a)
                        load_weights(RING * (i + 1) + a, a)
                        store_rows(r, RING * i + a, a)
                for a in range(RING):
                    store_rows(r, E1 // 2 - RING + a, a)

            def results(r):
                with sp.Fori(0, TILES) as j:
                    sp.wait_ge(acc_done, r * TILES + j + 1)
                    plain(sp)
                    dma(out_tile[bass.ds(j, 1)].rearrange("a p h -> (a p) h"),
                        x3[:, bass.ds(j, 1), :].rearrange("p a h -> p (a h)"), out_done)

            sp.wait_ge(combT_ready, 2)
            sp.wait_ge(*taken(GROUPS - 1))
            sp.wait_ge(*taken(GROUPS - 2))
            for a in range(RING):
                load_weights(a, a)
            sp.wait_ge(zero_fill_out, 16 * fill_out.shape[0])
            sp.wait_ge(sent, 16 + 16 * (TILES - TPB) * K1)
            sp.wait_ge(sends_ready, 2)
            for a in range(RING):
                need = [sp.value_load(sends[0:1, n, a:a + 1], min_val=SENT_LEVEL, max_val=SENT_LEVEL * K1 // 2)
                        for n in range(2)]
                for n in range(2):
                    sp.wait_ge(sent_last[n], need[n])
                load_rows(a, a)
            for n in range(2):
                sp.wait_ge(sent_last[n], SENT_LEVEL * K1 // 2)
            experts(0)
            results(0)
            sp.wait_ge(out_done, 16 * TILES)
            sp.wait_ge(more_ready, 1)
            again = sp.value_load(more[0:1, 0:1], min_val=0, max_val=1)
            with sp.If(again):
                with sp.Fori(1, MORE) as r:
                    sp.wait_ge(y1_done, r * E1)
                    plain(sp)
                    for a in range(RING):
                        load_weights(a, a)
                    sp.wait_ge(sent_more, r * 16 * TILES * K1)
                    plain(sp)
                    experts(r)
                    results(r)
                sp.wait_ge(out_done, MORE * 16 * TILES)

        @block.gpsimd
        def _(pool):
            pool.memset(idle[:, :], 0.0).then_inc(xn3_kept, 1)
            pool.memset(ident[:, :], 0.0).then_inc(pool_steps, 1)
            pool.memset(before[:, :], 1.0).then_inc(pool_steps, 1)
            pool.memset(ones[:, :], 1.0).then_inc(consts, 1)
            pool.memset(chosen_sum[:, :], 0.0).then_inc(consts, 1)
            pool.wait_ge(pool_steps, 2)
            pool.affine_select(out=ident[:, :], in_=ident[:, :], compare_op=ALU.not_equal, fill=1.0, base=0,
                               pattern=[[-1, P]], channel_multiplier=1).then_inc(consts, 1)
            pool.affine_select(out=before[:, :], in_=before[:, :], compare_op=ALU.is_gt, fill=0.0, base=0,
                               pattern=[[1, P]], channel_multiplier=-1).then_inc(consts, 1)
            pool.iota(iota64[:, :], pattern=[[1, E1]], base=0, channel_multiplier=0,
                      allow_small_or_imprecise_dtypes=True).then_inc(consts, 1)

            pool.wait_ge(xn3_kept, 1)
            for h in range(2):
                pool.memset(zeros[:, h * 1024:(h + 1) * 1024], 0.0).then_inc(zeros_ready, 1)

            pool.wait_ge(zeros_ready, 2)
            pool.wait_ge(ld_gu, 16 * 2 * E0)
            pool.dma_start(fill[0], zeros).then_inc(sent, 16)

            def body(b, tail):
                def scaled(c):
                    pool.wait_ge(silu_ready, b * NCH + c + 1)
                    pool.tensor_tensor(silu_c[:, c % 3, :], silu[:, c % 3, :], comb_b[:, :],
                                       ALU.mult).then_inc(scaled_ready, 1)

                pool.wait_ge(combb_ready, b + 1)
                for c in range(NSH, NCH):
                    if tail and c == SEND:
                        pool.wait_ge(rows_ready, b)
                        pool.wait_ge(slot_ready, b)
                    scaled(c)
                    if tail and c >= SEND:
                        send(b - 1, 2 * (c - SEND), 2 * (c - SEND + 1))
                if tail:
                    send(b - 1, 2 * (NCH - SEND), TPB * K1)

            def scatter(t, k, signal):
                pool.indirect_dma_start(xs_dram, bass.IndirectOffsetOnAxis(ap=slot[:, t, k:k + 1], axis=0),
                                        rows[:, t, :], None, bounds_check=E1 * CAP - 1,
                                        oob_is_err=False).then_inc(signal, 16)

            def send(q, n0, n1):
                for n in range(n0, n1):
                    scatter(n // K1, n % K1, sent)

            body(0, False)
            pool.wait_ge(zero_fill, 16 * FILLS)
            pool.wait_ge(sent, 16)
            with pool.Fori(1, B) as b:
                body(b, True)
            pool.wait_ge(rows_ready, B)
            pool.wait_ge(slot_ready, B)
            for lv in range(K1):
                if lv == 2:
                    pool.wait_ge(slot_ready, B + 1)
                if lv >= 2:
                    pool.wait_ge(sent_last[lv % 2], lv // 2 * SENT_LEVEL)
                for t in range(TPB):
                    scatter(t, K1 - 1 - lv, sent_last[lv % 2])

            def idle_step():
                pool.tensor_tensor(idle[:, :], idle[:, :], idle[:, :], ALU.add).then_inc(idled, 1)
                pool.wait_ge(idled, 1)

            def gather_level(r, lv):
                if lv == LATE:
                    pool.sem_clear(idled)
                    pool.wait_ge(y1_done, (r + 1) * E1)
                    idle_step()
                for j in range(TILES):
                    pool.indirect_dma_start(gath[lv][:, j, :], None, ys_dram,
                                            bass.IndirectOffsetOnAxis(ap=gidx[:, j, K1 - 1 - lv:K1 - lv], axis=0))\
                        .then_inc(gathered[lv] if lv < K1 - 1 else gathered_last[j], 16)

            def gather_early():
                pool.wait_ge(gidx_ready, 1)
                pool.wait_ge(stores_ready, 2)
                need = [[pool.value_load(stores[0:1, a, k:k + 1], min_val=16, max_val=16 * (E1 // 4))
                         for a in range(2)] for k in range(K1)]
                for lv in range(K1):
                    for a in range(2):
                        if lv < K1 - 1:
                            pool.sem_clear(idled)
                            pool.wait_ge(st_ys[a], need[K1 - 1 - lv][a])
                            idle_step()
                        else:
                            pool.wait_ge(st_ys[a], 16 * (E1 // 4))
                    gather_level(0, lv)

            def gather(r):
                for a in range(2):
                    pool.sem_clear(idled)
                    pool.wait_ge(st_ys[a], (r + 1) * 16 * (E1 // 4))
                    idle_step()
                pool.sem_clear(idled)
                pool.wait_ge(gidx_ready, r + 1)
                idle_step()
                for lv in range(K1):
                    gather_level(r, lv)

            gather_early()
            pool.wait_ge(more_ready, 1)
            again = pool.value_load(more[0:1, 0:1], min_val=0, max_val=1)
            with pool.If(again):
                with pool.Fori(1, MORE) as r:
                    with pool.Fori(0, TILES) as j:
                        pool.sem_clear(idled)
                        pool.wait_ge(staged, 2 * ((r - 1) * TILES + j + 1))
                        idle_step()
                        for k in range(K1):
                            pool.indirect_dma_start(xs_dram, bass.IndirectOffsetOnAxis(ap=slot[:, 0, k:k + 1], axis=0),
                                                    xn3[:, 0, :], None, bounds_check=E1 * CAP - 1,
                                                    oob_is_err=False).then_inc(sent_more, 16)
                    gather(r)

        @block.tensor
        def _(pe):
            pe.wait_ge(consts, 5)
            pe.wait_ge(ld_ctx, 16)
            for j in range(TILES):
                i = pe.transpose(bank[4 + j // 4][0:D, (j % 4) * P:(j % 4 + 1) * P], ctx_sb[:, j, :], ident[:, :])
                if j % 4 == 3:
                    i.then_inc(ctx_tr, 1)
            pe.wait_ge(ld_small, 16 * 4)
            for n in range(2):
                i = pe.transpose(bank[6][0:D, n * D:(n + 1) * D], wqk[:, n, :], ident[0:D, 0:D])
            i.then_inc(qkw_tr, 1)
            pe.wait_ge(ctxT_ready, 2)
            for j in range(TILES):
                i = pe.matmul(bank[7][:, j:j + 1], ctxT[:, j * P:(j + 1) * P], w_ij[:, 0:1], start=True, stop=True)
            i.then_inc(si_done, 1)
            pe.wait_ge(wij_ready, 2)
            for h in range(2):
                pe.matmul(bank[4 + h][:, :], wj_b[:, :], ctxT[:, h * 512:(h + 1) * 512], start=True, stop=True)\
                    .then_inc(z_ready, 1)
            pe.wait_ge(qkwT_ready, 1)
            pe.wait_ge(si_ready, 1)
            for n in (1, 0):
                for h in range(2):
                    if n == 0:
                        pe.wait_ge(adj_ready, 4 * h + 4)
                    pe.matmul(bank[4 + 2 * n + h][0:D, :], wqkT[:, n, :], ctxT[:, h * 512:(h + 1) * 512],
                              start=True, stop=True).then_inc(qk_done, 1)
            pe.wait_ge(ld_gates, 16 * 3)
            for k in range(KH):
                pe.transpose(bank[0][:, k * E0:(k + 1) * E0], gate0[:, k * P:(k + 1) * P], ident[0:E0, 0:E0])
            for k in range(KH):
                i = pe.transpose(bank[0][:, 256 + k * E1:256 + (k + 1) * E1], gate1[:, k * P:(k + 1) * P],
                                 ident[0:E1, 0:E1])
            i.then_inc(small_tr, 1)
            def transpose_weights(g):
                if g == 0:
                    pe.wait_ge(smallT_ready, 2)
                if g >= 4:
                    pe.wait_ge(*taken(g - 4))
                o = bank[g % 4]
                if g < NCH:
                    c = g
                    if c == 0:
                        pe.wait_ge(ld_sgu, 64)
                    if c == NSH:
                        pe.wait_ge(ld_gu, 16 * 2 * E0)
                    m = SHARED[c] if c < NSH else P
                    for k in range(KH):
                        for gu in range(2):
                            src = raw_sgu[0:m, gu, c, k * P:(k + 1) * P] if c < NSH else \
                                raw_gu[:, gu, c - NSH, k * P:(k + 1) * P]
                            i = pe.transpose(o[:, (k * 2 + gu) * P:(k * 2 + gu) * P + m], src, ident[0:m, 0:m])
                else:
                    if g == NCH:
                        pe.wait_ge(ld_dn, 48)
                    for n in range(2):
                        c = 2 * (g - NCH) + n
                        for k in range(KH):
                            if c < NSH:
                                m = SHARED[c]
                                src = raw_sdn[:, k, c * P:c * P + m]
                            else:
                                m = P
                                src = raw_dn[:, k, :, :].rearrange("p e (q j) -> p j (e q)", j=RJ)[:, c - NSH, :]
                            i = pe.transpose(o[0:m, (n * KH + k) * P:(n * KH + k + 1) * P], src, ident[:, :])
                i.then_inc(wt_done, 1)

            for g in range(FIRST_GROUPS):
                transpose_weights(g)
            pe.wait_ge(qkT_ready, 4)
            for b in range(B):
                for t in range(TPB):
                    j = b * TPB + t
                    i = pe.matmul(bank[4 + b][:, t * N:(t + 1) * N], qT[:, j * P:(j + 1) * P],
                                  kT[:, b * N:(b + 1) * N], start=True, stop=True)
                i.then_inc(sim_done, 1)

            for g in range(FIRST_GROUPS, 8):
                transpose_weights(g)
            for b in range(B):
                pe.wait_ge(xn_ready, TPB * (b + 1))
                pe.wait_ge(sim_ready, 2 * (b + 1))
                for k in range(KH):
                    for t in range(TPB):
                        i = pe.transpose(bank[4 + b][:, k * N + t * P:k * N + (t + 1) * P],
                                         xn[:, b * TPB + t, k * P:(k + 1) * P], ident[:, :])
                i.then_inc(xn_tr, 1)
                for g in range(8 + 2 * b, 10 + 2 * b):
                    transpose_weights(g)
            pe.wait_ge(xnT_ready, B)
            for j in range(TILES):
                for k in range(KH):
                    i = pe.matmul(bank[4][:, j * E0:(j + 1) * E0], xnT[:, k, j * P:(j + 1) * P], gate0T[:, k, :],
                                  start=(k == 0), stop=(k == KH - 1))
            i.then_inc(lg0_done, 1)
            for g in range(8 + 2 * B, GROUPS):
                transpose_weights(g)
            def gate_up(b, c, first):
                m = SHARED[c] if c < NSH else P
                if not (first and c < 3):
                    pe.wait_ge(hid_ready, b * NCH + (c - 1 if c < 2 else c - 2))
                for gu in range(2):
                    for k in range(KH):
                        i = pe.matmul(gu_bank[c % 3][0:m, gu * N:(gu + 1) * N], w_gu[:, c, k, gu, 0:m],
                                      xnT[:, k, bass.ds(b * N, N)], start=(k == 0), stop=(k == KH - 1))
                i.then_inc(gu_done, 1)

            def down(b, c, first):
                m = SHARED[c] if c < NSH else P
                pe.wait_ge(hid_ready, b * NCH + c + 1)
                if c == 0 and not first:
                    pe.wait_ge(y_read, b)
                for t in range(TPB):
                    i = pe.matmul(bank[2 + t][:, 0:H], hid[0:m, c % HIDS, t * P:(t + 1) * P], w_dn[0:m, c, :],
                                  start=(c == 0), stop=(c == NCH - 1))
                if c == NCH - 1:
                    i.then_inc(y_done, 1)

            def tail_transposes(q):
                pe.wait_ge(xn3_ready, q + 1)
                for k in range(KH):
                    for t in range(TPB):
                        i = pe.transpose(bank[4][:, k * N + t * P:k * N + (t + 1) * P],
                                         xn3[:, t, k * P:(k + 1) * P], ident[:, :])
                i.then_inc(xn3_tr, 1)

            def tail_logits(q):
                pe.wait_ge(xn3T_ready, q + 1)
                for t in range(TPB):
                    for k in range(KH):
                        i = pe.matmul(bank[5][:, t * E1:(t + 1) * E1], xn3T[:, k, t * P:(t + 1) * P],
                                      gate1T[:, k, :], start=(k == 0), stop=(k == KH - 1))
                i.then_inc(lg1_done, 1)

            def tail_ranks(q):
                pe.wait_ge(chosen_ready, q + 1)
                for t in range(TPB):
                    o = bank[5][:, (2 + t) * E1:(3 + t) * E1]
                    pe.matmul(o, before[:, :], chosen[:, t, :], start=True, stop=False)
                    if t == 1:
                        pe.matmul(o, ones[:, 0:P], chosen[:, 0, :], start=False, stop=False)
                    i = pe.matmul(o, ones[:, 0:P], chosen_sum[:, :], start=False, stop=True)
                i.then_inc(rank_done, 1)

            def turn_A(b):
                pe.wait_ge(A_ready, b + 1)
                for r in range(TPB):
                    for c in range(TPB):
                        i = pe.transpose(bank[6][:, c * N + r * P:c * N + (r + 1) * P],
                                         A[:, r, c * P:(c + 1) * P], ident[:, :])
                i.then_inc(AT_done, 1)

            def body(b, first, last=False):
                for c in range(2, NCH + 2):
                    if c < NCH:
                        gate_up(b, c, first)
                    elif not last:
                        gate_up(b + 1, c - NCH, False)
                    down(b, c - 2, first)
                    if last and c == NCH - 1:
                        turn_A(b)
                    if not first:
                        if c == 2:
                            turn_A(b - 1)
                        if c == 7:
                            tail_transposes(b - 1)
                        if c == 8:
                            tail_logits(b - 1)
                        if c == 10:
                            tail_ranks(b - 1)

            pe.wait_ge(*taken(GROUPS - 1))
            pe.wait_ge(*taken(GROUPS - 2))
            gate_up(0, 0, True)
            gate_up(0, 1, True)
            pe.wait_ge(combx_ready, 1)
            for j in range(TILES):
                i = pe.transpose(bank[5 + j // 4][:, (j % 4) * P:(j % 4 + 1) * P],
                                 comb_x[:, j, :, :].rearrange("p e q -> p (e q)"), ident[:, :])
                if j % 4 == 3:
                    i.then_inc(comb_tr, 1)
            body(0, True)
            with pe.Fori(1, B - 1) as b:
                body(b, False)
            body(B - 1, False, True)
            tail_transposes(B - 1)
            tail_logits(B - 1)
            tail_ranks(B - 1)
            pe.wait_ge(levels_ready, 1)
            pe.transpose(level_bank[0:2 * K1, P:2 * P], levels[:, :], ident[:, :]).then_inc(levels_tr, 1)
            pe.wait_ge(level_max_ready, 1)
            pe.matmul(level_bank[0:1, 2 * P:2 * P + 2 * K1], level_max[:, :], ident[0:2 * K1, 0:2 * K1],
                      start=True, stop=True)\
                .then_inc(level_row_done, 1)
            pe.wait_ge(chosen_counted, 1)
            pe.matmul(bank[4][:, 0:E1], ones[:, 0:P], chosen_sum[:, :], start=True, stop=True)\
                .then_inc(count_done, 1)

            def turn_rows(r, i, u):
                a, n = u // 2 % RING, u % 2
                if n == 0:
                    pe.wait_ge(ld_xs[a], (r * NI + i + u // UN + 1) * 16)
                if not (isinstance(r, int) and isinstance(i, int) and r == 0 and i == 0 and u < 2):
                    pe.wait_ge(xsT_ready, r * E1 + i * UN + u - 1)
                for k in range(KH):
                    for h in range(2):
                        ins = pe.transpose(bank[6 + n][:, k * CAP + h * SH:k * CAP + (h + 1) * SH],
                                           xs_sb[:, a, n, h, :].rearrange("p (q k) -> p k q", k=KH)[:, k, :],
                                           ident[0:SH, 0:SH])
                ins.then_inc(xs_tr, 1)

            def gate_up1(r, i, u, warm):
                a, n = u // 2, u % 2
                if n == 0:
                    pe.wait_ge(w1_ready, r * (E1 // 2) + i * RING + a + 1)
                if warm:
                    pe.wait_ge(hid1_ready, r * E1 + i * UN + u - 1)
                pe.wait_ge(xsT_ready, r * E1 + i * UN + u + 1)
                for g in range(2):
                    o = bank[n][0:F1, g * CAP:(g + 1) * CAP]
                    for k in range(KH):
                        c = ((n * 2 + g) * KH + k) * F1
                        high, low = [w[:, a % 2, c:c + F1] for w in (w1_hi, w1_lo)]
                        pe.matmul(o, high, xsT_hi[:, n, k, :], start=(k == 0), stop=False)
                        pe.matmul(o, high, xsT_lo[:, n, k, :], start=False, stop=False)
                        ins = pe.matmul(o, low, xsT_hi[:, n, k, :], start=False, stop=(k == KH - 1))
                ins.then_inc(gu1_done, 1)

            def down1(r, i, u, warm):
                a, n = u // 2 % RING, u % 2
                pe.wait_ge(hid1_ready, r * E1 + i * UN + u + 1)
                if warm:
                    pe.wait_ge(ys_ready, r * E1 + i * UN + u - 1)
                for h in range(2):
                    ins = pe.matmul(bank[2 + n][0:SH, h * H:(h + 1) * H], hid1[:, n, h * SH:(h + 1) * SH],
                                    wd_sb[:, a, n, :], start=True, stop=True)
                ins.then_inc(y1_done, 1)

            def experts(r):
                later = not isinstance(r, int)
                turn_rows(r, 0, 0)
                for u in range(UN):
                    turn_rows(r, 0, u + 1)
                    gate_up1(r, 0, u, u >= 2 or later)
                    if u >= 1:
                        down1(r, 0, u - 1, u >= 3 or later)
                with pe.Fori(1, NI - 1) as i:
                    for u in range(UN):
                        turn_rows(r, i, u + 1)
                        gate_up1(r, i, u, True)
                        down1(r, i, u - 1, True)
                for u in range(UN):
                    if u < UN - 1:
                        turn_rows(r, NI - 1, u + 1)
                    gate_up1(r, NI - 1, u, True)
                    down1(r, NI - 1, u - 1, True)
                down1(r, NI - 1, UN - 1, True)

            experts(0)
            pe.wait_ge(more_ready, 1)
            again = pe.value_load(more[0:1, 0:1], min_val=0, max_val=1)
            with pe.If(again):
                with pe.Fori(1, MORE) as r:
                    experts(r)

        @block.scalar
        def _(act):
            def dma(dst, src, s):
                return act.dma_start(dst, src).then_inc(s, 16)

            act.dma_start(w_ij[:, :], W.rearrange("a (n d) -> d (a n)", n=2), allow_slow_non_contiguous=True)\
               .then_inc(ld_small, 16)
            dma(b_sb[:, 0:1], b0.to_broadcast([P, 1]), ld_small)
            dma(wqk[:, 0, :], Wq, ld_small)
            dma(wqk[:, 1, :], Wk, ld_small)
            for n in range(2):
                act.wait_ge(ctx_tr, n + 1)
                act.copy(ctxT[:, n * 512:(n + 1) * 512], bank[4 + n][0:D, :]).then_inc(ctxT_ready, 1)
            act.wait_ge(qkw_tr, 1)
            act.copy(wqkT[:, :, :].rearrange("p n d -> p (n d)"), bank[6][0:D, 0:128]).then_inc(qkwT_ready, 1)
            act.wait_ge(si_ready, 1)
            for j in range(TILES):
                act.wait_ge(z_ready, j // 4 + 1)
                act.activation(adj[:, j, :], bank[4 + j // 4][:, j // TPB % 2 * N:(j // TPB % 2 + 1) * N], ACT.Tanh,
                               bias=si[:, j:j + 1], scale=0.5).then_inc(adj_ready, 1)
            for i in range(4):
                n, h = 1 - i // 2, i % 2
                act.wait_ge(qk_done, i + 1)
                act.copy((qT if n == 0 else kT)[:, h * 512:(h + 1) * 512], bank[4 + 2 * n + h][0:D, :])\
                   .then_inc(qkT_ready, 1)
            act.wait_ge(small_tr, 1)
            act.copy(gate0T[:, :, :].rearrange("p k e -> p (k e)"), bank[0][:, 0:KH * E0]).then_inc(smallT_ready, 1)
            act.copy(gate1T[:, :, :].rearrange("p k e -> p (k e)"), bank[0][:, 256:256 + KH * E1])\
               .then_inc(smallT_ready, 1)
            act.activation(gam[:, 1:2], gam[:, 0:1], ACT.Tanh, scale=0.5).then_inc(gam_t, 1)

            for g in range(FIRST_GROUPS):
                if g not in DVE_GROUPS:
                    keep_weights(act, act.copy, g)
            for b in range(B):
                act.wait_ge(sim_done, b + 1)
                dst = [v[:, b * TPB:(b + 1) * TPB, :].rearrange("p t n -> p (t n)") for v in (sim, sim_t)]
                act.mul(dst[0], bank[4 + b][:, :], SIM_SCALE).then_inc(sim_ready, 1)
                act.activation(dst[1], bank[4 + b][:, :], ACT.Tanh, scale=0.5 * SIM_SCALE).then_inc(sim_ready, 1)
            for g in range(FIRST_GROUPS, 8):
                if g not in DVE_GROUPS:
                    keep_weights(act, act.copy, g)
            for b in range(B):
                act.wait_ge(xn_tr, b + 1)
                act.copy(xnT[:, :, b * N:(b + 1) * N], bank[4 + b][:, :].rearrange("p (k n) -> p k n", k=KH))\
                   .then_inc(xnT_ready, 1)
                for g in range(8 + 2 * b, 10 + 2 * b):
                    if g not in DVE_GROUPS:
                        keep_weights(act, act.copy, g)
            for g in range(8 + 2 * B, GROUPS):
                if g not in DVE_GROUPS:
                    keep_weights(act, act.copy, g)
            act.wait_ge(pr0_in, 1)
            act.activation(pr0[:, :, :].rearrange("p t e -> p (t e)"), pr0[:, :, :].rearrange("p t e -> p (t e)"),
                           ACT.Exp).then_inc(pr0_ready, 1)

            def keep_tail(q):
                act.wait_ge(xn3_tr, q + 1)
                act.copy(xn3T[:, :, :].rearrange("p k n -> p (k n)"), bank[4][:, :]).then_inc(xn3T_ready, 1)

            def rows_to_send(q):
                act.wait_ge(sent, 16 + q * 16 * TPB * K1)
                act.copy(rows[:, :, :], xn3[:, :, :]).then_inc(rows_ready, 1)
                act.wait_ge(zero_fill, 16 * FILLS)
                act.wait_ge(zero_fill_out, 16 * fill_out.shape[0])
                act.copy(xn3_all[:, tiles_of(q), :], xn3[:, :, :]).then_inc(xn3_kept, 1)

            def body(b, first):
                for c in range(NCH):
                    m = SHARED[c] if c < NSH else P
                    act.wait_ge(gu_done, b * NCH + c + 1)
                    act.activation(silu[0:m, c % 3, :], gu_bank[c % 3][0:m, 0:N], ACT.Silu).then_inc(silu_ready, 1)
                    if c == 1 and first:
                        for n in range(2):
                            act.wait_ge(comb_tr, n + 1)
                            act.copy(combT[:, n * 512:(n + 1) * 512], bank[5 + n][:, :]).then_inc(combT_ready, 1)
                        act.wait_ge(combT_ready, 2)
                    if c == 2:
                        act.copy(comb_b[:, :], combT[:, bass.ds(b * N, N)]).then_inc(combb_ready, 1)
                    if c == 7 and not first:
                        keep_tail(b - 1)
                    if c == 10 and not first:
                        rows_to_send(b - 1)

            body(0, True)
            with act.Fori(1, B) as b:
                body(b, False)
            keep_tail(B - 1)
            rows_to_send(B - 1)
            act.wait_ge(wexp_in, 1)
            act.activation(lg_all[:, :, :], lg_all[:, :, :], ACT.Exp).then_inc(wexp_ready, 1)
            def gate(r, i, u):
                n = u % 2
                act.wait_ge(gu1_done, r * E1 + i * UN + u + 1)
                act.activation(silu1[:, n, :], bank[n][0:F1, 0:CAP], ACT.Silu).then_inc(silu1_ready, 1)

            def take(r, i, u):
                a, n = u // 2 % 2, u % 2
                if n == 0 and not (isinstance(i, int) and isinstance(r, int) and i == 0 and u < 4):
                    act.wait_ge(st_ys[a], (r * (E1 // 4) + i * (RING // 2) + u // 4) * 16)
                act.wait_ge(y1_done, r * E1 + i * UN + u + 1)
                act.copy(ys_sb[:, a, n, :, :].rearrange("p s h -> p (s h)"), bank[2 + n][0:SH, :])\
                   .then_inc(ys_ready, 1)

            def rows_high(r, i, u):
                n = u % 2
                act.wait_ge(xs_tr, r * E1 + i * UN + u + 1)
                act.copy(xsT_hi[:, n, :, :].rearrange("p k s -> p (k s)"), bank[6 + n][:, 0:KH * CAP])\
                   .then_inc(xsT_high, 1)

            def weights_high(r, i, a):
                act.wait_ge(ld_w1[a % RING], (r * NI + i + a // RING + 1) * 48)
                act.copy(w1_hi[:, a % 2, :], w1_pair(a % RING)).then_inc(w1_high, 1)

            def step(r, i, u, last=False):
                gate(r, i, u)
                if u % 2 == 0 and (u < UN - 2 or not last):
                    weights_high(r, i, u // 2 + 1)
                if not (u == 0 and isinstance(i, int) and i == 0):
                    take(r, i, u - 1)
                if u < UN - 2 or not last:
                    rows_high(r, i, u + 2)

            def experts(r):
                weights_high(r, 0, 0)
                rows_high(r, 0, 0)
                rows_high(r, 0, 1)
                for u in range(UN):
                    step(r, 0, u)
                with act.Fori(1, NI - 1) as i:
                    for u in range(UN):
                        step(r, i, u)
                for u in range(UN):
                    step(r, NI - 1, u, True)
                take(r, NI - 1, UN - 1)

            experts(0)
            act.wait_ge(more_ready, 1)
            again = act.value_load(more[0:1, 0:1], min_val=0, max_val=1)
            with act.If(again):
                with act.Fori(1, MORE) as r:
                    experts(r)

        @block.vector
        def _(dve):
            s = Steps(dve, dve_steps)
            dve.wait_ge(consts, 5)
            dve.wait_ge(ld_small, 16 * 4)
            dve.tensor_scalar(wj_b[:, :], ones[0:D, 0:P], w_ij[:, 1:2], None, ALU.mult).then_inc(wij_ready, 1)
            dve.tensor_scalar(b_sb[:, 1:2], b_sb[:, 0:1], 0.5, None, ALU.mult).then_inc(wij_ready, 1)
            def rsqrt(s, y, var, v, t):
                s.link(dve.tensor_scalar(v, var, EPS, None, ALU.add))
                s.link(dve.tensor_scalar(y.bitcast(I32), v.bitcast(I32), 1, None, ALU.logical_shift_right))
                s.link(dve.tensor_scalar(y.bitcast(I32), y.bitcast(I32), -1.0, float(0x5F3759DF),
                                         ALU.mult, ALU.add))
                for _ in range(3):
                    s.link(dve.scalar_tensor_tensor(out=t, in0=y, scalar=-0.5, in1=y, op0=ALU.mult, op1=ALU.mult))
                    s.link(dve.tensor_tensor(t, t, v, ALU.mult))
                    s.link(dve.scalar_tensor_tensor(out=y, in0=t, scalar=1.5, in1=y, op0=ALU.add, op1=ALU.mult))

            def moments(src, n, s, st, mv):
                s.link(*[dve.bn_stats(st[:, j, :], src(j)) for j in range(n)])
                s.link(*[dve.bn_aggr(mv[:, j, :], st[:, j, :]) for j in range(n)])

            def norm_stats(src, n, s, st, mv, rs, v, t):
                moments(src, n, s, st, mv)
                rsqrt(s, rs, mv[:, :, 1], v, t)

            for b in range(B):
                dve.wait_ge(ld_x[b], 16)
            moments(lambda j: x1[:, j, :], TILES, s, st, mv)
            dve.wait_ge(wij_ready, 2)
            dve.wait_ge(si_done, 1)
            dve.tensor_scalar(si[:, :], bank[7][:, 0:TILES], 0.5, b_sb[:, 1:2], ALU.mult, ALU.add)\
               .then_inc(si_ready, 1)
            rsqrt(s, rs[:, :], mv[:, :, 1], sc[:, :], of[:, :])
            q = 1.0 - P_ASEM
            s.link(dve.tensor_scalar(sc[:, :], rs[:, :], q, 1.0, ALU.mult, ALU.add),
                   dve.scalar_tensor_tensor(out=of[:, :], in0=mv[:, :, 0], scalar=-q, in1=rs[:, :],
                                            op0=ALU.mult, op1=ALU.mult))
            s.link(dve.tensor_scalar(of[:, :], of[:, :], P_ASEM / 2, None, ALU.add))
            s.link(*[dve.tensor_scalar(x1[:, j, :], x1[:, j, :], sc[:, j:j + 1], of[:, j:j + 1],
                                       ALU.mult, ALU.add) for j in range(TILES)])
            for b in range(B):
                dve.wait_ge(adj_ready, TPB * (b + 1))
                s.add(dve.scalar_tensor_tensor(out=x1[:, b * TPB:(b + 1) * TPB, :], in0=adj[:, b * TPB:(b + 1) * TPB, :],
                                               scalar=P_ASEM / 2, in1=x1[:, b * TPB:(b + 1) * TPB, :],
                                               op0=ALU.mult, op1=ALU.add))
            s.wait()
            norm_stats(lambda j: x1[:, j, :], TILES, s, st, mv, rs[:, :], sc[:, :], of[:, :])
            s.link(dve.scalar_tensor_tensor(out=of[:, :], in0=mv[:, :, 0], scalar=-1.0, in1=rs[:, :],
                                            op0=ALU.mult, op1=ALU.mult))
            for j in range(TILES):
                dve.tensor_scalar(xn[:, j, :], x1[:, j, :], rs[:, j:j + 1], of[:, j:j + 1],
                                  ALU.mult, ALU.add).then_inc(xn_ready, 1)
            dve.wait_ge(gam_t, 1)
            s.link(dve.tensor_scalar(gam[:, 2:3], gam[:, 1:2], 0.125, 0.125, ALU.mult, ALU.add),
                   dve.tensor_scalar(gam[:, 3:4], gam[:, 1:2], -0.5, 0.5, ALU.mult, ALU.add),
                   dve.tensor_scalar(gam[:, 4:5], gam[:, 1:2], 0.5, -0.5, ALU.mult, ALU.add))
            def topk_take(s, b):
                s.link(dve.tensor_scalar(simw[:, :, :], sim[:, tiles_of(b), :], 1.0, None, ALU.mult))

            def topk(s, rounds):
                for _ in range(rounds):
                    s.link(*[dve.max(v8[:, t, :], simw[:, t, :]) for t in range(TPB)])
                    s.link(*[dve.match_replace(simw[:, t, :], v8[:, t, :], simw[:, t, :], LOWEST)
                             for t in range(TPB)])

            def topk_keep(s):
                s.link(dve.tensor_copy(least[:, :], v8[:, :, (TOPK - 1) % 8]))

            dve.wait_ge(sim_ready, 2 * B)
            topk_take(s, 0)
            for r, g in enumerate(DVE_GROUPS):
                keep_weights(dve, dve.tensor_copy, g)
                if r < EARLY and g < 8 + 2 * B:
                    topk(s, 1)

            dve.wait_ge(lg0_done, 1)
            s.link(dve.tensor_copy(lg0[:, :, :].rearrange("p t e -> p (t e)"), bank[4][:, 0:TILES * E0]))
            s.link(*[dve.max(top0[:, j, :], lg0[:, j, :]) for j in range(TILES)])
            for j in range(TILES):
                s.add(dve.max_index(idx0[:, j, :], top0[:, j, :], lg0[:, j, :]))
            dve.tensor_tensor(pr0[:, :, :], lg0[:, :, :], top0[:, :, 0:1].to_broadcast([P, TILES, E0]),
                              ALU.subtract).then_inc(pr0_in, 1)
            s.wait()
            s.link(dve.tensor_copy(idx0f[:, :, :], idx0[:, :, :]))
            iota8 = iota64[:, 0:E0].unsqueeze(1).to_broadcast([P, TILES, E0])
            s.link(dve.tensor_tensor(eq0[:, :, :], iota8, idx0f[:, :, 0:1].to_broadcast([P, TILES, E0]),
                                     ALU.is_equal),
                   dve.tensor_tensor(eq1[:, :, :], iota8, idx0f[:, :, 1:2].to_broadcast([P, TILES, E0]),
                                     ALU.is_equal))
            s.link(dve.tensor_tensor(eq0[:, :, :], eq0[:, :, :], eq1[:, :, :], ALU.add))
            dve.wait_ge(pr0_ready, 1)
            s.link(dve.tensor_reduce(sum0[:, :], pr0[:, :, :], AX.X, ALU.add),
                   dve.tensor_tensor(eq0[:, :, :], eq0[:, :, :], pr0[:, :, :], ALU.mult))
            s.link(dve.reciprocal(sum0[:, :], sum0[:, :]))
            s.link(dve.tensor_tensor(eq0[:, :, :], eq0[:, :, :],
                                     sum0[:, :].unsqueeze(2).to_broadcast([P, TILES, E0]), ALU.mult))
            dve.tensor_copy(comb_x[:, :, :, :].rearrange("p t e q -> p (t e) q"),
                            eq0[:, :, :].rearrange("p t e -> p (t e)").unsqueeze(2)
                            .to_broadcast([P, TILES * E0, Q0])).then_inc(combx_ready, 1)
            s.link(*[dve.tensor_scalar(sim_t[:, j, :], sim_t[:, j, :], 1.0, gam[:, 2:3], ALU.add, ALU.mult)
                     for j in range(TILES)])

            def hidden(b, c):
                m = SHARED[c] if c < NSH else P
                if c < NSH:
                    dve.wait_ge(silu_ready, b * NCH + c + 1)
                    src = silu
                else:
                    dve.wait_ge(scaled_ready, b * RJ + c - NSH + 1)
                    src = silu_c
                dve.tensor_tensor(hid[0:m, c % HIDS, :], src[0:m, c % 3, :], gu_bank[c % 3][0:m, N:2 * N],
                                  ALU.mult).then_inc(hid_ready, 1)

            def learned(q, s):
                for t in range(TPB):
                    sim_tile, sig_tile = [v[:, bass.ds(q * TPB + t, 1), :].rearrange("p a n -> p (a n)")
                                          for v in (sim, sim_t)]
                    ins = dve.scalar_tensor_tensor(out=A[:, t, :], in0=sim_tile, scalar=least[:, t:t + 1],
                                                   in1=sig_tile, op0=ALU.is_ge, op1=ALU.mult)
                    if t < TPB - 1:
                        s.link(ins)
                ins.then_inc(A_ready, 1)
                dve.wait_ge(A_ready, q + 1)

            def mirror(q, s):
                dve.wait_ge(AT_done, q + 1)
                s.link(dve.tensor_tensor(S[:, :, :].rearrange("p t n -> p (t n)"),
                                         A[:, :, :].rearrange("p t n -> p (t n)"), bank[6][:, :], ALU.add))

            def take_y(q, s):
                dve.wait_ge(y_done, q + 1)
                s.add(dve.tensor_tensor(x2[:, 0, :], bank[2][:, 0:H], x1[:, bass.ds(q * TPB, 1), :]
                                        .rearrange("p a n -> p (a n)"), ALU.add))
                dve.tensor_tensor(x2[:, 1, :], bank[3][:, 0:H], x1[:, bass.ds(q * TPB + 1, 1), :]
                                  .rearrange("p a n -> p (a n)"), ALU.add).then_inc(y_read, 1)
                dve.wait_ge(y_read, q + 1)
                s.wait()

            def x3_tile(q, t):
                return x3[:, bass.ds(q * TPB + t, 1), :].rearrange("p a n -> p (a n)")

            def mix_stats(q, s):
                norm_stats(lambda t: x2[:, t, :], TPB, s, st2, mv2, sm[:, 0, :], sm[:, 1, :], sm[:, 2, :])

            def mix(q, s, mirrored=False):
                s.link(dve.tensor_scalar(sm[:, 1, :], sm[:, 0, :], gam[:, 3:4], 1.0, ALU.mult, ALU.add),
                       dve.scalar_tensor_tensor(out=sm[:, 2, :], in0=mv2[:, :, 0], scalar=gam[:, 4:5],
                                                in1=sm[:, 0, :], op0=ALU.mult, op1=ALU.mult))
                s.link(*[dve.tensor_scalar(x2[:, t, :], x2[:, t, :], sm[:, 1, t:t + 1], sm[:, 2, t:t + 1],
                                           ALU.mult, ALU.add) for t in range(TPB)])
                if not mirrored:
                    mirror(q, s)
                s.link(dve.tensor_tensor(x3[:, tiles_of(q), :], x2[:, :, :], S[:, :, :], ALU.add))

            def norm3(q, s):
                norm_stats(lambda t: x3_tile(q, t), TPB, s, st2, mv2, sm[:, 0, :], sm[:, 1, :], sm[:, 2, :])
                s.link(dve.scalar_tensor_tensor(out=sm[:, 1, :], in0=mv2[:, :, 0], scalar=-1.0, in1=sm[:, 0, :],
                                                op0=ALU.mult, op1=ALU.mult))
                dve.wait_ge(xn3_kept, q + 1)
                s.link(dve.tensor_scalar(xn3[:, 0, :], x3_tile(q, 0), sm[:, 0, 0:1], sm[:, 1, 0:1],
                                         ALU.mult, ALU.add))
                dve.tensor_scalar(xn3[:, 1, :], x3_tile(q, 1), sm[:, 0, 1:2], sm[:, 1, 1:2],
                                  ALU.mult, ALU.add).then_inc(xn3_ready, 1)

            def choose(q, s):
                dve.wait_ge(lg1_done, q + 1)
                s.link(dve.tensor_copy(lg1[:, :, :].rearrange("p t e -> p (t e)"), bank[5][:, 0:TPB * E1]))
                s.link(*[dve.max(t8[:, t, :], lg1[:, t, :]) for t in range(TPB)])
                s.link(*[dve.match_replace(lgr[:, t, :], t8[:, t, :], lg1[:, t, :], LOWEST) for t in range(TPB)],
                       dve.tensor_scalar(lg_all[:, tiles_of(q), :], lg1[:, :, :], 1.0, None, ALU.mult))
                dve.tensor_tensor(chosen[:, :, :], lg1[:, :, :], lgr[:, :, :], ALU.not_equal)\
                   .then_inc(chosen_ready, 1)
                dve.wait_ge(chosen_ready, q + 1)
                s.link(*[dve.scalar_tensor_tensor(out=lgr[:, t, :], in0=iota64[:, :], scalar=1.0,
                                                  in1=chosen[:, t, :], op0=ALU.add, op1=ALU.mult)
                         for t in range(TPB)])
                s.link(*[dve.max(i8f[:, t, :], lgr[:, t, :]) for t in range(TPB)])
                s.link(dve.tensor_scalar(i8f[:, :, :], i8f[:, :, :], -1.0, None, ALU.add))

            def ranks(q, s, ts, ks=range(K1)):
                dve.wait_ge(rank_done, q + 1)
                for t in ts:
                    for k in ks:
                        s.add(dve.scalar_tensor_tensor(out=junk[:, t * K1 + k, :], in0=iota64[:, :],
                                                       scalar=i8f[:, t, k:k + 1],
                                                       in1=bank[5][:, (2 + t) * E1:(3 + t) * E1],
                                                       op0=ALU.is_equal, op1=ALU.mult, accum_out=rk[:, t, k:k + 1]))

            def find_slots(q, s, k0=0, k1=K1):
                s.link(dve.tensor_scalar(ovf[:, :, k0:k1], rk[:, :, k0:k1], float(CAP), BIG, ALU.is_ge, ALU.mult),
                       dve.scalar_tensor_tensor(out=slf[:, :, k0:k1], in0=i8f[:, :, k0:k1], scalar=float(CAP),
                                                in1=rk[:, :, k0:k1], op0=ALU.mult, op1=ALU.add))
                dve.wait_ge(sent, 16 + q * 16 * TPB * K1)
                dve.tensor_tensor(slot[:, :, k0:k1], slf[:, :, k0:k1], ovf[:, :, k0:k1], ALU.add)\
                   .then_inc(slot_ready, 1)

            def keep(q, s, *pairs):
                s.link(*[dve.tensor_scalar(d[:, tiles_of(q), :], v[:, :, :], 1.0, None, ALU.mult) for d, v in pairs])

            def count_chosen(s):
                for t in range(TPB):
                    s.link(dve.tensor_tensor(chosen_sum[:, :], chosen_sum[:, :], chosen[:, t, :], ALU.add))

            def slots(q, s):
                s.wait()
                keep(q, s, (rank_all, rk), (exp_all, i8f), (top_all, t8))
                count_chosen(s)
                find_slots(q, s)

            def plan_slots(s):
                s.link(dve.tensor_scalar(valid[:, :, :], rank_all[:, :, :], float(CAP), None, ALU.is_lt),
                       dve.tensor_scalar(clamp[:, :, :], rank_all[:, :, :], 0.0, float(CAP - 1), ALU.max, ALU.min))
                s.link(dve.scalar_tensor_tensor(out=valid[:, :, :], in0=rank_all[:, :, :], scalar=0.0,
                                                in1=valid[:, :, :], op0=ALU.is_ge, op1=ALU.mult))
                dve.scalar_tensor_tensor(out=gidx[:, :, :], in0=exp_all[:, :, :], scalar=float(CAP),
                                         in1=clamp[:, :, :], op0=ALU.mult, op1=ALU.add).then_inc(gidx_ready, 1)

            def body(b, first, last=False):
                dve.sem_clear(topk_steps)
                s = Steps(dve, topk_steps)
                if not first:
                    dve.sem_clear(tail_steps)
                tl = Steps(dve, tail_steps)
                for c in range(NCH):
                    hidden(b, c)
                    if not first:
                        if c == 0:
                            take_y(b - 1, tl)
                            learned(b - 1, tl)
                        if c == 1:
                            mix_stats(b - 1, tl)
                        if c == 2:
                            mix(b - 1, tl)
                        if c == 4:
                            norm3(b - 1, tl)
                        if c == 7:
                            choose(b - 1, tl)
                        if c == 9:
                            ranks(b - 1, tl, (0,))
                        if c == 10:
                            ranks(b - 1, tl, (1,))
                            slots(b - 1, tl)
                    if first:
                        if c == FINISH:
                            topk_keep(s)
                            topk_take(s, 1)
                        topk(s, MAXIMA0[c])
                    else:
                        if c == 0:
                            topk_keep(s)
                            if not last:
                                topk_take(s, b + 1)
                        if not last:
                            topk(s, MAXIMA[c])
                    if last and c == 11:
                        learned(b, tl)
                    if last and c == NCH - 1:
                        mirror(b, tl)
            body(0, True)
            with dve.Fori(1, B - 1) as b:
                body(b, False)
            body(B - 1, False, True)
            dve.sem_clear(tail_steps)
            tl = Steps(dve, tail_steps)
            take_y(B - 1, tl)
            mix_stats(B - 1, tl)
            mix(B - 1, tl, True)
            norm3(B - 1, tl)
            choose(B - 1, tl)
            ranks(B - 1, tl, range(TPB), (K1 - 1, K1 - 2))
            tl.wait()
            find_slots(B - 1, tl, K1 - 2, K1)
            keep(B - 1, tl, (exp_all, i8f), (top_all, t8))
            tl.link(dve.tensor_reduce(levels[:, 0:K1], exp_all[:, :, :].rearrange("p t k -> p k t"), AX.X, ALU.max),
                    dve.tensor_tensor(levels[:, K1:2 * K1], exp_all[:, TILES - 2, :], exp_all[:, TILES - 1, :],
                                      ALU.min))
            dve.tensor_scalar(levels[:, K1:2 * K1], levels[:, K1:2 * K1], -1.0, None, ALU.mult)\
               .then_inc(levels_ready, 1)
            ranks(B - 1, tl, range(TPB), range(3, K1 - 2))
            dve.wait_ge(levels_tr, 1)
            dve.tensor_reduce(level_max[:, :], level_bank[0:2 * K1, P:2 * P], AX.X, ALU.max).then_inc(level_max_ready, 1)
            ranks(B - 1, tl, range(TPB), range(3))
            tl.wait()
            dve.wait_ge(slot_ready, B)
            find_slots(B - 1, tl, 0, K1 - 2)
            dve.wait_ge(level_row_done, 1)
            tl.link(*[dve.scalar_tensor_tensor(out=level_hits[:, a, :], in0=level_bank[0:1, 2 * P + K1:2 * P + 2 * K1],
                                               scalar=-float(2 * a + 1), in1=ones[0:1, 0:K1], op0=ALU.is_ge,
                                               op1=ALU.mult, accum_out=level_count[:, a:a + 1])
                      for a in range(RING)])
            tl.link(*[dve.tensor_scalar(sends[:, n, :], level_count[:, :], float(1 - n), None, ALU.add)
                      for n in range(2)])
            tl.link(*[dve.tensor_scalar(sends[:, n, :], sends[:, n, :], 1, None, ALU.logical_shift_right)
                      for n in range(2)])
            for n in range(2):
                dve.tensor_scalar(sends[:, n, :], sends[:, n, :], float(SENT_LEVEL), float(SENT_LEVEL),
                                  ALU.mult, ALU.max).then_inc(sends_ready, 1)
            keep(B - 1, tl, (rank_all, rk))
            count_chosen(tl)
            dve.tensor_copy(cnt[:, :], chosen_sum[:, 0:1]).then_inc(chosen_counted, 1)
            dve.wait_ge(count_done, 1)
            tl.link(dve.tensor_reduce(cnt[:, :], bank[4][:, 0:E1], AX.X, ALU.max))
            dve.tensor_scalar(more[:, :], cnt[:, :], float(CAP), None, ALU.is_gt).then_inc(more_ready, 1)
            tl.link(dve.tensor_copy(max_all[:, :], top_all[:, :, 0]))
            dve.tensor_tensor(lg_all[:, :, :], lg_all[:, :, :], max_all[:, :].unsqueeze(2).to_broadcast([P, TILES, E1]),
                              ALU.subtract).then_inc(wexp_in, 1)
            plan_slots(tl)
            tl.link(dve.tensor_copy(level_row[:, :], level_bank[0:1, 2 * P:2 * P + K1]))
            tl.link(dve.tensor_scalar(stores[:, 1, :], level_row[:, :], 2, None, ALU.add))
            tl.link(dve.tensor_scalar(stores[:, 0, :], level_row[:, :], 2, None, ALU.logical_shift_right),
                    dve.tensor_scalar(stores[:, 1, :], stores[:, 1, :], 2, None, ALU.logical_shift_right))
            dve.tensor_scalar(stores[:, 0, :], stores[:, 0, :], 16.0, 16.0, ALU.mult, ALU.add)\
               .then_inc(stores_ready, 1)
            dve.tensor_scalar(stores[:, 1, :], stores[:, 1, :], 16.0, 16.0, ALU.mult, ALU.max)\
               .then_inc(stores_ready, 1)
            def rows_low(r, i, u):
                n = u % 2
                dve.wait_ge(xsT_high, r * E1 + i * UN + u + 1)
                high, low = [v[:, n, :, :].rearrange("p k s -> p (k s)") for v in (xsT_hi, xsT_lo)]
                dve.tensor_tensor(low, bank[6 + n][:, 0:KH * CAP], high.bitcast(F32), ALU.subtract)\
                   .then_inc(xsT_ready, 1)

            def weights_low(r, i, a):
                dve.wait_ge(w1_high, r * (E1 // 2) + i * RING + a + 1)
                dve.tensor_tensor(w1_lo[:, a % 2, :], w1_pair(a % RING), w1_hi[:, a % 2, :].bitcast(F32),
                                  ALU.subtract).then_inc(w1_ready, 1)

            def hidden1(r, i, u):
                n = u % 2
                dve.wait_ge(silu1_ready, r * E1 + i * UN + u + 1)
                dve.tensor_tensor(hid1[:, n, :], silu1[:, n, :], bank[n][0:F1, CAP:2 * CAP], ALU.mult)\
                   .then_inc(hid1_ready, 1)

            def pick(s, j, u):
                if u == 0:
                    s.link(dve.tensor_scalar(exp_j[:, :, :], exp_all[:, bass.ds(j, 1), :], 1.0, None, ALU.mult),
                           dve.tensor_scalar(lg_j[:, :, :], lg_all[:, bass.ds(j, 1), :], 1.0, None, ALU.mult))
                elif u < UN - 1:
                    ks = range(0, 2) if u == 1 else range(u, u + 1)
                    for k in ks:
                        s.add(dve.scalar_tensor_tensor(out=junk[:, k, :], in0=iota64[:, :],
                                                       scalar=exp_j[:, 0, k:k + 1], in1=lg_j[:, 0, :],
                                                       op0=ALU.is_equal, op1=ALU.mult,
                                                       accum_out=top_j[:, 0, k:k + 1]))
                    s.wait()
                else:
                    s.link(dve.scalar_tensor_tensor(out=junk[:, u, :], in0=iota64[:, :],
                                                    scalar=exp_j[:, 0, u:u + 1], in1=lg_j[:, 0, :],
                                                    op0=ALU.is_equal, op1=ALU.mult, accum_out=top_j[:, 0, u:u + 1]))
                    s.link(dve.tensor_scalar(top_all[:, bass.ds(j, 1), :], top_j[:, :, :], 1.0, None, ALU.mult))

            def experts(r):
                first = isinstance(r, int)
                weights_low(r, 0, 0)
                rows_low(r, 0, 0)
                rows_low(r, 0, 1)
                if first:
                    dve.wait_ge(wexp_ready, 1)
                with dve.Fori(0, NI - 1) as i:
                    dve.sem_clear(pick_steps)
                    for u in range(UN):
                        hidden1(r, i, u)
                        if u % 2 == 0:
                            weights_low(r, i, u // 2 + 1)
                        rows_low(r, i, u + 2)
                        if first:
                            pick(Steps(dve, pick_steps, u + (u > 0) + (u > 1)), i, u)
                dve.sem_clear(pick_steps)
                for u in range(UN):
                    hidden1(r, NI - 1, u)
                    if u < UN - 2:
                        if u % 2 == 0:
                            weights_low(r, NI - 1, u // 2 + 1)
                        rows_low(r, NI - 1, u + 2)
                    if first:
                        pick(Steps(dve, pick_steps, u + (u > 0) + (u > 1)), NI - 1, u)

            def combine(r):
                dve.sem_clear(acc_steps)
                steps = Steps(dve, acc_steps)
                for lv in range(K1):
                    last = lv == K1 - 1
                    if not last:
                        dve.wait_ge(gathered[lv], (r + 1) * 16 * TILES)
                    for j in range(TILES):
                        if last:
                            dve.wait_ge(gathered_last[j], (r + 1) * 16)
                        ins = dve.scalar_tensor_tensor(out=x3[:, j, :], in0=gath[lv][:, j, :],
                                                       scalar=w_now[:, j, K1 - 1 - lv:K1 - lv], in1=x3[:, j, :],
                                                       op0=ALU.mult, op1=ALU.add)
                        if last:
                            ins.then_inc(acc_done, 1)
                        else:
                            steps.add(ins)
                    steps.wait()

            experts(0)
            dve.sem_clear(acc_steps)
            ws = Steps(dve, acc_steps)
            ws.link(dve.tensor_reduce(wsum[:, :], top_all[:, :, :], AX.X, ALU.add))
            ws.link(dve.reciprocal(wsum[:, :], wsum[:, :]))
            ws.link(dve.tensor_tensor(top_all[:, :, :], top_all[:, :, :],
                                      wsum[:, :].unsqueeze(2).to_broadcast([P, TILES, K1]), ALU.mult))
            ws.link(dve.tensor_tensor(w_now[:, :, :], valid[:, :, :], top_all[:, :, :], ALU.mult))
            combine(0)
            dve.wait_ge(more_ready, 1)
            again = dve.value_load(more[0:1, 0:1], min_val=0, max_val=1)
            with dve.If(again):
                with dve.Fori(1, MORE) as r:
                    dve.wait_ge(out_done, r * 16 * TILES)
                    dve.memset(cnt[:, :], 0.0)
                    dve.sem_clear(plan_steps)
                    s2 = Steps(dve, plan_steps)
                    s2.link(dve.tensor_scalar(rank_all[:, :, :], rank_all[:, :, :], -float(CAP), None, ALU.add))
                    plan_slots(s2)
                    s2.link(dve.tensor_tensor(w_now[:, :, :], valid[:, :, :], top_all[:, :, :], ALU.mult))
                    s2.link(dve.tensor_scalar(ovf_all[:, :, :], valid[:, :, :], -BIG, BIG, ALU.mult, ALU.add),
                            dve.scalar_tensor_tensor(out=slf_all[:, :, :], in0=exp_all[:, :, :], scalar=float(CAP),
                                                     in1=clamp[:, :, :], op0=ALU.mult, op1=ALU.add))
                    s2.link(dve.tensor_tensor(slf_all[:, :, :], slf_all[:, :, :], ovf_all[:, :, :], ALU.add))
                    with dve.Fori(0, TILES) as j:
                        for n in range(2):
                            dve.wait_ge(sent_last[n], SENT_LEVEL * K1 // 2)
                        dve.tensor_scalar(slot[:, 0:1, :], slf_all[:, bass.ds(j, 1), :], 1.0, None, ALU.mult)\
                           .then_inc(staged, 1)
                        dve.tensor_scalar(xn3[:, 0:1, :], xn3_all[:, bass.ds(j, 1), :], 1.0, None, ALU.mult)\
                           .then_inc(staged, 1)
                        dve.wait_ge(sent_more, ((r - 1) * TILES + j + 1) * 16 * K1)
                        dve.memset(cnt[:, :], 0.0)
                    experts(r)
                    combine(r)


_INS = ['x', 'ctx_512', 'L0_xattn_W', 'L0_xattn_b', 'L0_ffn_gate_weight', 'L0_ffn_gate_up_weights',
        'L0_ffn_down_weights', 'L0_ffn_shared_gate_up', 'L0_ffn_shared_down', 'L1_xattn_Wq', 'L1_xattn_Wk',
        'L1_xattn_gamma_raw', 'L1_ffn_gate_weight', 'L1_ffn_w_gate', 'L1_ffn_w_up', 'L1_ffn_w_down']


def kernel(**inputs):
    import numpy as _np
    import concourse.bacc as _bacc
    from concourse import mybir as _mybir
    from concourse.bass_utils import run_bass_kernel_spmd as _run

    nc = _bacc.Bacc("TRN2", target_bir_lowering=False, num_devices=1)
    arrays, args = {}, []
    for name in _INS:
        a = _np.ascontiguousarray(inputs[name])
        if a.ndim < 2:
            a = a.reshape(1, 1)
        arrays[f"in_{name}_dram"] = a
        args.append(nc.dram_tensor(f"in_{name}_dram", a.shape, _mybir.dt.from_np(a.dtype), kind="ExternalInput").ap())
    args.append(nc.dram_tensor("out_0_dram", (B, N, H), F32, kind="ExternalOutput").ap())
    build(nc, *args)
    r = _run(nc, [arrays], core_ids=[0])
    return r.results[0]["out_0_dram"]
```
